# Optimizing a Trainium2 kernel written in Bass

```python
import numpy as np
import jax
import jax.numpy as jnp

def _softmax(x, axis=-1):
    return jax.nn.softmax(x, axis=axis)

def _gelu(x):
    return jax.nn.gelu(x, approximate=True)

def _silu(x):
    return jax.nn.silu(x)

def _sigmoid(x):
    return jax.nn.sigmoid(x)

def _layernorm(x, axis=-1, eps=1e-05):
    m = jnp.mean(x, axis=axis, keepdims=True)
    v = jnp.var(x, axis=axis, keepdims=True)
    return (x - m) / jnp.sqrt(v + eps)

def _scatter_add(tgt, idx, src, axis=0):
    return tgt.at[idx].add(src)

def _segment_sum(src, seg, n):
    return jax.ops.segment_sum(src, seg, n)
kernel_name = 'mk_gnn_resnorm_d4_gnn_r32_2504b9'

def setup_inputs(seed: int=0):
    np.random.seed(seed)
    _w = jnp.asarray

    def _rec_inputs():
        import jax
        import jax.numpy as jnp
        _gk = jax.random.key(seed)
        x = -0.000125 + 0.9999 * jax.random.normal(jax.random.fold_in(_gk, 1), (2048, 512), jnp.float32)
        src = jax.random.randint(jax.random.fold_in(_gk, 2), (32768,), 0, 2048, jnp.int32)
        dst = jnp.minimum((2048 * jax.random.uniform(jax.random.fold_in(_gk, 3), (32768,)) ** 2.0).astype(jnp.int32), 65535)
        _o = jnp.argsort(dst, stable=True)
        src = src[_o]
        dst = dst[_o]
        edge_attr_2 = 0.00222621 + 0.99962 * jax.random.normal(jax.random.fold_in(_gk, 12), (32768, 2), jnp.float32)
        edge_attr_64 = 0.000279952 + 1.00013 * jax.random.normal(jax.random.fold_in(_gk, 13), (32768, 64), jnp.float32)
        edge_weight = jax.random.uniform(jax.random.fold_in(_gk, 15), (32768,), jnp.float32, 0.0, 0.999998)
        return (x, src, dst, edge_attr_2, edge_attr_64, edge_weight)
    x, src, dst, edge_attr_2, edge_attr_64, edge_weight = _rec_inputs()

    def _L0_gnn_setup():
        import jax, jax.numpy as jnp
        import numpy as np
        N_NODES = 2048
        N_EDGES = 16384
        FEAT_DIM = 512
        EMBED_DIM = 512
        key = jax.random.key(seed)
        k1, k2, k3, k4, k5 = jax.random.split(key, 5)
        x = jax.random.normal(k1, (N_NODES, FEAT_DIM), dtype=jnp.float32)
        limit = float(np.sqrt(6.0 / (EMBED_DIM + FEAT_DIM)))
        weight = jax.random.uniform(k2, (EMBED_DIM, FEAT_DIM), dtype=jnp.float32, minval=-limit, maxval=limit)
        row = jax.random.randint(k3, (N_EDGES,), 0, N_NODES, dtype=jnp.int64)
        col = jax.random.randint(k4, (N_EDGES,), 0, N_NODES, dtype=jnp.int64)
        vals = jax.random.uniform(k5, (N_EDGES,), dtype=jnp.float32)
        return {'x': x, 'weight': weight, 'row': row, 'col': col, 'vals': vals}
    _L0_gnn_all = _L0_gnn_setup()
    _L0_gnn_in = {k: v for k, v in _L0_gnn_all.items() if k in ('weight',)}
    del _L0_gnn_all

    def _L1_gnn_setup():
        import jax, jax.numpy as jnp
        import numpy as np
        N, E, D, ED, L = (512, 8192, 512, 2, 3)
        EPS = 1e-05
        SLOPE = 0.2

        def _segment_softmax(logits, seg, n):
            m = jax.ops.segment_max(logits, seg, num_segments=n)
            m = jnp.where(jnp.isfinite(m), m, 0.0)
            ex = jnp.exp(logits - m[seg])
            den = jax.ops.segment_sum(ex, seg, num_segments=n)
            return ex / (den[seg] + 1e-16)

        def _forward(x, edge_attr, Wl, bl, Wr, br, We, att, b_out, gamma, beta, edge_index):
            n = x.shape[0]
            src, dst = (edge_index[0], edge_index[1])
            ones = jnp.ones((src.shape[0],), x.dtype)
            cnt = jax.ops.segment_sum(ones, dst, num_segments=n)
            mean_ea = jax.ops.segment_sum(edge_attr, dst, num_segments=n) / jnp.maximum(cnt, 1.0)[:, None]
            loop = jnp.arange(n, dtype=edge_index.dtype)
            src2 = jnp.concatenate([src, loop])
            dst2 = jnp.concatenate([dst, loop])
            ea2 = jnp.concatenate([edge_attr, mean_ea], axis=0)
            for k in range(Wl.shape[0]):
                xl = x @ Wl[k] + bl[k]
                xr = x @ Wr[k] + br[k]
                ef = ea2 @ We[k]
                m = jax.nn.leaky_relu(xl[src2] + xr[dst2] + ef, SLOPE)
                logit = m @ att[k]
                alpha = _segment_softmax(logit, dst2, n)
                out = jax.ops.segment_sum(xl[src2] * alpha[:, None], dst2, num_segments=n) + b_out[k]
                h = out + x
                mu = jnp.mean(h, axis=-1, keepdims=True)
                var = jnp.var(h, axis=-1, keepdims=True)
                h = (h - mu) * jax.lax.rsqrt(var + EPS) * gamma[k] + beta[k]
                x = jax.nn.relu(h)
            return x
        key = jax.random.key(seed)
        ks = jax.random.split(key, 8)
        s = np.float32(1.0 / np.sqrt(D))
        return dict(x=jax.random.normal(ks[0], (N, D), jnp.float32), edge_attr=jax.random.normal(ks[1], (E, ED), jnp.float32), Wl=jax.random.normal(ks[2], (L, D, D), jnp.float32) * s, bl=jnp.zeros((L, D), jnp.float32), Wr=jax.random.normal(ks[3], (L, D, D), jnp.float32) * s, br=jnp.zeros((L, D), jnp.float32), We=jax.random.normal(ks[4], (L, ED, D), jnp.float32) * s, att=jax.random.normal(ks[5], (L, D), jnp.float32) * s, b_out=jnp.zeros((L, D), jnp.float32), gamma=jnp.ones((L, D), jnp.float32), beta=jnp.zeros((L, D), jnp.float32), edge_index=jax.random.randint(ks[6], (2, E), 0, N, dtype=jnp.int32))
    _L1_gnn_all = _L1_gnn_setup()
    _L1_gnn_in = {k: v for k, v in _L1_gnn_all.items() if k in ('Wl', 'bl', 'Wr', 'br', 'We', 'att', 'b_out', 'gamma', 'beta')}
    del _L1_gnn_all

    def _L2_gnn_setup():
        import jax, jax.numpy as jnp
        import numpy as np
        N_NODES = 10000

        def gcn_conv(x, edge_index, W, b):
            n = x.shape[0]
            h = x @ W
            loop = jnp.arange(n, dtype=edge_index.dtype)
            src = jnp.concatenate([edge_index[0], loop])
            dst = jnp.concatenate([edge_index[1], loop])
            ones = jnp.ones(src.shape[0], dtype=h.dtype)
            deg = jax.ops.segment_sum(ones, dst, num_segments=n)
            dis = jnp.where(deg > 0, jax.lax.rsqrt(deg), 0.0)
            norm = dis[src] * dis[dst]
            msg = h[src] * norm[:, None]
            out = jax.ops.segment_sum(msg, dst, num_segments=n)
            return out + b
        key = jax.random.key(seed)
        k1, k2, k3, k4, k5 = jax.random.split(key, 5)
        num_features, hidden, num_classes = (512, 512, 512)
        x = jax.random.normal(k1, (N_NODES, num_features), dtype=jnp.float32)
        edge_index = jax.random.randint(k2, (2, 5000), 0, N_NODES, dtype=jnp.int64)
        s1 = 1.0 / np.sqrt(num_features)
        s2 = 1.0 / np.sqrt(hidden)
        W1 = jax.random.uniform(k3, (num_features, hidden), jnp.float32, -s1, s1)
        b1 = jnp.zeros((hidden,), jnp.float32)
        W2 = jax.random.uniform(k4, (hidden, num_classes), jnp.float32, -s2, s2)
        b2 = jnp.zeros((num_classes,), jnp.float32)
        return {'x': x, 'edge_index': edge_index, 'W1': W1, 'b1': b1, 'W2': W2, 'b2': b2}
    _L2_gnn_all = _L2_gnn_setup()
    _L2_gnn_in = {k: v for k, v in _L2_gnn_all.items() if k in ('W1', 'b1', 'W2', 'b2')}
    del _L2_gnn_all

    def _L3_gnn_setup():
        import jax, jax.numpy as jnp
        import numpy as np
        N_NODES = 625
        N_EDGES = 10000
        HIDDEN = 512
        EDGE_DIM = 64
        LN_EPS = 1e-05

        def mish(x):
            return x * jnp.tanh(jax.nn.softplus(x))
        key = jax.random.key(seed)
        ks = jax.random.split(key, 8)
        s = lambda fan_in: 1.0 / np.sqrt(fan_in)
        return {'x': jax.random.normal(ks[0], (N_NODES, HIDDEN), dtype=jnp.float32), 'edge_index': jax.random.randint(ks[1], (2, N_EDGES), 0, N_NODES, dtype=jnp.int64), 'edge_attr': jax.random.normal(ks[2], (N_EDGES, EDGE_DIM), dtype=jnp.float32), 'W1': jax.random.normal(ks[3], (2 * HIDDEN + EDGE_DIM, HIDDEN), dtype=jnp.float32) * s(2 * HIDDEN + EDGE_DIM), 'b1': jnp.zeros((HIDDEN,), dtype=jnp.float32), 'W2': jax.random.normal(ks[4], (HIDDEN, HIDDEN), dtype=jnp.float32) * s(HIDDEN), 'b2': jnp.zeros((HIDDEN,), dtype=jnp.float32), 'W3': jax.random.normal(ks[5], (2 * HIDDEN, HIDDEN), dtype=jnp.float32) * s(2 * HIDDEN), 'b3': jnp.zeros((HIDDEN,), dtype=jnp.float32), 'W4': jax.random.normal(ks[6], (HIDDEN, HIDDEN), dtype=jnp.float32) * s(HIDDEN), 'b4': jnp.zeros((HIDDEN,), dtype=jnp.float32), 'gamma': jnp.ones((HIDDEN,), dtype=jnp.float32), 'beta': jnp.zeros((HIDDEN,), dtype=jnp.float32)}
    _L3_gnn_all = _L3_gnn_setup()
    _L3_gnn_in = {k: v for k, v in _L3_gnn_all.items() if k in ('W1', 'b1', 'W2', 'b2', 'W3', 'b3', 'W4', 'b4', 'gamma', 'beta')}
    del _L3_gnn_all
    return {'x': x, 'src': src, 'dst': dst, 'edge_attr_2': edge_attr_2, 'edge_attr_64': edge_attr_64, 'edge_weight': edge_weight, 'L0_gnn_weight': _L0_gnn_in['weight'], 'L1_gnn_Wl': _L1_gnn_in['Wl'], 'L1_gnn_bl': _L1_gnn_in['bl'], 'L1_gnn_Wr': _L1_gnn_in['Wr'], 'L1_gnn_br': _L1_gnn_in['br'], 'L1_gnn_We': _L1_gnn_in['We'], 'L1_gnn_att': _L1_gnn_in['att'], 'L1_gnn_b_out': _L1_gnn_in['b_out'], 'L1_gnn_gamma': _L1_gnn_in['gamma'], 'L1_gnn_beta': _L1_gnn_in['beta'], 'L2_gnn_W1': _L2_gnn_in['W1'], 'L2_gnn_b1': _L2_gnn_in['b1'], 'L2_gnn_W2': _L2_gnn_in['W2'], 'L2_gnn_b2': _L2_gnn_in['b2'], 'L3_gnn_W1': _L3_gnn_in['W1'], 'L3_gnn_b1': _L3_gnn_in['b1'], 'L3_gnn_W2': _L3_gnn_in['W2'], 'L3_gnn_b2': _L3_gnn_in['b2'], 'L3_gnn_W3': _L3_gnn_in['W3'], 'L3_gnn_b3': _L3_gnn_in['b3'], 'L3_gnn_W4': _L3_gnn_in['W4'], 'L3_gnn_b4': _L3_gnn_in['b4'], 'L3_gnn_gamma': _L3_gnn_in['gamma'], 'L3_gnn_beta': _L3_gnn_in['beta']}

def reference(x, src, dst, edge_attr_2, edge_attr_64, edge_weight, L0_gnn_weight, L1_gnn_Wl, L1_gnn_bl, L1_gnn_Wr, L1_gnn_br, L1_gnn_We, L1_gnn_att, L1_gnn_b_out, L1_gnn_gamma, L1_gnn_beta, L2_gnn_W1, L2_gnn_b1, L2_gnn_W2, L2_gnn_b2, L3_gnn_W1, L3_gnn_b1, L3_gnn_W2, L3_gnn_b2, L3_gnn_W3, L3_gnn_b3, L3_gnn_W4, L3_gnn_b4, L3_gnn_gamma, L3_gnn_beta):
    import jax
    import jax.numpy as jnp

    def _L0_gnn_ref(x, weight, row, col, vals):
        import jax, jax.numpy as jnp
        import numpy as np
        N_NODES = 2048
        N_EDGES = 16384
        FEAT_DIM = 512
        EMBED_DIM = 512
        h = jnp.einsum('nf,ef->ne', x, weight)
        msgs = vals[:, None] * h[col]
        out = jax.ops.segment_sum(msgs, row, num_segments=N_NODES)
        return out

    def _L1_gnn_ref(x, edge_attr, Wl, bl, Wr, br, We, att, b_out, gamma, beta, edge_index):
        import jax, jax.numpy as jnp
        import numpy as np
        N, E, D, ED, L = (512, 8192, 512, 2, 3)
        EPS = 1e-05
        SLOPE = 0.2

        def _segment_softmax(logits, seg, n):
            m = jax.ops.segment_max(logits, seg, num_segments=n)
            m = jnp.where(jnp.isfinite(m), m, 0.0)
            ex = jnp.exp(logits - m[seg])
            den = jax.ops.segment_sum(ex, seg, num_segments=n)
            return ex / (den[seg] + 1e-16)

        def _forward(x, edge_attr, Wl, bl, Wr, br, We, att, b_out, gamma, beta, edge_index):
            n = x.shape[0]
            src, dst = (edge_index[0], edge_index[1])
            ones = jnp.ones((src.shape[0],), x.dtype)
            cnt = jax.ops.segment_sum(ones, dst, num_segments=n)
            mean_ea = jax.ops.segment_sum(edge_attr, dst, num_segments=n) / jnp.maximum(cnt, 1.0)[:, None]
            loop = jnp.arange(n, dtype=edge_index.dtype)
            src2 = jnp.concatenate([src, loop])
            dst2 = jnp.concatenate([dst, loop])
            ea2 = jnp.concatenate([edge_attr, mean_ea], axis=0)
            for k in range(Wl.shape[0]):
                xl = x @ Wl[k] + bl[k]
                xr = x @ Wr[k] + br[k]
                ef = ea2 @ We[k]
                m = jax.nn.leaky_relu(xl[src2] + xr[dst2] + ef, SLOPE)
                logit = m @ att[k]
                alpha = _segment_softmax(logit, dst2, n)
                out = jax.ops.segment_sum(xl[src2] * alpha[:, None], dst2, num_segments=n) + b_out[k]
                h = out + x
                mu = jnp.mean(h, axis=-1, keepdims=True)
                var = jnp.var(h, axis=-1, keepdims=True)
                h = (h - mu) * jax.lax.rsqrt(var + EPS) * gamma[k] + beta[k]
                x = jax.nn.relu(h)
            return x
        return _forward(x, edge_attr, Wl, bl, Wr, br, We, att, b_out, gamma, beta, edge_index)

    def _L2_gnn_ref(x, edge_index, W1, b1, W2, b2):
        import jax, jax.numpy as jnp
        import numpy as np
        N_NODES = 10000

        def gcn_conv(x, edge_index, W, b):
            n = x.shape[0]
            h = x @ W
            loop = jnp.arange(n, dtype=edge_index.dtype)
            src = jnp.concatenate([edge_index[0], loop])
            dst = jnp.concatenate([edge_index[1], loop])
            ones = jnp.ones(src.shape[0], dtype=h.dtype)
            deg = jax.ops.segment_sum(ones, dst, num_segments=n)
            dis = jnp.where(deg > 0, jax.lax.rsqrt(deg), 0.0)
            norm = dis[src] * dis[dst]
            msg = h[src] * norm[:, None]
            out = jax.ops.segment_sum(msg, dst, num_segments=n)
            return out + b
        h = jax.nn.relu(gcn_conv(x, edge_index, W1, b1))
        out = gcn_conv(h, edge_index, W2, b2)
        return out

    def _L3_gnn_ref(x, edge_index, edge_attr, W1, b1, W2, b2, W3, b3, W4, b4, gamma, beta):
        import jax, jax.numpy as jnp
        import numpy as np
        N_NODES = 625
        N_EDGES = 10000
        HIDDEN = 512
        EDGE_DIM = 64
        LN_EPS = 1e-05

        def mish(x):
            return x * jnp.tanh(jax.nn.softplus(x))
        src, dst = (edge_index[0], edge_index[1])
        edge_feat = jnp.concatenate([x[src], x[dst], edge_attr], axis=-1)
        h = mish(edge_feat @ W1 + b1)
        messages = mish(h @ W2 + b2)
        agg = jax.ops.segment_sum(messages, dst, num_segments=x.shape[0])
        u = mish(jnp.concatenate([x, agg], axis=-1) @ W3 + b3)
        out = u @ W4 + b4
        y = x + out
        mu = jnp.mean(y, axis=-1, keepdims=True)
        var = jnp.mean(jnp.square(y - mu), axis=-1, keepdims=True)
        return (y - mu) * jax.lax.rsqrt(var + LN_EPS) * gamma + beta
    edge_index = jnp.stack([src, dst])
    x = _layernorm(x + _L0_gnn_ref(x, L0_gnn_weight, src, dst, edge_weight), axis=-1)
    x = _layernorm(x + _L1_gnn_ref(x, edge_attr_2, L1_gnn_Wl, L1_gnn_bl, L1_gnn_Wr, L1_gnn_br, L1_gnn_We, L1_gnn_att, L1_gnn_b_out, L1_gnn_gamma, L1_gnn_beta, edge_index), axis=-1)
    x = _layernorm(x + _L2_gnn_ref(x, edge_index, L2_gnn_W1, L2_gnn_b1, L2_gnn_W2, L2_gnn_b2), axis=-1)
    x = _layernorm(x + _L3_gnn_ref(x, edge_index, edge_attr_64, L3_gnn_W1, L3_gnn_b1, L3_gnn_W2, L3_gnn_b2, L3_gnn_W3, L3_gnn_b3, L3_gnn_W4, L3_gnn_b4, L3_gnn_gamma, L3_gnn_beta), axis=-1)
    return x

_drawn_inputs = setup_inputs


def setup_inputs(seed=0):
    import zlib

    import numpy as np

    out = dict(_drawn_inputs(seed))
    spreads = {'L1_gnn_bl': (0.0, 0.1),
     'L1_gnn_br': (0.0, 0.8),
     'L1_gnn_b_out': (0.0, 0.1),
     'L1_gnn_gamma': (1.0, 0.2),
     'L1_gnn_beta': (0.0, 0.1),
     'L2_gnn_b1': (0.0, 0.1),
     'L2_gnn_b2': (0.0, 0.1),
     'L3_gnn_b1': (0.0, 0.1),
     'L3_gnn_b2': (0.0, 0.1),
     'L3_gnn_b3': (0.0, 0.391),
     'L3_gnn_b4': (0.0, 0.306),
     'L3_gnn_gamma': (1.0, 0.2),
     'L3_gnn_beta': (0.0, 0.1)}
    factors = {'edge_attr_2': 8.0, 'L1_gnn_We': 7.548}
    for name, (base, spread) in spreads.items():
        noise = np.random.default_rng([zlib.crc32(name.encode()), seed]).standard_normal(out[name].shape)
        drawn = base * np.exp(spread * noise) if base else spread * noise
        out[name] = jnp.asarray(drawn.astype(out[name].dtype))
    for name, factor in factors.items():
        out[name] = (out[name] * factor).astype(out[name].dtype)
    return out
```

```python
from contextlib import ExitStack

import concourse.bass as bass
from concourse import mybir

F32 = mybir.dt.float32
I32 = mybir.dt.int32
ALU = mybir.AluOpType
ACT = mybir.ActivationFunctionType
AX = mybir.AxisListType

P = 128
N, D, E = 2048, 512, 32768
T = N // P
KD = D // P
EC = E // P
EA = 64
NCH = 272
C1 = T + NCH
HW = 5
RW = HW + EA
SW = 4
TW = 520
SLOPE = 0.2
EPS = 1e-5
FAR = 1e30
U = 8
assert NCH * P >= E + T * (P - 1) and NCH % U == 0 and C1 % U == 0


class Chip:
    pass



def wait(eng, sem, value):
    if isinstance(value, int) and value <= 0:
        return
    eng.wait_ge(sem, value)


def wait_apart(eng, sem, value, passed):
    if isinstance(value, int) and value <= 0:
        return
    eng.wait_ge(sem, value)
    eng.sem_inc(passed, 1)


def back(k, u, lag):
    return k * U + (u - lag), (u - lag) % U, (k if u >= lag else k - 1)


def live(i, count):
    return not isinstance(i, int) or 0 <= i < count


def run_steps(eng, count, step, lag=0):
    for u in range(U):
        step(0, u)
    with eng.Fori(1, count // U) as k:
        for u in range(U):
            step(k, u)
    for u in range(lag):
        step(count // U, u)


def tile_of(buf, t):
    return buf[:, t * D:(t + 1) * D] if isinstance(t, int) else buf[:, bass.ds(t * D, D)]


def col(buf, i, n=1):
    return buf[:, i * n:(i + 1) * n] if isinstance(i, int) else buf[:, bass.ds(i * n, n)]


def end_stage(nc, c):
    nc.clear_and_free_semaphores(c.sems)
    nc.all_engine_barrier()
    c.sems.clear()


def stage(build):
    def built(nc, c, *args, **named):
        build(nc, c, *args, **named)
        end_stage(nc, c)
    return built



@stage
def stage_constants(nc, c):
    s_fill, s_shape = c.sem("const_filled"), c.sem("const_shaped")
    with nc.Block() as block:
        @block.gpsimd
        def _(pool):
            pool.iota(c.iota_i[:, :], pattern=[[1, P]], base=0, channel_multiplier=0).then_inc(s_fill, 1)
            pool.iota(c.node_i[:, :], pattern=[[P, T]], base=0, channel_multiplier=1).then_inc(s_fill, 1)
            pool.iota(c.chunk_i[:, :], pattern=[[1, NCH]], base=0, channel_multiplier=0).then_inc(s_fill, 1)
            pool.iota(c.tile_i[:, :], pattern=[[1, T]], base=0, channel_multiplier=0).then_inc(s_fill, 1)
            pool.iota(c.lane_i[:, :], pattern=[[0, 1]], base=0, channel_multiplier=1).then_inc(s_fill, 1)
            pool.memset(c.ones[:, :], 1.0).then_inc(s_fill, 1)
            pool.memset(c.ident[:, :], 0.0).then_inc(s_fill, 1)
            pool.wait_ge(s_fill, 7)
            pool.affine_select(out=c.ident[:, :], in_=c.ident[:, :], compare_op=ALU.not_equal, fill=1.0, base=0,
                               pattern=[[-1, P]], channel_multiplier=1).then_inc(s_shape, 1)
            pool.affine_select(out=c.upper[:, :], in_=c.ones[:, :], compare_op=ALU.is_gt, fill=0.0, base=0,
                               pattern=[[1, P]], channel_multiplier=-1).then_inc(s_shape, 1)

        @block.vector
        def _(dve):
            dve.wait_ge(s_fill, 7)
            nc.vector.tensor_copy(c.iota[:, :], c.iota_i[:, :])
            nc.vector.tensor_copy(c.chunk_f[:, :], c.chunk_i[:, :])
            nc.vector.tensor_copy(c.lane_f[:, :], c.lane_i[:, :])
            nc.vector.memset(c.eps[:, :], EPS)
            nc.vector.tensor_copy(c.tiles_dst[0:1, 0:T], c.tile_i[0:1, :])


def bin_edges(nc, c, dve, chain, key, rec_local, rows, ends_sem, totals_sem, tiles_out, uses):
    def link(ins):
        chain[0] += 1
        ins.then_inc(c.s_chain, 1)
        dve.wait_ge(c.s_chain, chain[0])

    link(nc.vector.tensor_scalar(c.tmp_i[:, 0:EC], key, 7, None, ALU.logical_shift_right))
    link(nc.vector.tensor_copy(c.bin_f[:, :], c.tmp_i[:, 0:EC]))
    link(nc.vector.tensor_scalar(c.tmp_i[:, 0:EC], key, P - 1, None, ALU.bitwise_and))
    nc.vector.tensor_copy(rec_local, c.tmp_i[:, 0:EC])
    for b in range(T):
        last = nc.vector.tensor_scalar(c.member[:, b * EC:(b + 1) * EC], c.bin_f[:, :], float(b), None, ALU.is_equal)
    link(last)
    for b in range(T):
        last = nc.vector.tensor_tensor_scan(c.running[:, b * EC:(b + 1) * EC], c.edge_ones[:, :],
                                            c.member[:, b * EC:(b + 1) * EC], 0.0, ALU.mult, ALU.add)
    link(last)
    counts = c.running[:, :].rearrange("p (b j) -> p b j", b=T)[:, :, EC - 1]
    nc.vector.tensor_copy(c.counts[:, :], counts).then_inc(ends_sem, 1)
    dve.wait_ge(totals_sem, uses)
    before, total = c.ps[:, 0, 0:T], c.ps[:, 1, 0:T]
    link(nc.vector.tensor_scalar(c.small[:, 0:T], total, float(P - 1), None, ALU.add))
    link(nc.vector.tensor_copy(c.small_i[:, 0:T], c.small[:, 0:T]))
    link(nc.vector.tensor_scalar(c.small_i[:, T:2 * T], c.small_i[:, 0:T], 7, None, ALU.logical_shift_right))
    link(nc.vector.tensor_copy(c.small[:, T:2 * T], c.small_i[:, T:2 * T]))
    link(nc.vector.tensor_tensor_scan(c.small[:, 2 * T:3 * T], c.ones[:, 0:T], c.small[:, T:2 * T], 0.0,
                                      ALU.mult, ALU.add))
    link(nc.vector.tensor_tensor(c.small[:, 3 * T:4 * T], c.small[:, 2 * T:3 * T], c.small[:, T:2 * T], ALU.subtract))
    link(nc.vector.tensor_scalar(c.small[:, 3 * T:4 * T], c.small[:, 3 * T:4 * T], float(P), -1.0, ALU.mult, ALU.add))
    link(nc.vector.tensor_tensor(c.small[:, 3 * T:4 * T], c.small[:, 3 * T:4 * T], before, ALU.add))
    for b in range(T):
        run = c.running[:, b * EC:(b + 1) * EC]
        last = nc.vector.scalar_tensor_tensor(run, run, c.small[:, 3 * T + b:3 * T + b + 1],
                                              c.member[:, b * EC:(b + 1) * EC], ALU.add, ALU.mult)
    link(last)
    link(nc.vector.tensor_reduce(c.bin_f[:, :], c.running[:, :].rearrange("p (b j) -> p j b", b=T), AX.X, ALU.add))
    link(nc.vector.tensor_copy(c.tmp_i[:, 0:EC], c.bin_f[:, :]))
    nc.vector.tensor_scalar(c.tmp_i[:, EC:2 * EC], c.tmp_i[:, 0:EC], 7, None, ALU.logical_shift_right)
    link(nc.vector.tensor_scalar(c.tmp_i[:, 2 * EC:3 * EC], c.tmp_i[:, 0:EC], P - 1, None, ALU.bitwise_and))
    nc.vector.tensor_copy(c.bin_f[:, :], c.tmp_i[:, EC:2 * EC])
    link(nc.vector.tensor_copy(c.bin_g[:, :], c.tmp_i[:, 2 * EC:3 * EC]))
    link(nc.vector.scalar_tensor_tensor(c.bin_g[:, :], c.bin_g[:, :], float(NCH), c.bin_f[:, :], ALU.mult, ALU.add))
    link(nc.vector.tensor_copy(rows, c.bin_g[:, :]))
    link(nc.vector.memset(c.tile_f[0:1, :], 0.0))
    for b in range(T - 1):
        link(nc.vector.scalar_tensor_tensor(c.tile_f[0:1, :], c.chunk_f[0:1, :], c.small[0:1, 2 * T + b:2 * T + b + 1],
                                            c.tile_f[0:1, :], ALU.is_ge, ALU.add))
    link(nc.vector.tensor_copy(tiles_out, c.tile_f[0:1, :]))


@stage
def stage_bin(nc, c, src, dst, edge_attr_2, edge_attr_64, edge_weight):
    s_key, s_attr, s_wide, s_pads = (c.sem(f"bin_{n}") for n in ("keys_in", "attrs_in", "wide_in", "pads_out"))
    s_cnt, s_tot, s_pad = (c.sem(f"bin_{n}") for n in ("counts", "totals", "pad_rows"))
    c.chain, c.s_chain = [0], c.sem("bin_chain")
    by_p = lambda a: a.rearrange("(p j) -> p j", p=P)
    with nc.Block() as block:
        @block.sync
        def _(sp):
            sp.dma_start(c.key_src[:, :], by_p(src)).then_inc(s_key, 16)
            sp.dma_start(c.key_dst[:, :], by_p(dst)).then_inc(s_key, 16)
            sp.dma_start(c.attr2[:, :], edge_attr_2.rearrange("(p j) a -> p (j a)", p=P)).then_inc(s_attr, 16)
            sp.dma_start(c.weight[:, :], by_p(edge_weight)).then_inc(s_attr, 16)
            sp.dma_start(c.recs3[:, :, HW:RW], edge_attr_64.rearrange("(p j) a -> p j a", p=P)).then_inc(s_wide, 16)
            sp.wait_ge(s_pad, 2)
            for n in range(NCH // c.PADS):
                sp.dma_start(c.by_dst.rearrange("(p c) w -> p (c w)", p=P)[:, n * c.PADS * RW:(n + 1) * c.PADS * RW],
                             c.pads[:, :]).then_inc(s_pads, 16)
            sp.dma_start(c.by_src.rearrange("(p c) w -> p (c w)", p=P), c.pads0[:, :]).then_inc(s_pads, 16)
            sp.wait_ge(s_pads, 16 * (NCH // c.PADS + 1))
            sp.wait_ge(s_wide, 16)

        @block.gpsimd
        def _(pool):
            s_zero = c.sem("bin_zeroed")
            pool.memset(c.pads[:, :], 0.0).then_inc(s_zero, 1)
            pool.memset(c.pads0[:, :], 0.0).then_inc(s_zero, 1)
            pool.wait_ge(s_zero, 2)
            pool.memset(c.pads[:, :].rearrange("p (c w) -> p c w", w=RW)[:, :, 1], -1.0).then_inc(s_pad, 1)
            pool.memset(c.pads0[:, :].rearrange("p (c w) -> p c w", w=SW)[:, :, 1], -1.0).then_inc(s_pad, 1)

        @block.tensor
        def _(pe):
            for n in range(2):
                pe.wait_ge(s_cnt, n + 1)
                nc.tensor.matmul(c.ps[:, 0, 0:T], c.upper[:, :], c.counts[:, :], start=True, stop=True)
                nc.tensor.matmul(c.ps[:, 1, 0:T], c.ones[:, :], c.counts[:, :], start=True, stop=True).then_inc(s_tot, 1)

        @block.vector
        def _(dve):
            chain = c.chain
            nc.vector.memset(c.edge_ones[:, :], 1.0)
            nc.vector.memset(c.recs3[:, :, 4], 1.0)
            nc.vector.memset(c.recs0_3[:, :, 3], 0.0)
            dve.wait_ge(s_key, 32)
            nc.vector.tensor_copy(c.recs3_i[:, :, 0], c.key_src[:, :])
            nc.vector.tensor_copy(c.recs0_3i[:, :, 0], c.key_dst[:, :])
            bin_edges(nc, c, dve, chain, c.key_dst[:, :], c.recs3[:, :, 1], c.rows_dst[:, :], s_cnt, s_tot,
                      c.tiles_dst[0:1, T:C1], 1)
            bin_edges(nc, c, dve, chain, c.key_src[:, :], c.recs0_3[:, :, 1], c.rows_src[:, :], s_cnt, s_tot,
                      c.tiles_src[0:1, :], 2)
            dve.wait_ge(s_attr, 32)
            nc.vector.tensor_copy(c.recs3[:, :, 2:4], c.attr2[:, :].rearrange("p (j a) -> p j a", a=2))
            nc.vector.tensor_copy(c.recs0_3[:, :, 2], c.weight[:, :])


@stage
def stage_scatter(nc, c):
    s_rec, s_rec0 = c.sem("scatter_staged_dst"), c.sem("scatter_staged_src")
    s_passed, s_idx = c.sem("scatter_wait_passed"), c.sem("scatter_rows_copied")
    s_out = [c.sem(f"scatter_dst_out{u}") for u in range(U)]
    s_out0 = [c.sem(f"scatter_src_out{u}") for u in range(U)]
    with nc.Block() as block:
        @block.scalar
        def _(act):
            def step(k, u):
                i = k * U + u
                wait_apart(act, s_out[u], 16 * k, s_passed)
                nc.scalar.activation(c.stage[:, u * RW:(u + 1) * RW], col(c.recs, i, RW), ACT.Copy).then_inc(s_rec, 1)
                wait_apart(act, s_out0[u], 16 * k, s_passed)
                nc.scalar.activation(c.stage0[:, u * SW:(u + 1) * SW], col(c.recs0, i, SW), ACT.Copy).then_inc(s_rec0, 1)
            run_steps(act, EC, step)

        @block.gpsimd
        def _(pool):
            half = U // 2

            def step(k, u):
                i = k * U + u
                if u % half == 0:
                    h = u // half
                    for v in range(u, u + half):
                        wait_apart(pool, s_out[v], 16 * k, s_passed)
                        wait_apart(pool, s_out0[v], 16 * k, s_passed)
                    n = k * 2 + h
                    nc.gpsimd.tensor_copy(c.idx[:, h * half:(h + 1) * half], col(c.rows_dst, n, half)).then_inc(s_idx, 1)
                    nc.gpsimd.tensor_copy(c.idx0[:, h * half:(h + 1) * half], col(c.rows_src, n, half)).then_inc(s_idx, 1)
                    wait_apart(pool, s_idx, 2 * n + 2, s_passed)
                wait_apart(pool, s_rec, i + 1, s_passed)
                pool.indirect_dma_start(out=c.by_dst, out_offset=bass.IndirectOffsetOnAxis(ap=c.idx[:, u:u + 1], axis=0),
                                        in_=c.stage[:, u * RW:(u + 1) * RW], in_offset=None).then_inc(s_out[u], 16)
                wait_apart(pool, s_rec0, i + 1, s_passed)
                pool.indirect_dma_start(out=c.by_src, out_offset=bass.IndirectOffsetOnAxis(ap=c.idx0[:, u:u + 1], axis=0),
                                        in_=c.stage0[:, u * SW:(u + 1) * SW], in_offset=None).then_inc(s_out0[u], 16)
            run_steps(pool, EC, step)
            for u in range(U):
                pool.wait_ge(s_out[u], 16 * (EC // U))
                pool.wait_ge(s_out0[u], 16 * (EC // U))


@stage
def stage_heads(nc, c, x):
    s_all, s_head0, s_x = c.sem("heads_rows_in"), c.sem("heads_src_in"), c.sem("nodes_in")
    with nc.Block() as block:
        @block.sync
        def _(sp):
            sp.dma_start(c.wide[:, :], c.by_dst.rearrange("(p c) w -> p (c w)", p=P)).then_inc(s_all, 16)
            sp.dma_start(c.rec0[:, :], c.by_src.rearrange("(p c) w -> p (c w)", p=P)).then_inc(s_head0, 16)
            sp.wait_ge(s_head0, 16)

        @block.vector
        def _(dve):
            dve.wait_ge(s_all, 16)
            wide = c.wide[:, :].rearrange("p (c w) -> p c w", w=RW)
            nc.vector.tensor_copy(c.rec3[:, T:C1, 1:HW], wide[:, :, 1:HW])
            nc.vector.tensor_copy(c.rec3_i[:, T:C1, 0], wide.bitcast(I32)[:, :, 0])
    with nc.Block() as block:
        @block.sync
        def _(sp):
            sp.dma_start(c.X[:, :].rearrange("p (t d) -> p t d", t=T), x.rearrange("(t p) d -> p t d", p=P)).then_inc(s_x, 16)
            sp.wait_ge(s_x, 16)


@stage
def stage_degrees(nc, c):
    s_hot, s_sum, s_add, s_last = (c.sem(f"degree_{n}") for n in ("onehot", "summed", "added", "zeroed"))
    with nc.Block() as block:
        @block.vector
        def _(dve):
            nc.vector.memset(c.deg[:, :], 0.0).then_inc(s_last, 1)
            dve.wait_ge(s_last, 1)

            def step(k, u):
                i, s, _ = back(k, u, 0)
                if live(i, NCH):
                    wait(dve, s_sum, i - 1)
                    nc.vector.tensor_scalar(c.hot[:, u % 2, :], c.iota[:, :], col(c.rec, T + i, HW)[:, 1:2], None,
                                            ALU.is_equal).then_inc(s_hot, 1)
                j, s, _ = back(k, u, 1)
                if live(j, NCH):
                    t = dve.value_load(c.tiles_dst[0:1, T + j:T + j + 1] if isinstance(j, int)
                                       else c.tiles_dst[0:1, bass.ds(T + j, 1)], min_val=0, max_val=T - 1)
                    wait(dve, s_sum, j + 1)
                    wait(dve, s_add, j)
                    acc = c.deg[:, bass.ds(t * 3, 3)]
                    nc.vector.tensor_tensor(acc, acc, c.ps[:, s % 2, 0:3], ALU.add).then_inc(s_add, 1)
            run_steps(dve, NCH, step, lag=1)

        @block.tensor
        def _(pe):
            def step(k, u):
                i = k * U + u
                wait(pe, s_hot, i + 1)
                wait(pe, s_add, i - 1)
                nc.tensor.matmul(c.ps[:, u % 2, 0:3], c.hot[:, u % 2, :], col(c.rec, T + i, HW)[:, 2:5],
                                 start=True, stop=True).then_inc(s_sum, 1)
            run_steps(pe, NCH, step)
    c.chain, c.s_chain = [0], c.sem("degree_chain")
    s_sq, s_rt = c.sem("degree_plus_one"), c.sem("degree_root")
    with nc.Block() as block:
        @block.vector
        def _(dve):
            def link(ins):
                c.chain[0] += 1
                ins.then_inc(c.s_chain, 1)
                dve.wait_ge(c.s_chain, c.chain[0])
            deg = c.deg[:, :].rearrange("p (t w) -> p t w", w=3)
            nc.vector.tensor_scalar(c.deg1[:, :], deg[:, :, 2], 1.0, None, ALU.add).then_inc(s_sq, 1)
            link(nc.vector.tensor_scalar(c.dis[:, :], deg[:, :, 2], 1.0, None, ALU.max))
            link(nc.vector.reciprocal(c.small[:, 0:T], c.dis[:, :]))
            for a in range(2):
                nc.vector.tensor_tensor(c.rec3[:, 0:T, 2 + a], deg[:, :, a], c.small[:, 0:T], ALU.mult)
            nc.vector.tensor_copy(c.rec3_i[:, 0:T, 0], c.node_i[:, :])
            nc.vector.tensor_scalar(c.rec3[:, 0:T, 1], c.ones[:, 0:T], c.lane_f[:, :], None, ALU.mult)
            nc.vector.tensor_copy(c.rec3[:, 0:T, 4], c.ones[:, 0:T])
            dve.wait_ge(s_rt, 1)
            nc.vector.reciprocal(c.dis[:, :], c.root[:, 0:T])

        @block.scalar
        def _(act):
            act.wait_ge(s_sq, 1)
            nc.scalar.activation(c.root[:, 0:T], c.deg1[:, :], ACT.Sqrt).then_inc(s_rt, 1)



def load_weights(sp, c, sem, w, slot):
    sp.dma_start(c.W[:, slot, :].rearrange("p (k o) -> p k o", k=KD), w.rearrange("(k p) o -> p k o", p=P)).then_inc(sem, 16)


@stage
def stage_transpose_weight(nc, c, w):
    s_in, s_t, s_c = c.sem("wt_in"), c.sem("wt_turned"), c.sem("wt_copied")
    with nc.Block() as block:
        @block.sync
        def _(sp):
            load_weights(sp, c, s_in, w, 0)

        @block.tensor
        def _(pe):
            pe.wait_ge(s_in, 16)
            for k in range(KD):
                for o in range(KD):
                    last = nc.tensor.transpose(c.ps[:, k, o * P:(o + 1) * P], c.W[:, 0, o * D + k * P:o * D + (k + 1) * P],
                                               c.ident[:, :])
                last.then_inc(s_t, 1)

        @block.vector
        def _(dve):
            for k in range(KD):
                dve.wait_ge(s_t, k + 1)
                nc.vector.tensor_copy(c.W[:, 1, k * D:(k + 1) * D], c.ps[:, k, :])


@stage
def stage_linear(nc, c, name, sources, outputs, weights=(), rows=(), table=None):
    S, O = len(sources), len(outputs)
    s_w, s_in, s_turn, s_even, s_prod, s_fin, s_store = (
        c.sem(f"{name}_{n}") for n in ("weights_in", "staged", "turned", "turned_copied", "product", "finished", "stored0"))
    s_store = [s_store, c.sem(f"{name}_stored1")]
    with nc.Block() as block:
        @block.sync
        def _(sp):
            for w, slot in weights:
                load_weights(sp, c, s_w, w, slot)
            for buf, a in rows:
                sp.dma_start(buf, a.partition_broadcast(P)).then_inc(s_w, 16)
            if table is not None:
                width = table.shape[1]

                def store(k, u):
                    t = k * 2 + u
                    wait(sp, s_fin, O * t + 1)
                    row = table[t * P:(t + 1) * P, :] if isinstance(t, int) else table[bass.ds(t * P, P), :]
                    sp.dma_start(row, c.out[:, u, 0:width]).then_inc(s_store[u], 16)
                with sp.Fori(0, T // 2) as k:
                    for u in range(2):
                        store(k, u)
                for u in range(2):
                    sp.wait_ge(s_store[u], 16 * (T // 2))

        @block.scalar
        def _(act):
            def stage(t, s, slot):
                nc.scalar.activation(c.xs[:, slot, :], tile_of(sources[s], t), ACT.Copy).then_inc(s_in, 1)

            def turn(q, slot, t, o_done):
                wait(act, s_turn, q + 1)
                wait(act, s_prod, o_done)
                nc.scalar.activation(c.xT[:, slot, :], c.ps[:, slot, :], ACT.Copy).then_inc(s_even, 1)

            def pair(k, first=False):
                for u in range(2):
                    t = k * 2 + u
                    for s in range(S):
                        slot = (u * S + s) % 2
                        q = t * S + s
                        turn(q, slot, t, 0 if first and q < 2 else O * ((q - 2) // S + 1) if first else
                             (O * (t - 1) if S == 1 else O * t))
                        if first or not isinstance(t, int) or q + 2 < T * S:
                            pass
                        nq = u * S + s + 2
                        if isinstance(k, int) and k == T // 2 - 1 and nq >= 2 * S:
                            continue
                        stage(k * 2 + nq // S, nq % S, slot)
            stage(0, 0, 0)
            stage(1 // S, 1 % S, 1)
            pair(0, first=True)
            with act.Fori(1, T // 2 - 1) as k:
                pair(k)
            pair(T // 2 - 1)

        @block.tensor
        def _(pe):
            pe.wait_ge(s_w, 16 * (len(weights) + len(rows))) if weights or rows else None

            def turn(q, slot):
                wait(pe, s_in, q + 1)
                wait(pe, s_even, q - 1)
                for b in range(KD):
                    last = nc.tensor.transpose(c.ps[:, slot, b * P:(b + 1) * P], c.xs[:, slot, b * P:(b + 1) * P],
                                               c.ident[:, :])
                last.then_inc(s_turn, 1)

            def multiply(t, u, s, slot):
                wait(pe, s_even, t * S + s + 1)
                for o in range(O):
                    if s == 0:
                        wait(pe, s_fin, O * (t - 2) + o + 1)
                    for b in range(KD):
                        last = nc.tensor.matmul(c.ps[:, 2 + 2 * o + u, :], c.xT[:, slot, b * P:(b + 1) * P],
                                                c.W[:, outputs[o][0][s], b * D:(b + 1) * D],
                                                start=(s == 0 and b == 0), stop=(s == S - 1 and b == KD - 1))
                    if s == S - 1:
                        last.then_inc(s_prod, 1)

            def pair(k, last_pair):
                for u in range(2):
                    t = k * 2 + u
                    for s in range(S):
                        q = t * S + s
                        if not (last_pair and u * S + s == 2 * S - 1):
                            turn(q + 1, (u * S + s + 1) % 2)
                        multiply(t, u, s, (u * S + s) % 2)
            turn(0, 0)
            pair(0, False)
            with pe.Fori(1, T // 2 - 1) as k:
                pair(k, False)
            pair(T // 2 - 1, True)

        @block.vector
        def _(dve):
            s_link = c.sem(f"{name}_link")
            if rows:
                dve.wait_ge(s_w, 16 * (len(weights) + len(rows)))

            def step(k, u):
                t = k * 2 + u
                wait(dve, s_fin, O * t)
                count = [0]
                per_tile = outputs_links(outputs)

                def link(ins):
                    count[0] += 1
                    ins.then_inc(s_link, 1)
                    wait(dve, s_link, t * per_tile + count[0])
                for o in range(O):
                    wait(dve, s_prod, O * t + o + 1)
                    if o == 0 and table is not None:
                        wait(dve, s_store[u], 16 * k)
                    outputs[o][1](link, t, c.ps[:, 2 + 2 * o + u, :], c.out[:, u, :]).then_inc(s_fin, 1)
            for u in range(2):
                step(0, u)
            with dve.Fori(1, T // 2) as k:
                for u in range(2):
                    step(k, u)


def outputs_links(outputs):
    return sum(o[2] for o in outputs)


@stage
def stage_rows(nc, c, name, pairs):
    s_in = c.sem(f"{name}_rows_in")
    with nc.Block() as block:
        @block.sync
        def _(sp):
            for buf, a in pairs:
                sp.dma_start(buf, a.partition_broadcast(P)).then_inc(s_in, 16)
            sp.wait_ge(s_in, 16 * len(pairs))


@stage
def stage_norm(nc, c, name, h, out, gamma=None, beta=None, relu=False, residual=None, copy=None, store=None):
    s_stat, s_var, s_root = (c.sem(f"{name}_{n}") for n in ("stats", "variance", "root"))
    s_link, s_out = c.sem(f"{name}_link"), c.sem(f"{name}_out")
    mv = c.mv[:, :].rearrange("p (t w) -> p t w", w=2)
    full = lambda b: b[:, :].rearrange("p (t d) -> p t d", t=T)
    wide = lambda row: row.unsqueeze(1).to_broadcast([P, T, D])
    with nc.Block() as block:
        @block.vector
        def _(dve):
            n = [0]

            def link(ins):
                n[0] += 1
                ins.then_inc(s_link, 1)
                dve.wait_ge(s_link, n[0])
            for t in range(T):
                last = nc.vector.bn_stats(c.st[:, t * 6:(t + 1) * 6], tile_of(h, t))
            link(last)
            for t in range(T):
                last = nc.vector.bn_aggr(c.mv[:, t * 2:(t + 1) * 2], c.st[:, t * 6:(t + 1) * 6])
            last.then_inc(s_var, 1)
            dve.wait_ge(s_root, 1)
            link(nc.vector.reciprocal(c.rstd[:, :], c.root[:, 0:T]))
            for t in range(T):
                last = nc.vector.tensor_scalar(tile_of(out, t), tile_of(h, t), c.mv[:, 2 * t:2 * t + 1],
                                               c.rstd[:, t:t + 1], ALU.subtract, ALU.mult)
            if gamma is not None:
                link(last)
                link(nc.vector.tensor_tensor(full(out), full(out), wide(gamma), ALU.mult))
                last = nc.vector.tensor_tensor(full(out), full(out), wide(beta), ALU.add)
            if relu:
                link(last)
                last = nc.vector.tensor_scalar(out[:, :], out[:, :], 0.0, None, ALU.max)
            if residual is not None:
                link(last)
                last = nc.vector.tensor_tensor(out[:, :], out[:, :], residual[:, :], ALU.add)
            last.then_inc(s_stat, 1)

        @block.scalar
        def _(act):
            act.wait_ge(s_var, 1)
            nc.scalar.activation(c.root[:, 0:T], mv[:, :, 1], ACT.Sqrt, bias=c.eps[:, :]).then_inc(s_root, 1)

        @block.sync
        def _(sp):
            if store is not None:
                sp.wait_ge(s_stat, 1)
                sp.dma_start(store.rearrange("(t p) d -> p t d", p=P), full(out)).then_inc(s_out, 16)
                sp.wait_ge(s_out, 16)



def gather_rows(nc, c, pool, count, table, width, source, sems):
    half = U // 2

    def step(k, u):
        i = k * U + u
        if u % half == 0:
            h = u // half
            for v in range(u, u + half):
                wait_apart(pool, sems.got[v], 16 * k, sems.passed)
            n = k * 2 + h
            nc.gpsimd.tensor_copy(c.idx[:, h * half:(h + 1) * half], source(n, half)).then_inc(sems.idx, 1)
            wait_apart(pool, sems.idx, n + 1, sems.passed)
        wait_apart(pool, sems.used, i - U + 1, sems.passed)
        pool.indirect_dma_start(out=c.G[:, u, 0:width], out_offset=None, in_=table,
                                in_offset=bass.IndirectOffsetOnAxis(ap=c.idx[:, u:u + 1], axis=0)).then_inc(sems.got[u], 16)
    run_steps(pool, count, step)


def edge_sems(c, name):
    s = Chip()
    s.got = [c.sem(f"{name}_got{u}") for u in range(U)]
    s.idx, s.used, s.passed = c.sem(f"{name}_indices"), c.sem(f"{name}_rows_used"), c.sem(f"{name}_wait_passed")
    return s


def tile_index(eng, tiles, i):
    return eng.value_load(tiles[0:1, i:i + 1] if isinstance(i, int) else tiles[0:1, bass.ds(i, 1)],
                          min_val=0, max_val=T - 1)


@stage
def stage_aggregate(nc, c, name, count, table, rec, width, tiles, first, weighted):
    s = edge_sems(c, name)
    s_hot, s_add, s_zero = (c.sem(f"{name}_{n}") for n in ("onehot", "added", "zeroed"))
    rec_i = rec.bitcast(I32)

    def source(n, half):
        lo = first + n * half
        r = rec_i.rearrange("p (c w) -> p c w", w=width)
        return r[:, lo:lo + half, 0] if isinstance(n, int) else r[:, bass.ds(lo, half), 0]
    with nc.Block() as block:
        @block.gpsimd
        def _(pool):
            gather_rows(nc, c, pool, count, table, D, source, s)

        @block.tensor
        def _(pe):
            def step(k, u):
                i = k * U + u
                wait(pe, s.got[u], 16 * (k + 1))
                wait(pe, s_hot, i + 1)
                wait(pe, s_add, i - 1)
                nc.tensor.matmul(c.ps[:, u % 2, :], c.hot[:, u % 2, :], c.G[:, u, 0:D],
                                 start=True, stop=True).then_inc(s.used, 1)
            run_steps(pe, count, step)

        @block.vector
        def _(dve):
            nc.vector.memset(c.ACC[:, :], 0.0).then_inc(s_zero, 1)
            dve.wait_ge(s_zero, 1)

            def step(k, u):
                i = k * U + u
                if live(i, count):
                    wait(dve, s.used, i - 1)
                    r = col(rec, first + i, width)
                    if weighted:
                        ins = nc.vector.tensor_scalar(c.hot[:, u % 2, :], c.iota[:, :], r[:, 1:2], r[:, 2:3],
                                                      ALU.is_equal, ALU.mult)
                    else:
                        ins = nc.vector.tensor_scalar(c.hot[:, u % 2, :], c.iota[:, :], r[:, 1:2], None, ALU.is_equal)
                    ins.then_inc(s_hot, 1)
                j, slot, _ = back(k, u, 1)
                if live(j, count):
                    t = tile_index(dve, tiles, first + j)
                    wait(dve, s.used, j + 1)
                    wait(dve, s_add, j)
                    acc = tile_of(c.ACC, t)
                    nc.vector.tensor_tensor(acc, acc, c.ps[:, slot % 2, :], ALU.add).then_inc(s_add, 1)
            run_steps(dve, count, step, lag=1)


@stage
def stage_attention_edges(nc, c, name, table):
    s = edge_sems(c, name)
    (s_hot, s_neg, s_tr, s_ev, s_z, s_s, s_lg, s_lg1, s_msk, s_mT, s_mx, s_mn, s_df, s_upd, s_exp, s_pT, s_w, s_acc,
     s_den, s_init, s_sc) = (c.sem(f"{name}_{n}") for n in (
        "onehot", "far", "turned", "turned_copied", "product", "sum", "dot", "logit", "masked", "masked_turned", "chunk_max",
        "new_max", "shifts", "max_kept", "exp", "exp_turned", "exp_copied", "acc_added", "den_added", "init", "scale"))

    def source(n, half):
        r = c.rec_i[:, :].rearrange("p (c w) -> p c w", w=HW)
        return r[:, n * half:(n + 1) * half, 0] if isinstance(n, int) else r[:, bass.ds(n * half, half), 0]
    B_T, B_Z, B_M, B_O = 0, 2, 4, 6
    s_prep = c.sem(f"{name}_prep")
    with nc.Block() as block:
        @block.vector
        def _(dve):
            n = [0]

            def link(ins):
                n[0] += 1
                ins.then_inc(s_prep, 1)
                dve.wait_ge(s_prep, n[0])
            for a in range(2):
                link(nc.vector.tensor_tensor_reduce(out=c.S[:, 0, :], in0=c.WeB[:, a * D:(a + 1) * D], in1=c.attB[:, :],
                                                    scale=SLOPE, scalar=0.0, op0=ALU.mult, op1=ALU.add,
                                                    accum_out=c.cvec[:, a:a + 1]))
            link(nc.vector.tensor_scalar(c.lin[:, :], c.rec3[:, :, 2], c.cvec[:, 0:1], None, ALU.mult))
            link(nc.vector.scalar_tensor_tensor(c.lin[:, :], c.rec3[:, :, 3], c.cvec[:, 1:2], c.lin[:, :],
                                                ALU.mult, ALU.add))
            nc.vector.memset(c.ACC[:, :], 0.0)
            nc.vector.memset(c.den[:, :], 0.0)
            nc.vector.memset(c.MA[:, :].rearrange("p (t w) -> p t w", w=2)[:, :, 0], -FAR)
    with nc.Block() as block:
        @block.gpsimd
        def _(pool):
            half = U // 2

            def step(k, u):
                i = k * U + u
                if u % half == 0:
                    h = u // half
                    for v in range(u, u + half):
                        wait_apart(pool, s.got[v], 16 * k, s.passed)
                    n = k * 2 + h
                    nc.gpsimd.tensor_copy(c.idx[:, h * half:(h + 1) * half], source(n, half)).then_inc(s.idx, 1)
                    wait_apart(pool, s.idx, n + 1, s.passed)
                wait_apart(pool, s.used, i - U + 1, s.passed)
                pool.indirect_dma_start(out=c.G[:, u, 0:TW], out_offset=None, in_=table,
                                        in_offset=bass.IndirectOffsetOnAxis(ap=c.idx[:, u:u + 1], axis=0)).then_inc(s.got[u], 16)
            run_steps(pool, C1, step)

        @block.scalar
        def _(act):
            def step(k, u):
                i, v, _ = back(k, u, 0)
                if live(i, C1):
                    wait(act, s_tr, i + 1)
                    wait(act, s_z, i - 1)
                    nc.scalar.activation(c.oT[:, v % 2, :], c.ps[:, B_T + v % 2, 0:P], ACT.Copy)
                    nc.scalar.activation(c.eT[0:2, v % 2, :], c.ps[0:2, B_T + v % 2, P:2 * P], ACT.Copy).then_inc(s_ev, 1)
                j, v, _ = back(k, u, 2)
                if live(j, C1):
                    wait(act, s_df, j + 1)
                    wait(act, s_den, j - 1)
                    nc.scalar.activation(c.scale[:, v % 2:v % 2 + 1], c.diff[:, 2 * (v % 2):2 * (v % 2) + 1],
                                         ACT.Exp).then_inc(s_sc, 1)
                    wait(act, s_pT, j - 1)
                    nc.scalar.activation(c.PT[:, v % 2, :], c.ps[:, B_M + v % 2, 0:P], ACT.Exp,
                                         bias=c.diff[:, 2 * (v % 2) + 1:2 * (v % 2) + 2],
                                         accum_out=c.rowsum[:, v % 2:v % 2 + 1]).then_inc(s_exp, 1)
                    wait(act, s_pT, j + 1)
                    wait(act, s.used, j - 1)
                    nc.scalar.activation(c.Wt[:, v % 2, :], c.ps[:, B_M + v % 2, P:2 * P], ACT.Copy).then_inc(s_w, 1)
            run_steps(act, C1, step, lag=2)

        @block.tensor
        def _(pe):
            def step(k, u):
                i, v, _ = back(k, u, 0)
                if live(i, C1):
                    wait(pe, s_hot, i + 1)
                    wait(pe, s_ev, i - 1)
                    nc.tensor.transpose(c.ps[:, B_T + v % 2, 0:P], c.hot[:, v % 2, :], c.ident[:, :])
                    nc.tensor.transpose(c.ps[0:2, B_T + v % 2, P:2 * P], c.eat[:, v % 2, :], c.ident[:, :]).then_inc(s_tr, 1)
                j, v, _ = back(k, u, 1)
                if live(j, C1):
                    t = tile_index(pe, c.tiles_dst, j)
                    wait(pe, s_ev, j + 1)
                    wait(pe, s_s, j - 1)
                    nc.tensor.matmul(c.ps[:, B_Z + v % 2, :], c.oT[:, v % 2, :], tile_of(c.XR, t), start=True, stop=False)
                    nc.tensor.matmul(c.ps[:, B_Z + v % 2, :], c.eT[0:2, v % 2, :], c.We[0:2, :], start=False,
                                     stop=True).then_inc(s_z, 1)
                j, v, _ = back(k, u, 2)
                if live(j, C1):
                    wait(pe, s_msk, j + 1)
                    wait(pe, s_w, j - 1)
                    nc.tensor.transpose(c.ps[:, B_M + v % 2, 0:P], c.masked[:, v % 2, :], c.ident[:, :]).then_inc(s_mT, 1)
                j, v, _ = back(k, u, 3)
                if live(j, C1):
                    wait(pe, s_exp, j + 1)
                    nc.tensor.transpose(c.ps[:, B_M + v % 2, P:2 * P], c.PT[:, v % 2, :], c.ident[:, :]).then_inc(s_pT, 1)
                j, v, _ = back(k, u, 4)
                if live(j, C1):
                    wait(pe, s_w, j + 1)
                    wait(pe, s_acc, j - 1)
                    nc.tensor.matmul(c.ps[:, B_O + v % 2, :], c.Wt[:, v % 2, :], c.G[:, v, 0:D],
                                     start=True, stop=True).then_inc(s.used, 1)
            run_steps(pe, C1, step, lag=4)

        @block.vector
        def _(dve):
            def step(k, u):
                i, v, _ = back(k, u, 0)
                if live(i, C1):
                    r = col(c.rec, i, HW)
                    wait(dve, s_tr, i - 1)
                    nc.vector.tensor_scalar(c.hot[:, v % 2, :], c.iota[:, :], r[:, 1:2], None, ALU.is_equal)
                    nc.vector.tensor_copy(c.eat[:, v % 2, :], r[:, 2:4]).then_inc(s_hot, 1)
                    nc.vector.tensor_scalar(c.far[:, v % 4, :], c.iota[:, :], r[:, 1:2], -FAR, ALU.not_equal,
                                            ALU.mult).then_inc(s_neg, 1)
                j, v, r = back(k, u, 2)
                if live(j, C1):
                    wait(dve, s_z, j + 1)
                    wait(dve, s.got[v], 16 * (r + 1))
                    nc.vector.tensor_tensor(c.S[:, v % 2, :], c.ps[:, B_Z + v % 2, :], c.G[:, v, 0:D], ALU.add).then_inc(s_s, 1)
                    wait(dve, s_s, j + 1)
                    nc.vector.scalar_tensor_tensor(c.R[:, :], c.S[:, v % 2, :], 0.0, c.attB[:, :], ALU.max, ALU.mult,
                                                   accum_out=c.dot[:, v % 2:v % 2 + 1]).then_inc(s_lg, 1)
                    wait(dve, s_lg, j + 1)
                    nc.vector.scalar_tensor_tensor(c.lg[:, v % 2:v % 2 + 1], c.dot[:, v % 2:v % 2 + 1], 1.0 - SLOPE,
                                                   c.G[:, v, D:D + 1], ALU.mult, ALU.add).then_inc(s_lg1, 1)
                    wait(dve, s_lg1, j + 1)
                    wait(dve, s_neg, j + 1)
                    wait(dve, s_mT, j - 1)
                    nc.vector.tensor_scalar(c.masked[:, v % 2, :], c.far[:, v % 4, :], c.lg[:, v % 2:v % 2 + 1],
                                            col(c.lin, j), ALU.add, ALU.add).then_inc(s_msk, 1)
                j, v, _ = back(k, u, 3)
                if live(j, C1):
                    t = tile_index(dve, c.tiles_dst, j)
                    wait(dve, s_mT, j + 1)
                    nc.vector.tensor_reduce(c.cmax[:, v % 2:v % 2 + 1], c.ps[:, B_M + v % 2, 0:P], AX.X, ALU.max).then_inc(s_mx, 1)
                    wait(dve, s_mx, j + 1)
                    wait(dve, s_upd, j)
                    MA = c.MA[:, bass.ds(t * 2, 2)]
                    nc.vector.scalar_tensor_tensor(c.mnew[:, v % 2:v % 2 + 1], c.cmax[:, v % 2:v % 2 + 1], MA[:, 1:2],
                                                   MA[:, 0:1], ALU.add, ALU.max).then_inc(s_mn, 1)
                    wait(dve, s_mn, j + 1)
                    wait(dve, s_exp, j - 1)
                    nc.vector.tensor_scalar(c.diff[:, 2 * (v % 2):2 * (v % 2) + 2], MA, c.mnew[:, v % 2:v % 2 + 1], None,
                                            ALU.subtract).then_inc(s_df, 1)
                    wait(dve, s_df, j + 1)
                    nc.vector.tensor_scalar(MA[:, 0:1], c.mnew[:, v % 2:v % 2 + 1], 0.0, None, ALU.add).then_inc(s_upd, 1)
                j, v, _ = back(k, u, 5)
                if live(j, C1):
                    t = tile_index(dve, c.tiles_dst, j)
                    den = c.den[:, bass.ds(t, 1)]
                    acc = tile_of(c.ACC, t)
                    wait(dve, s_sc, j + 1)
                    wait(dve, s_exp, j + 1)
                    wait(dve, s_den, j)
                    nc.vector.scalar_tensor_tensor(den, den, c.scale[:, v % 2:v % 2 + 1], c.rowsum[:, v % 2:v % 2 + 1],
                                                   ALU.mult, ALU.add)
                    wait(dve, s.used, j + 1)
                    nc.vector.scalar_tensor_tensor(acc, acc, c.scale[:, v % 2:v % 2 + 1], c.ps[:, B_O + v % 2, :],
                                                   ALU.mult, ALU.add).then_inc(s_den, 1)
                    nc.vector.engine_nop().then_inc(s_acc, 1)
            run_steps(dve, C1, step, lag=5)


@stage
def stage_attention_close(nc, c, name, cur):
    s_link = c.sem(f"{name}_link")
    full = lambda b: b[:, :].rearrange("p (t d) -> p t d", t=T)
    with nc.Block() as block:
        @block.vector
        def _(dve):
            n = [0]

            def link(ins):
                n[0] += 1
                ins.then_inc(s_link, 1)
                dve.wait_ge(s_link, n[0])
            link(nc.vector.tensor_scalar(c.den[:, :], c.den[:, :], 1e-16, None, ALU.add))
            link(nc.vector.reciprocal(c.den[:, :], c.den[:, :]))
            for t in range(T):
                last = nc.vector.scalar_tensor_tensor(tile_of(c.XR, t), tile_of(c.ACC, t), c.den[:, t:t + 1],
                                                      tile_of(cur, t), ALU.mult, ALU.add)
            link(last)
            nc.vector.tensor_tensor(full(c.XR), full(c.XR), c.row2[:, :].unsqueeze(1).to_broadcast([P, T, D]), ALU.add)


@stage
def stage_messages(nc, c, table):
    s = edge_sems(c, "msg")
    (s_hot, s_ea, s_tr, s_ev, s_z, s_s, s_e, s_q, s_y, s_h, s_hT, s_hc, s_o, s_e2, s_q2, s_y2, s_m, s_agg, s_acc,
     s_init) = (c.sem(f"msg_{n}") for n in (
        "onehot", "attrs_in", "turned", "turned_copied", "product1", "sum", "sigmoid1", "square1", "ratio1", "hidden",
        "hidden_turned", "hidden_copied", "product2", "sigmoid2", "square2", "ratio2", "message", "agg", "acc_added", "init"))
    s_attr = [c.sem(f"msg_attr_in{u}") for u in range(U)]
    B_T, B_Z, B_H, B_O, B_A = 0, 2, 4, 5, 7
    rows = c.by_dst.rearrange("(p c) w -> p c w", p=P)

    def source(n, half):
        r = c.rec_i[:, :].rearrange("p (c w) -> p c w", w=HW)
        lo = n * half + T
        return r[:, lo:lo + half, 0] if isinstance(n, int) else r[:, bass.ds(lo, half), 0]
    with nc.Block() as block:
        @block.sync
        def _(sp):
            def step(k, u):
                i = k * U + u
                wait_apart(sp, s_tr, i - U + 1, s.passed)
                a = rows[:, i, HW:RW] if isinstance(i, int) else rows[:, bass.ds(i, 1), HW:RW]
                sp.dma_start(c.ea[:, u, :], a).then_inc(s_attr[u], 16)
            run_steps(sp, NCH, step)

        @block.gpsimd
        def _(pool):
            gather_rows(nc, c, pool, NCH, table, D, source, s)

        @block.tensor
        def _(pe):
            def step(k, u):
                i, v, r = back(k, u, 0)
                if live(i, NCH):
                    wait(pe, s_hot, i + 1)
                    wait(pe, s_attr[v], 16 * (r + 1))
                    wait(pe, s_ev, i - 1)
                    nc.tensor.transpose(c.ps[:, B_T + v % 2, 0:P], c.hot4[:, v % 4, :], c.ident[:, :])
                    nc.tensor.transpose(c.ps[0:EA, B_T + v % 2, P:2 * P], c.ea[:, v, :], c.ident[:, :]).then_inc(s_tr, 1)
                j, v, _ = back(k, u, 1)
                if live(j, NCH):
                    t = tile_index(pe, c.tiles_dst, T + j)
                    wait(pe, s_ev, j + 1)
                    wait(pe, s_s, j - 1)
                    nc.tensor.matmul(c.ps[:, B_Z + v % 2, :], c.oT[:, v % 2, :], tile_of(c.XR, t), start=True, stop=False)
                    nc.tensor.matmul(c.ps[:, B_Z + v % 2, :], c.eT[0:EA, v % 2, :], c.W1c[:, :], start=False,
                                     stop=True).then_inc(s_z, 1)
                j, v, _ = back(k, u, 2)
                if live(j, NCH):
                    wait(pe, s_h, j + 1)
                    wait(pe, s_hc, j)
                    for b in range(KD):
                        last = nc.tensor.transpose(c.ps[:, B_H, b * P:(b + 1) * P], c.H[:, v % 2, b * P:(b + 1) * P],
                                                   c.ident[:, :])
                    last.then_inc(s_hT, 1)
                j, v, _ = back(k, u, 3)
                if live(j, NCH):
                    wait(pe, s_hc, j + 1)
                    wait(pe, s_m, j - 1)
                    nc.tensor.matmul(c.ps[:, B_O + v % 2, :], c.ones[0:1, :], c.b2r[0:1, :], start=True, stop=False)
                    for b in range(KD):
                        last = nc.tensor.matmul(c.ps[:, B_O + v % 2, :], c.hT[:, v % 2, b * P:(b + 1) * P],
                                                c.W[:, 2, b * D:(b + 1) * D], start=False, stop=(b == KD - 1))
                    last.then_inc(s_o, 1)
                j, v, _ = back(k, u, 4)
                if live(j, NCH):
                    wait(pe, s_m, j + 1)
                    wait(pe, s_acc, j)
                    nc.tensor.matmul(c.ps[:, B_A, :], c.hot4[:, v % 4, :] if False else c.hotm[:, v % 2, :], c.M[:, v % 2, :],
                                     start=True, stop=True).then_inc(s_agg, 1)
            run_steps(pe, NCH, step, lag=4)

        @block.scalar
        def _(act):
            def step(k, u):
                i, v, _ = back(k, u, 0)
                if live(i, NCH):
                    wait(act, s_tr, i + 1)
                    wait(act, s_z, i - 1)
                    nc.scalar.activation(c.oT[:, v % 2, :], c.ps[:, B_T + v % 2, 0:P], ACT.Copy)
                    nc.scalar.activation(c.eT[0:EA, v % 2, :], c.ps[0:EA, B_T + v % 2, P:2 * P], ACT.Copy).then_inc(s_ev, 1)
                j, v, _ = back(k, u, 1)
                if live(j, NCH):
                    wait(act, s_s, j + 1)
                    wait(act, s_q, j)
                    nc.scalar.activation(c.Eb[:, 0, :], c.S[:, v % 2, :], ACT.Sigmoid, scale=-1.0).then_inc(s_e, 1)
                    wait(act, s_e, 2 * j + 1)
                    wait(act, s_y, j - 1)
                    nc.scalar.activation(c.Q[:, v % 2, :], c.Eb[:, 0, :], ACT.Square).then_inc(s_e, 1)
                    wait(act, s_e, 2 * j + 2)
                    nc.scalar.activation(c.Q[:, v % 2, :], c.Q[:, v % 2, :], ACT.Identity, bias=c.ones[:, 0:1]).then_inc(s_q, 1)
                j, v, _ = back(k, u, 2)
                if live(j, NCH):
                    wait(act, s_hT, j + 1)
                    wait(act, s_o, j - 1)
                    nc.scalar.activation(c.hT[:, v % 2, :], c.ps[:, B_H, :], ACT.Copy).then_inc(s_hc, 1)
                j, v, _ = back(k, u, 3)
                if live(j, NCH):
                    wait(act, s_o, j + 1)
                    wait(act, s_q2, j)
                    nc.scalar.activation(c.Eb[:, 1, :], c.ps[:, B_O + v % 2, :], ACT.Sigmoid, scale=-1.0).then_inc(s_e2, 1)
                    wait(act, s_e2, 2 * j + 1)
                    wait(act, s_y2, j - 1)
                    nc.scalar.activation(c.Q2[:, v % 2, :], c.Eb[:, 1, :], ACT.Square).then_inc(s_e2, 1)
                    wait(act, s_e2, 2 * j + 2)
                    nc.scalar.activation(c.Q2[:, v % 2, :], c.Q2[:, v % 2, :], ACT.Identity, bias=c.ones[:, 0:1]).then_inc(s_q2, 1)
            run_steps(act, NCH, step, lag=3)

        @block.vector
        def _(dve):
            nc.vector.memset(c.ACC[:, :], 0.0).then_inc(s_init, 1)
            dve.wait_ge(s_init, 1)

            def step(k, u):
                i, v, _ = back(k, u, 0)
                if live(i, NCH):
                    wait(dve, s_tr, i - 3)
                    nc.vector.tensor_scalar(c.hot4[:, v % 4, :], c.iota[:, :], col(c.rec, T + i, HW)[:, 1:2], None,
                                            ALU.is_equal).then_inc(s_hot, 1)
                j, v, r = back(k, u, 1)
                if live(j, NCH):
                    wait(dve, s_z, j + 1)
                    wait(dve, s.got[v], 16 * (r + 1))
                    wait(dve, s_h, j - 1)
                    nc.vector.tensor_tensor(c.S[:, v % 2, :], c.ps[:, B_Z + v % 2, :], c.G[:, v, 0:D], ALU.add).then_inc(s_s, 1)
                    nc.vector.engine_nop().then_inc(s.used, 1)
                j, v, _ = back(k, u, 2)
                if live(j, NCH):
                    wait(dve, s_q, j + 1)
                    wait(dve, s_h, j)
                    nc.vector.reciprocal(c.Y[:, :], c.Q[:, v % 2, :]).then_inc(s_y, 1)
                    wait(dve, s_y, j + 1)
                    wait(dve, s_hT, j - 1)
                    nc.vector.scalar_tensor_tensor(c.H[:, v % 2, :], c.Y[:, :], 0.5, c.S[:, v % 2, :], ALU.subtract,
                                                   ALU.mult).then_inc(s_h, 1)
                j, v, _ = back(k, u, 4)
                if live(j, NCH):
                    wait(dve, s_q2, j + 1)
                    wait(dve, s_m, j)
                    nc.vector.reciprocal(c.Y2[:, :], c.Q2[:, v % 2, :]).then_inc(s_y2, 1)
                    wait(dve, s_y2, j + 1)
                    wait(dve, s_agg, j - 1)
                    nc.vector.tensor_scalar(c.hotm[:, v % 2, :], c.iota[:, :], col(c.rec, T + j, HW)[:, 1:2], 2.0,
                                            ALU.is_equal, ALU.mult)
                    nc.vector.scalar_tensor_tensor(c.M[:, v % 2, :], c.Y2[:, :], 0.5, c.ps[:, B_O + v % 2, :], ALU.subtract,
                                                   ALU.mult).then_inc(s_m, 1)
                j, v, _ = back(k, u, 5)
                if live(j, NCH):
                    t = tile_index(dve, c.tiles_dst, T + j)
                    acc = tile_of(c.ACC, t)
                    wait(dve, s_agg, j + 1)
                    wait(dve, s_acc, j)
                    nc.vector.tensor_tensor(acc, acc, c.ps[:, B_A, :], ALU.add).then_inc(s_acc, 1)
            run_steps(dve, NCH, step, lag=5)


@stage
def stage_mish(nc, c, buf):
    s_e, s_q, s_y, s_m = (c.sem(f"mish_{n}") for n in ("sigmoid", "square", "ratio", "half"))
    with nc.Block() as block:
        @block.scalar
        def _(act):
            for t in range(T):
                if t >= 2:
                    act.wait_ge(s_y, t - 1)
                nc.scalar.activation(c.Q[:, t % 2, :], tile_of(buf, t), ACT.Sigmoid, scale=-1.0).then_inc(s_e, 1)
                act.wait_ge(s_e, 2 * t + 1)
                nc.scalar.activation(c.Q[:, t % 2, :], c.Q[:, t % 2, :], ACT.Square).then_inc(s_e, 1)
                act.wait_ge(s_e, 2 * t + 2)
                nc.scalar.activation(c.Q2[:, t % 2, :], c.Q[:, t % 2, :], ACT.Identity, bias=c.ones[:, 0:1]).then_inc(s_q, 1)

        @block.vector
        def _(dve):
            for t in range(T):
                b = tile_of(buf, t)
                dve.wait_ge(s_q, t + 1)
                nc.vector.reciprocal(c.H[:, t % 2, :], c.Q2[:, t % 2, :]).then_inc(s_y, 1)
                dve.wait_ge(s_y, t + 1)
                nc.vector.scalar_tensor_tensor(b, c.H[:, t % 2, :], 0.5, b, ALU.subtract, ALU.mult).then_inc(s_m, 1)
                dve.wait_ge(s_m, t + 1)
                nc.vector.tensor_scalar(b, b, 2.0, None, ALU.mult)


@stage
def stage_scaled_table(nc, c, table):
    s_sc, s_st = c.sem("scaled_ready"), c.sem("scaled_stored")
    with nc.Block() as block:
        @block.vector
        def _(dve):
            for t in range(T):
                last = nc.vector.tensor_scalar(tile_of(c.XR, t), tile_of(c.X, t), c.dis[:, t:t + 1], None, ALU.mult)
            last.then_inc(s_sc, 1)

        @block.sync
        def _(sp):
            sp.wait_ge(s_sc, 1)
            sp.dma_start(table.rearrange("(t p) d -> p t d", p=P), c.XR[:, :].rearrange("p (t d) -> p t d", t=T))\
              .then_inc(s_st, 16)
            sp.wait_ge(s_st, 16)


def gnn_stack(nc, a, out):
    ctx = ExitStack()
    with ctx:
        c = Chip()
        c.sems = []

        def sem(name):
            c.sems.append(nc.alloc_semaphore(name=name))
            return c.sems[-1]
        c.sem = sem

        def sb(name, shape, dt=F32):
            return ctx.enter_context(nc.sbuf_tensor(name, shape, dt))

        arena = sb("arena", [P, 3 * T * D])
        c.X, c.XR, c.ACC = (arena[:, n * T * D:(n + 1) * T * D] for n in range(3))
        gathered = sb("gathered", [P, U * TW])
        c.G = gathered[:, :].rearrange("p (u d) -> p u d", u=U)
        weights = sb("weights", [P, 3 * KD * D])
        c.W = weights[:, :].rearrange("p (s d) -> p s d", s=3)
        work = sb("work", [P, 6 * TW])
        c.recs = arena[:, 0:EC * RW]
        at = EC * RW
        c.recs3 = c.recs.rearrange("p (j w) -> p j w", w=RW)
        c.recs3_i = c.recs.bitcast(I32).rearrange("p (j w) -> p j w", w=RW)
        c.member, c.running = gathered[:, 0:T * EC], weights[:, 0:T * EC]
        c.recs0 = arena[:, at:at + EC * SW]
        c.recs0_3 = c.recs0.rearrange("p (j w) -> p j w", w=SW)
        c.recs0_3i = c.recs0.bitcast(I32).rearrange("p (j w) -> p j w", w=SW)
        at += EC * SW
        c.PADS = 16
        c.pads = arena[:, at:at + c.PADS * RW]
        at += c.PADS * RW
        c.pads0 = arena[:, at:at + NCH * SW]
        at += NCH * SW
        taken = [at]

        def take(n, whole=False):
            taken[0] += n
            v = arena[:, taken[0] - n:taken[0]]
            return v.bitcast(I32) if whole else v
        c.bin_f, c.bin_g, c.edge_ones, c.weight, c.attr2 = take(EC), take(EC), take(EC), take(EC), take(2 * EC)
        c.key_src, c.key_dst, c.tmp_i = take(EC, True), take(EC, True), take(3 * EC, True)
        c.rows_dst, c.rows_src = take(EC, True), take(EC, True)
        assert taken[0] <= 3 * T * D
        late = T * EC
        c.upper, c.iota_i = weights[:, late:late + P], weights[:, late + P:late + 2 * P].bitcast(I32)
        late += 2 * P
        c.chunk_f, c.tile_f = weights[:, late:late + NCH], weights[:, late + NCH:late + 2 * NCH]
        c.chunk_i = weights[:, late + 2 * NCH:late + 3 * NCH].bitcast(I32)
        c.wide = arena[:, 0:NCH * RW]

        c.rec = sb("rec", [P, C1 * HW])
        c.rec = c.rec[:, :]
        c.rec_i = c.rec.bitcast(I32)
        c.rec3, c.rec3_i = (r.rearrange("p (c w) -> p c w", w=HW) for r in (c.rec, c.rec_i))
        c.rec0 = sb("rec0", [P, NCH * SW])[:, :]
        c.tiles_dst, c.tiles_src = sb("tiles_dst", [1, C1], I32), sb("tiles_src", [1, NCH], I32)
        c.iota = sb("iota", [P, P])
        c.node_i, c.tile_i, c.lane_i = sb("node_i", [P, T], I32), sb("tile_i", [P, T], I32), sb("lane_i", [P, 1], I32)
        c.lane_f = sb("lane_f", [P, 1])
        c.ones, c.ident, c.eps = sb("ones", [P, P]), sb("ident", [P, P]), sb("eps", [P, 1])
        c.counts, c.small, c.small_i = sb("counts", [P, T]), sb("small", [P, 4 * T]), sb("small_i", [P, 2 * T], I32)
        c.idx, c.idx0 = sb("idx", [P, U], I32), sb("idx0", [P, U], I32)
        c.stage, c.stage0 = work[:, 0:U * RW], work[:, U * RW:U * (RW + SW)]
        c.deg, c.deg1, c.dis, c.root = sb("deg", [P, 3 * T]), sb("deg1", [P, T]), sb("dis", [P, T]), sb("root", [P, T])
        c.mv, c.st, c.rstd = sb("mv", [P, 2 * T]), sb("st", [P, 6 * T]), sb("rstd", [P, T])
        c.hot = sb("hot", [P, 2, P])
        c.row0, c.row1, c.row2, c.row3 = (sb(f"row{n}", [P, D]) for n in range(4))
        c.S, c.H, c.Q, c.Q2 = (sb(n, [P, 2, D]) for n in ("S", "H", "Q", "Q2"))
        c.attB, c.WeB, c.We = c.row3, c.Q[:, :, :].rearrange("p s d -> p (s d)"), sb("We", [2, D])
        c.xs = work[:, 0:2 * D].rearrange("p (s d) -> p s d", s=2)
        c.xT = work[:, 2 * D:4 * D].rearrange("p (s d) -> p s d", s=2)
        c.out = work[:, 4 * D:4 * D + 2 * TW].rearrange("p (s d) -> p s d", s=2)
        c.hT = work[:, 0:2 * D].rearrange("p (s d) -> p s d", s=2)
        c.M = work[:, 2 * D:4 * D].rearrange("p (s d) -> p s d", s=2)
        c.Y, c.Y2 = work[:, 4 * D:5 * D], work[:, 5 * D:6 * D]
        c.Eb = c.W[:, 0, 0:2 * D].rearrange("p (s d) -> p s d", s=2)
        c.R = c.Y
        c.oT, c.eT = sb("oT", [P, 2, P]), sb("eT", [EA, 2, P])
        c.eat, c.far, c.masked = sb("eat", [P, 2, 2]), sb("far", [P, 4, P]), sb("masked", [P, 2, P])
        c.PT, c.Wt = sb("PT", [P, 2, P]), sb("Wt", [P, 2, P])
        c.hot4, c.hotm = c.far, c.masked
        c.scale, c.rowsum, c.dot, c.lg, c.cmax, c.mnew = (sb(n, [P, 2]) for n in (
            "scale", "rowsum", "dot", "lg", "cmax", "mnew"))
        c.diff, c.cvec, c.lin, c.den, c.MA = (sb("diff", [P, 4]), sb("cvec", [P, 2]), sb("lin", [P, C1]),
                                              sb("den", [P, T]), sb("MA", [P, 2 * T]))
        c.ea, c.W1c, c.b2r = sb("ea", [P, U, EA]), c.row2[0:EA, :], c.row3[0:1, :]
        c.ps = ctx.enter_context(nc.psum_tensor("ps", [P, 8, 512], F32))

        def dram(name, shape):
            return nc.dram_tensor(name, shape, F32, kind="Internal").ap()

        c.by_dst, c.by_src = dram("by_dst", [P * NCH, RW]), dram("by_src", [P * NCH, SW])
        table, table_att, table_res = dram("table", [N, D]), dram("table_att", [N, TW]), dram("table_res", [N, D])

        stage_constants(nc, c)
        stage_bin(nc, c, a["src"], a["dst"], a["edge_attr_2"], a["edge_attr_64"], a["edge_weight"])
        stage_scatter(nc, c)
        stage_heads(nc, c, a["x"])
        stage_degrees(nc, c)

        stage_aggregate(nc, c, "L0", NCH, a["x"], c.rec0, SW, c.tiles_src, 0, weighted=True)
        stage_transpose_weight(nc, c, a["L0_gnn_weight"])
        stage_linear(nc, c, "L0lin", [c.ACC], [(
            [1], lambda link, t, ps, o: nc.vector.tensor_tensor(tile_of(c.XR, t), ps, tile_of(c.X, t), ALU.add), 0)])
        stage_norm(nc, c, "L0norm", c.XR, c.X, store=table_res)

        def attention(k, cur):
            n = f"L1_{k}"
            wl, wr, we = a["L1_gnn_Wl"][k], a["L1_gnn_Wr"][k], a["L1_gnn_We"][k]

            def left(link, t, ps, o):
                link(nc.vector.tensor_tensor(o[:, 0:D], ps, c.row0[:, :], ALU.add))
                return nc.vector.tensor_tensor_reduce(out=c.S[:, 0, :], in0=o[:, 0:D], in1=c.attB[:, :], scale=SLOPE,
                                                      scalar=0.0, op0=ALU.mult, op1=ALU.add, accum_out=o[:, D:D + 1])

            def right(link, t, ps, o):
                link(nc.vector.tensor_tensor(tile_of(c.XR, t), ps, c.row1[:, :], ALU.add))
                ar = c.MA[:, 2 * t + 1:2 * t + 2] if isinstance(t, int) else c.MA[:, bass.ds(2 * t + 1, 1)]
                link(nc.vector.scalar_tensor_tensor(c.S[:, 1, :], tile_of(c.XR, t), SLOPE, c.attB[:, :], ALU.mult, ALU.mult,
                                                    accum_out=c.cvec[:, 0:1]))
                return nc.vector.tensor_scalar(ar, c.cvec[:, 0:1], 0.0, None, ALU.add)
            s_pad, s_we = c.sem(f"{n}_pad"), c.sem(f"{n}_We_in")
            with nc.Block() as block:
                @block.gpsimd
                def _(pool):
                    pool.memset(c.out[:, :, D:TW], 0.0).then_inc(s_pad, 1)

                @block.sync
                def _(sp):
                    sp.dma_start(c.We[:, :], we).then_inc(s_we, 16)
                    sp.wait_ge(s_we, 16)
            stage_linear(nc, c, n + "lin", [cur], [([0], left, 1), ([1], right, 2)], weights=[(wl, 0), (wr, 1)],
                         rows=[(c.row0[:, :], a["L1_gnn_bl"][k]), (c.row1[:, :], a["L1_gnn_br"][k]),
                               (c.attB[:, :], a["L1_gnn_att"][k]),
                               (c.WeB[:, :], we.rearrange("a d -> (a d)"))], table=table_att)
            stage_attention_edges(nc, c, n, table_att)
            stage_rows(nc, c, n, [(c.row2[:, :], a["L1_gnn_b_out"][k]), (c.row0[:, :], a["L1_gnn_gamma"][k]),
                                  (c.row1[:, :], a["L1_gnn_beta"][k])])
            stage_attention_close(nc, c, n + "close", cur)
            stage_norm(nc, c, n + "norm", c.XR, c.X, gamma=c.row0[:, :], beta=c.row1[:, :], relu=True)
        for k in range(3):
            attention(k, c.X)
        s_res, s_sum = c.sem("L1_residual_in"), c.sem("L1_residual_added")
        with nc.Block() as block:
            @block.sync
            def _(sp):
                sp.dma_start(c.ACC.rearrange("p (t d) -> p t d", t=T), table_res.rearrange("(t p) d -> p t d", p=P))\
                  .then_inc(s_res, 16)

            @block.vector
            def _(dve):
                dve.wait_ge(s_res, 16)
                nc.vector.tensor_tensor(c.X[:, :], c.X[:, :], c.ACC[:, :], ALU.add)
        stage_norm(nc, c, "L1norm", c.X, c.X)

        def conv1(link, t, ps, o):
            dis = col(c.dis, t)
            link(nc.vector.scalar_tensor_tensor(c.S[:, 0, :], ps, dis, c.row0[:, :], ALU.mult, ALU.add))
            return nc.vector.tensor_scalar(o[:, 0:D], c.S[:, 0, :], 0.0, dis, ALU.max, ALU.mult)

        def conv2(link, t, ps, o):
            link(nc.vector.scalar_tensor_tensor(c.S[:, 0, :], ps, col(c.dis, t), c.row0[:, :], ALU.mult, ALU.add))
            return nc.vector.tensor_tensor(tile_of(c.XR, t), c.S[:, 0, :], tile_of(c.X, t), ALU.add)
        stage_scaled_table(nc, c, table)
        stage_aggregate(nc, c, "L2a", C1, table, c.rec, HW, c.tiles_dst, 0, weighted=False)
        stage_linear(nc, c, "L2alin", [c.ACC], [([0], conv1, 1)], weights=[(a["L2_gnn_W1"], 0)],
                     rows=[(c.row0[:, :], a["L2_gnn_b1"])], table=table)
        stage_aggregate(nc, c, "L2b", C1, table, c.rec, HW, c.tiles_dst, 0, weighted=False)
        stage_linear(nc, c, "L2blin", [c.ACC], [([0], conv2, 1)], weights=[(a["L2_gnn_W2"], 0)],
                     rows=[(c.row0[:, :], a["L2_gnn_b2"])])
        stage_norm(nc, c, "L2norm", c.XR, c.X)

        s_w = c.sem("L3_weights_in")
        with nc.Block() as block:
            @block.sync
            def _(sp):
                sp.dma_start(c.W1c[:, :], a["L3_gnn_W1"][2 * D:2 * D + EA, :]).then_inc(s_w, 16)
                sp.dma_start(c.b2r[:, :], a["L3_gnn_b2"].rearrange("(o d) -> o d", o=1)).then_inc(s_w, 16)
                load_weights(sp, c, s_w, a["L3_gnn_W2"], 2)
                sp.wait_ge(s_w, 48)

            @block.vector
            def _(dve):
                dve.wait_ge(s_w, 48)
                nc.vector.tensor_scalar(c.W[:, 2, :], c.W[:, 2, :], 2.0, None, ALU.mult)
        stage_linear(nc, c, "L3lin", [c.X], [
            ([0], lambda link, t, ps, o: nc.vector.tensor_tensor(o[:, 0:D], ps, c.row0[:, :], ALU.add), 0),
            ([1], lambda link, t, ps, o: nc.vector.tensor_scalar(tile_of(c.XR, t), ps, 0.0, None, ALU.add), 0)],
            weights=[(a["L3_gnn_W1"][0:D, :], 0), (a["L3_gnn_W1"][D:2 * D, :], 1)], rows=[(c.row0[:, :], a["L3_gnn_b1"])],
            table=table)
        stage_messages(nc, c, table)
        stage_linear(nc, c, "L3u", [c.X, c.ACC], [
            ([0, 1], lambda link, t, ps, o: nc.vector.tensor_tensor(tile_of(c.XR, t), ps, c.row0[:, :], ALU.add), 0)],
            weights=[(a["L3_gnn_W3"][0:D, :], 0), (a["L3_gnn_W3"][D:2 * D, :], 1)], rows=[(c.row0[:, :], a["L3_gnn_b3"])])
        stage_mish(nc, c, c.XR)

        def close(link, t, ps, o):
            link(nc.vector.tensor_tensor(c.S[:, 0, :], ps, c.row0[:, :], ALU.add))
            return nc.vector.tensor_tensor(tile_of(c.ACC, t), c.S[:, 0, :], tile_of(c.X, t), ALU.add)
        stage_linear(nc, c, "L3out", [c.XR], [([0], close, 1)], weights=[(a["L3_gnn_W4"], 0)],
                     rows=[(c.row0[:, :], a["L3_gnn_b4"]), (c.row1[:, :], a["L3_gnn_gamma"]), (c.row2[:, :], a["L3_gnn_beta"])])
        stage_norm(nc, c, "L3norm", c.ACC, c.XR, gamma=c.row1[:, :], beta=c.row2[:, :], residual=c.X)
        stage_norm(nc, c, "outnorm", c.XR, c.ACC, store=out)


_INS = ['x', 'src', 'dst', 'edge_attr_2', 'edge_attr_64', 'edge_weight', 'L0_gnn_weight', 'L1_gnn_Wl', 'L1_gnn_bl',
        'L1_gnn_Wr', 'L1_gnn_br', 'L1_gnn_We', 'L1_gnn_att', 'L1_gnn_b_out', 'L1_gnn_gamma', 'L1_gnn_beta',
        'L2_gnn_W1', 'L2_gnn_b1', 'L2_gnn_W2', 'L2_gnn_b2', 'L3_gnn_W1', 'L3_gnn_b1', 'L3_gnn_W2', 'L3_gnn_b2',
        'L3_gnn_W3', 'L3_gnn_b3', 'L3_gnn_W4', 'L3_gnn_b4', 'L3_gnn_gamma', 'L3_gnn_beta']


def kernel(**inputs):
    import numpy as _np
    import concourse.bacc as _bacc
    from concourse import mybir as _mybir
    from concourse.bass_utils import run_bass_kernel_spmd as _run

    nc = _bacc.Bacc("TRN2", target_bir_lowering=False, num_devices=1)
    arrays, args = {}, {}
    for name in _INS:
        v = _np.ascontiguousarray(inputs[name])
        arrays[f"in_{name}_dram"] = v
        args[name] = nc.dram_tensor(f"in_{name}_dram", v.shape, _mybir.dt.from_np(v.dtype), kind="ExternalInput").ap()
    out = nc.dram_tensor("out_0_dram", (N, D), F32, kind="ExternalOutput").ap()
    gnn_stack(nc, args, out)
    r = _run(nc, [arrays], core_ids=[0])
    return r.results[0]["out_0_dram"]
```

```python
from contextlib import ExitStack

import concourse.bass as bass
from concourse import mybir

F32 = mybir.dt.float32
I32 = mybir.dt.int32
F32R = mybir.dt.float32r
ALU = mybir.AluOpType
ACT = mybir.ActivationFunctionType
AX = mybir.AxisListType

P = 128
N, D, E = 2048, 512, 32768
T = N // P
KD = D // P
EC = E // P
EA = 64
NCH = 272
C1 = T + NCH
HW = 5
RW = HW + EA
SW = 4
TW = 520
AW = 7
SLOPE = 0.2
EPS = 1e-5
CLAMP = 20.0
FAR = 1e30
U = 8
assert NCH * P >= E + T * (P - 1) and NCH % U == 0 and C1 % U == 0


class Chip:
    pass



def wait(eng, sem, value):
    if isinstance(value, int) and value <= 0:
        return
    eng.wait_ge(sem, value)


def wait_apart(eng, sem, value, passed):
    if isinstance(value, int) and value <= 0:
        return
    eng.wait_ge(sem, value)
    eng.sem_inc(passed, 1)


def back(k, u, lag):
    return k * U + (u - lag), (u - lag) % U, (k if u >= lag else k - 1)


def live(i, count):
    return not isinstance(i, int) or 0 <= i < count


def run_steps(eng, count, step, lag=0):
    for u in range(U):
        step(0, u)
    with eng.Fori(1, count // U) as k:
        for u in range(U):
            step(k, u)
    for u in range(lag):
        step(count // U, u)


def tile_of(buf, t):
    return buf[:, t * D:(t + 1) * D] if isinstance(t, int) else buf[:, bass.ds(t * D, D)]


def col(buf, i, n=1):
    return buf[:, i * n:(i + 1) * n] if isinstance(i, int) else buf[:, bass.ds(i * n, n)]


def end_stage(nc, c):
    nc.clear_and_free_semaphores(c.sems)
    nc.all_engine_barrier()
    c.sems.clear()


def stage(build):
    def built(nc, c, *args, **named):
        build(nc, c, *args, **named)
        end_stage(nc, c)
    return built



@stage
def stage_constants(nc, c):
    s_low = c.sem("const_low")
    s_fill, s_shape = c.sem("const_filled"), c.sem("const_shaped")
    with nc.Block() as block:
        @block.gpsimd
        def _(pool):
            pool.iota(c.iota_i[:, :], pattern=[[1, P]], base=0, channel_multiplier=0).then_inc(s_fill, 1)
            pool.iota(c.node_i[:, :], pattern=[[P, T]], base=0, channel_multiplier=1).then_inc(s_fill, 1)
            pool.iota(c.chunk_i[:, :], pattern=[[1, NCH]], base=0, channel_multiplier=0).then_inc(s_fill, 1)
            pool.iota(c.tile_i[:, :], pattern=[[1, T]], base=0, channel_multiplier=0).then_inc(s_fill, 1)
            pool.iota(c.lane_i[:, :], pattern=[[0, 1]], base=0, channel_multiplier=1).then_inc(s_fill, 1)
            pool.memset(c.ones[:, :], 1.0).then_inc(s_fill, 1)
            pool.memset(c.ident[:, :], 0.0).then_inc(s_fill, 1)
            pool.wait_ge(s_fill, 7)
            pool.affine_select(out=c.ident[:, :], in_=c.ident[:, :], compare_op=ALU.not_equal, fill=1.0, base=0,
                               pattern=[[-1, P]], channel_multiplier=1).then_inc(s_shape, 1)
            pool.affine_select(out=c.upper[:, :], in_=c.ones[:, :], compare_op=ALU.is_gt, fill=0.0, base=0,
                               pattern=[[1, P]], channel_multiplier=-1).then_inc(s_shape, 1)

        @block.vector
        def _(dve):
            dve.wait_ge(s_fill, 7)
            nc.vector.tensor_copy(c.iota[:, :], c.iota_i[:, :])
            nc.vector.tensor_copy(c.chunk_f[:, :], c.chunk_i[:, :])
            nc.vector.tensor_copy(c.lane_f[:, :], c.lane_i[:, :]).then_inc(s_low, 1)
            dve.wait_ge(s_low, 1)
            nc.vector.memset(c.eps[:, :], EPS)
            nc.vector.tensor_scalar(c.low2[:, :], c.lane_f[:, :], 4.0, None, ALU.is_lt).then_inc(s_low, 1)
            dve.wait_ge(s_low, 2)
            nc.vector.scalar_tensor_tensor(c.low[:, :], c.lane_f[:, :], 2.0, c.low2[:, :], ALU.is_ge, ALU.mult).then_inc(s_low, 1)
            dve.wait_ge(s_low, 3)
            nc.vector.tensor_scalar(c.sign[:, :], c.low[:, :], -2.0, 1.0, ALU.mult, ALU.add)
            nc.vector.tensor_copy(c.tiles_dst[0:1, 0:T], c.tile_i[0:1, :])


def bin_edges(nc, c, dve, chain, key, rec_local, rows, ends_sem, totals_sem, tiles_out, uses):
    def link(ins):
        chain[0] += 1
        ins.then_inc(c.s_chain, 1)
        dve.wait_ge(c.s_chain, chain[0])

    link(nc.vector.tensor_scalar(c.tmp_i[:, 0:EC], key, 7, None, ALU.logical_shift_right))
    link(nc.vector.tensor_copy(c.bin_f[:, :], c.tmp_i[:, 0:EC]))
    link(nc.vector.tensor_scalar(c.tmp_i[:, 0:EC], key, P - 1, None, ALU.bitwise_and))
    nc.vector.tensor_copy(rec_local, c.tmp_i[:, 0:EC])
    for b in range(T):
        last = nc.vector.tensor_scalar(c.member[:, b * EC:(b + 1) * EC], c.bin_f[:, :], float(b), None, ALU.is_equal)
    link(last)
    for b in range(T):
        last = nc.vector.tensor_tensor_scan(c.running[:, b * EC:(b + 1) * EC], c.edge_ones[:, :],
                                            c.member[:, b * EC:(b + 1) * EC], 0.0, ALU.mult, ALU.add)
    link(last)
    counts = c.running[:, :].rearrange("p (b j) -> p b j", b=T)[:, :, EC - 1]
    nc.vector.tensor_copy(c.counts[:, :], counts).then_inc(ends_sem, 1)
    dve.wait_ge(totals_sem, uses)
    before, total = c.ps[:, 0, 0:T], c.ps[:, 1, 0:T]
    link(nc.vector.tensor_scalar(c.small[:, 0:T], total, float(P - 1), None, ALU.add))
    link(nc.vector.tensor_copy(c.small_i[:, 0:T], c.small[:, 0:T]))
    link(nc.vector.tensor_scalar(c.small_i[:, T:2 * T], c.small_i[:, 0:T], 7, None, ALU.logical_shift_right))
    link(nc.vector.tensor_copy(c.small[:, T:2 * T], c.small_i[:, T:2 * T]))
    link(nc.vector.tensor_tensor_scan(c.small[:, 2 * T:3 * T], c.ones[:, 0:T], c.small[:, T:2 * T], 0.0,
                                      ALU.mult, ALU.add))
    link(nc.vector.tensor_tensor(c.small[:, 3 * T:4 * T], c.small[:, 2 * T:3 * T], c.small[:, T:2 * T], ALU.subtract))
    link(nc.vector.tensor_scalar(c.small[:, 3 * T:4 * T], c.small[:, 3 * T:4 * T], float(P), -1.0, ALU.mult, ALU.add))
    link(nc.vector.tensor_tensor(c.small[:, 3 * T:4 * T], c.small[:, 3 * T:4 * T], before, ALU.add))
    for b in range(T):
        run = c.running[:, b * EC:(b + 1) * EC]
        last = nc.vector.scalar_tensor_tensor(run, run, c.small[:, 3 * T + b:3 * T + b + 1],
                                              c.member[:, b * EC:(b + 1) * EC], ALU.add, ALU.mult)
    link(last)
    link(nc.vector.tensor_reduce(c.bin_f[:, :], c.running[:, :].rearrange("p (b j) -> p j b", b=T), AX.X, ALU.add))
    link(nc.vector.tensor_copy(c.tmp_i[:, 0:EC], c.bin_f[:, :]))
    nc.vector.tensor_scalar(c.tmp_i[:, EC:2 * EC], c.tmp_i[:, 0:EC], 7, None, ALU.logical_shift_right)
    link(nc.vector.tensor_scalar(c.tmp_i[:, 2 * EC:3 * EC], c.tmp_i[:, 0:EC], P - 1, None, ALU.bitwise_and))
    nc.vector.tensor_copy(c.bin_f[:, :], c.tmp_i[:, EC:2 * EC])
    link(nc.vector.tensor_copy(c.bin_g[:, :], c.tmp_i[:, 2 * EC:3 * EC]))
    link(nc.vector.scalar_tensor_tensor(c.bin_g[:, :], c.bin_g[:, :], float(NCH), c.bin_f[:, :], ALU.mult, ALU.add))
    link(nc.vector.tensor_copy(rows, c.bin_g[:, :]))
    link(nc.vector.memset(c.tile_f[0:1, :], 0.0))
    for b in range(T - 1):
        link(nc.vector.scalar_tensor_tensor(c.tile_f[0:1, :], c.chunk_f[0:1, :], c.small[0:1, 2 * T + b:2 * T + b + 1],
                                            c.tile_f[0:1, :], ALU.is_ge, ALU.add))
    link(nc.vector.tensor_copy(tiles_out, c.tile_f[0:1, :]))


@stage
def stage_bin(nc, c, src, dst, edge_attr_2, edge_attr_64, edge_weight):
    s_key, s_attr, s_wide, s_pads = (c.sem(f"bin_{n}") for n in ("keys_in", "attrs_in", "wide_in", "pads_out"))
    s_cnt, s_tot, s_pad = (c.sem(f"bin_{n}") for n in ("counts", "totals", "pad_rows"))
    c.chain, c.s_chain = [0], c.sem("bin_chain")
    by_p = lambda a: a.rearrange("(p j) -> p j", p=P)
    with nc.Block() as block:
        @block.sync
        def _(sp):
            sp.dma_start(c.key_src[:, :], by_p(src)).then_inc(s_key, 16)
            sp.dma_start(c.key_dst[:, :], by_p(dst)).then_inc(s_key, 16)
            sp.dma_start(c.attr2[:, :], edge_attr_2.rearrange("(p j) a -> p (j a)", p=P)).then_inc(s_attr, 16)
            sp.dma_start(c.weight[:, :], by_p(edge_weight)).then_inc(s_attr, 16)
            sp.dma_start(c.recs3[:, :, HW:RW], edge_attr_64.rearrange("(p j) a -> p j a", p=P)).then_inc(s_wide, 16)
            sp.wait_ge(s_pad, 2)
            for n in range(NCH // c.PADS):
                sp.dma_start(c.by_dst.rearrange("(p c) w -> p (c w)", p=P)[:, n * c.PADS * RW:(n + 1) * c.PADS * RW],
                             c.pads[:, :]).then_inc(s_pads, 16)
            sp.dma_start(c.by_src.rearrange("(p c) w -> p (c w)", p=P), c.pads0[:, :]).then_inc(s_pads, 16)
            sp.wait_ge(s_pads, 16 * (NCH // c.PADS + 1))
            sp.wait_ge(s_wide, 16)

        @block.gpsimd
        def _(pool):
            s_zero = c.sem("bin_zeroed")
            pool.memset(c.pads[:, :], 0.0).then_inc(s_zero, 1)
            pool.memset(c.pads0[:, :], 0.0).then_inc(s_zero, 1)
            pool.wait_ge(s_zero, 2)
            pool.memset(c.pads[:, :].rearrange("p (c w) -> p c w", w=RW)[:, :, 1], -1.0).then_inc(s_pad, 1)
            pool.memset(c.pads0[:, :].rearrange("p (c w) -> p c w", w=SW)[:, :, 1], -1.0).then_inc(s_pad, 1)

        @block.tensor
        def _(pe):
            for n in range(2):
                pe.wait_ge(s_cnt, n + 1)
                nc.tensor.matmul(c.ps[:, 0, 0:T], c.upper[:, :], c.counts[:, :], start=True, stop=True)
                nc.tensor.matmul(c.ps[:, 1, 0:T], c.ones[:, :], c.counts[:, :], start=True, stop=True).then_inc(s_tot, 1)

        @block.vector
        def _(dve):
            chain = c.chain
            nc.vector.memset(c.edge_ones[:, :], 1.0)
            nc.vector.memset(c.recs3[:, :, 4], 1.0)
            nc.vector.memset(c.recs0_3[:, :, 3], 0.0)
            dve.wait_ge(s_key, 32)
            nc.vector.tensor_copy(c.recs3_i[:, :, 0], c.key_src[:, :])
            nc.vector.tensor_copy(c.recs0_3i[:, :, 0], c.key_dst[:, :])
            bin_edges(nc, c, dve, chain, c.key_dst[:, :], c.recs3[:, :, 1], c.rows_dst[:, :], s_cnt, s_tot,
                      c.tiles_dst[0:1, T:C1], 1)
            bin_edges(nc, c, dve, chain, c.key_src[:, :], c.recs0_3[:, :, 1], c.rows_src[:, :], s_cnt, s_tot,
                      c.tiles_src[0:1, :], 2)
            dve.wait_ge(s_attr, 32)
            nc.vector.tensor_copy(c.recs3[:, :, 2:4], c.attr2[:, :].rearrange("p (j a) -> p j a", a=2))
            nc.vector.tensor_copy(c.recs0_3[:, :, 2], c.weight[:, :])


@stage
def stage_scatter(nc, c):
    s_rec, s_rec0 = c.sem("scatter_staged_dst"), c.sem("scatter_staged_src")
    s_passed, s_idx = c.sem("scatter_wait_passed"), c.sem("scatter_rows_copied")
    s_out = [c.sem(f"scatter_dst_out{u}") for u in range(U)]
    s_out0 = [c.sem(f"scatter_src_out{u}") for u in range(U)]
    with nc.Block() as block:
        @block.scalar
        def _(act):
            def step(k, u):
                i = k * U + u
                wait_apart(act, s_out[u], 16 * k, s_passed)
                nc.scalar.activation(c.stage[:, u * RW:(u + 1) * RW], col(c.recs, i, RW), ACT.Copy).then_inc(s_rec, 1)
                wait_apart(act, s_out0[u], 16 * k, s_passed)
                nc.scalar.activation(c.stage0[:, u * SW:(u + 1) * SW], col(c.recs0, i, SW), ACT.Copy).then_inc(s_rec0, 1)
            run_steps(act, EC, step)

        @block.gpsimd
        def _(pool):
            half = U // 2

            def step(k, u):
                i = k * U + u
                if u % half == 0:
                    h = u // half
                    for v in range(u, u + half):
                        wait_apart(pool, s_out[v], 16 * k, s_passed)
                        wait_apart(pool, s_out0[v], 16 * k, s_passed)
                    n = k * 2 + h
                    nc.gpsimd.tensor_copy(c.idx[:, h * half:(h + 1) * half], col(c.rows_dst, n, half)).then_inc(s_idx, 1)
                    nc.gpsimd.tensor_copy(c.idx0[:, h * half:(h + 1) * half], col(c.rows_src, n, half)).then_inc(s_idx, 1)
                    wait_apart(pool, s_idx, 2 * n + 2, s_passed)
                wait_apart(pool, s_rec, i + 1, s_passed)
                pool.indirect_dma_start(out=c.by_dst, out_offset=bass.IndirectOffsetOnAxis(ap=c.idx[:, u:u + 1], axis=0),
                                        in_=c.stage[:, u * RW:(u + 1) * RW], in_offset=None).then_inc(s_out[u], 16)
                wait_apart(pool, s_rec0, i + 1, s_passed)
                pool.indirect_dma_start(out=c.by_src, out_offset=bass.IndirectOffsetOnAxis(ap=c.idx0[:, u:u + 1], axis=0),
                                        in_=c.stage0[:, u * SW:(u + 1) * SW], in_offset=None).then_inc(s_out0[u], 16)
            run_steps(pool, EC, step)
            for u in range(U):
                pool.wait_ge(s_out[u], 16 * (EC // U))
                pool.wait_ge(s_out0[u], 16 * (EC // U))


@stage
def stage_heads(nc, c, x):
    s_all, s_head0, s_x = c.sem("heads_rows_in"), c.sem("heads_src_in"), c.sem("nodes_in")
    with nc.Block() as block:
        @block.sync
        def _(sp):
            sp.dma_start(c.wide[:, :], c.by_dst.rearrange("(p c) w -> p (c w)", p=P)).then_inc(s_all, 16)
            sp.dma_start(c.rec0[:, :], c.by_src.rearrange("(p c) w -> p (c w)", p=P)).then_inc(s_head0, 16)
            sp.wait_ge(s_head0, 16)

        @block.vector
        def _(dve):
            dve.wait_ge(s_all, 16)
            wide = c.wide[:, :].rearrange("p (c w) -> p c w", w=RW)
            nc.vector.tensor_copy(c.rec3[:, T:C1, 1:HW], wide[:, :, 1:HW])
            nc.vector.tensor_copy(c.rec3_i[:, T:C1, 0], wide.bitcast(I32)[:, :, 0])
    with nc.Block() as block:
        @block.sync
        def _(sp):
            sp.dma_start(c.X[:, :].rearrange("p (t d) -> p t d", t=T), x.rearrange("(t p) d -> p t d", p=P)).then_inc(s_x, 16)
            sp.wait_ge(s_x, 16)


@stage
def stage_degrees(nc, c):
    s_hot, s_sum, s_add, s_last = (c.sem(f"degree_{n}") for n in ("onehot", "summed", "added", "zeroed"))
    with nc.Block() as block:
        @block.vector
        def _(dve):
            nc.vector.memset(c.deg[:, :], 0.0).then_inc(s_last, 1)
            dve.wait_ge(s_last, 1)

            def step(k, u):
                i, s, _ = back(k, u, 0)
                if live(i, NCH):
                    wait(dve, s_sum, i - 3)
                    nc.vector.tensor_scalar(c.hot4[:, u % 4, :], c.iota[:, :], col(c.rec, T + i, HW)[:, 1:2], None,
                                            ALU.is_equal).then_inc(s_hot, 1)
                j, s, _ = back(k, u, 3)
                if live(j, NCH):
                    t = dve.value_load(c.tiles_dst[0:1, T + j:T + j + 1] if isinstance(j, int)
                                       else c.tiles_dst[0:1, bass.ds(T + j, 1)], min_val=0, max_val=T - 1)
                    wait(dve, s_sum, j + 1)
                    wait(dve, s_add, j)
                    acc = c.deg[:, bass.ds(t * 3, 3)]
                    nc.vector.tensor_tensor(acc, acc, c.ps[:, s % 4, 0:3], ALU.add).then_inc(s_add, 1)
            run_steps(dve, NCH, step, lag=3)

        @block.tensor
        def _(pe):
            def step(k, u):
                i = k * U + u
                wait(pe, s_hot, i + 1)
                wait(pe, s_add, i - 3)
                nc.tensor.matmul(c.ps[:, u % 4, 0:3], c.hot4[:, u % 4, :], col(c.rec, T + i, HW)[:, 2:5],
                                 start=True, stop=True).then_inc(s_sum, 1)
            run_steps(pe, NCH, step)
    c.chain, c.s_chain = [0], c.sem("degree_chain")
    s_sq, s_rt = c.sem("degree_plus_one"), c.sem("degree_root")
    with nc.Block() as block:
        @block.vector
        def _(dve):
            def link(ins):
                c.chain[0] += 1
                ins.then_inc(c.s_chain, 1)
                dve.wait_ge(c.s_chain, c.chain[0])
            deg = c.deg[:, :].rearrange("p (t w) -> p t w", w=3)
            nc.vector.tensor_scalar(c.deg1[:, :], deg[:, :, 2], 1.0, None, ALU.add).then_inc(s_sq, 1)
            link(nc.vector.tensor_scalar(c.dis[:, :], deg[:, :, 2], 1.0, None, ALU.max))
            link(nc.vector.reciprocal(c.small[:, 0:T], c.dis[:, :]))
            for a in range(2):
                nc.vector.tensor_tensor(c.rec3[:, 0:T, 2 + a], deg[:, :, a], c.small[:, 0:T], ALU.mult)
            nc.vector.tensor_copy(c.rec3_i[:, 0:T, 0], c.node_i[:, :])
            nc.vector.tensor_scalar(c.rec3[:, 0:T, 1], c.ones[:, 0:T], c.lane_f[:, :], None, ALU.mult)
            nc.vector.tensor_copy(c.rec3[:, 0:T, 4], c.ones[:, 0:T])
            dve.wait_ge(s_rt, 1)
            nc.vector.reciprocal(c.dis[:, :], c.root[:, 0:T])

        @block.scalar
        def _(act):
            act.wait_ge(s_sq, 1)
            nc.scalar.activation(c.root[:, 0:T], c.deg1[:, :], ACT.Sqrt).then_inc(s_rt, 1)



def load_weights(sp, c, sem, w, slot):
    sp.dma_start(c.W[:, slot, :].rearrange("p (k o) -> p k o", k=KD), w.rearrange("(k p) o -> p k o", p=P)).then_inc(sem, 16)


@stage
def stage_transpose_weight(nc, c, w):
    s_in, s_t, s_c = c.sem("wt_in"), c.sem("wt_turned"), c.sem("wt_copied")
    with nc.Block() as block:
        @block.sync
        def _(sp):
            load_weights(sp, c, s_in, w, 0)

        @block.tensor
        def _(pe):
            pe.wait_ge(s_in, 16)
            for k in range(KD):
                for o in range(KD):
                    last = nc.tensor.transpose(c.ps[:, k, o * P:(o + 1) * P], c.W[:, 0, o * D + k * P:o * D + (k + 1) * P],
                                               c.ident[:, :])
                last.then_inc(s_t, 1)

        @block.vector
        def _(dve):
            for k in range(KD):
                dve.wait_ge(s_t, k + 1)
                nc.vector.tensor_copy(c.W[:, 1, k * D:(k + 1) * D], c.ps[:, k, :])


@stage
def stage_linear(nc, c, name, sources, outputs, weights=(), rows=(), table=None):
    S, O = len(sources), len(outputs)
    s_w, s_in, s_turn, s_even, s_prod, s_fin, s_store = (
        c.sem(f"{name}_{n}") for n in ("weights_in", "staged", "turned", "turned_copied", "product", "finished", "stored0"))
    s_store = [s_store, c.sem(f"{name}_stored1")]
    with nc.Block() as block:
        @block.sync
        def _(sp):
            for w, slot in weights:
                load_weights(sp, c, s_w, w, slot)
            for buf, a in rows:
                sp.dma_start(buf, a.partition_broadcast(P)).then_inc(s_w, 16)
            if table is not None:
                width = table.shape[1]

                def store(k, u):
                    t = k * 2 + u
                    wait(sp, s_fin, O * t + 1)
                    row = table[t * P:(t + 1) * P, :] if isinstance(t, int) else table[bass.ds(t * P, P), :]
                    sp.dma_start(row, c.out[:, u, 0:width]).then_inc(s_store[u], 16)
                with sp.Fori(0, T // 2) as k:
                    for u in range(2):
                        store(k, u)
                for u in range(2):
                    sp.wait_ge(s_store[u], 16 * (T // 2))

        @block.scalar
        def _(act):
            def stage(t, s, slot):
                nc.scalar.activation(c.xs[:, slot, :], tile_of(sources[s], t), ACT.Copy).then_inc(s_in, 1)

            def turn(q, slot, t, o_done):
                wait(act, s_turn, q + 1)
                wait(act, s_prod, o_done)
                nc.scalar.activation(c.xT[:, slot, :], c.ps[:, slot, :], ACT.Copy).then_inc(s_even, 1)

            def pair(k, first=False):
                for u in range(2):
                    t = k * 2 + u
                    for s in range(S):
                        slot = (u * S + s) % 2
                        q = t * S + s
                        turn(q, slot, t, 0 if first and q < 2 else O * ((q - 2) // S + 1) if first else
                             (O * (t - 1) if S == 1 else O * t))
                        if first or not isinstance(t, int) or q + 2 < T * S:
                            pass
                        nq = u * S + s + 2
                        if isinstance(k, int) and k == T // 2 - 1 and nq >= 2 * S:
                            continue
                        stage(k * 2 + nq // S, nq % S, slot)
            stage(0, 0, 0)
            stage(1 // S, 1 % S, 1)
            pair(0, first=True)
            with act.Fori(1, T // 2 - 1) as k:
                pair(k)
            pair(T // 2 - 1)

        @block.tensor
        def _(pe):
            pe.wait_ge(s_w, 16 * (len(weights) + len(rows))) if weights or rows else None

            def turn(q, slot):
                wait(pe, s_in, q + 1)
                wait(pe, s_even, q - 1)
                for b in range(KD):
                    last = nc.tensor.transpose(c.ps[:, slot, b * P:(b + 1) * P], c.xs[:, slot, b * P:(b + 1) * P],
                                               c.ident[:, :])
                last.then_inc(s_turn, 1)

            def multiply(t, u, s, slot):
                wait(pe, s_even, t * S + s + 1)
                for o in range(O):
                    if s == 0:
                        wait(pe, s_fin, O * (t - 2) + o + 1)
                    for b in range(KD):
                        last = nc.tensor.matmul(c.ps[:, 2 + 2 * o + u, :], c.xT[:, slot, b * P:(b + 1) * P],
                                                c.W[:, outputs[o][0][s], b * D:(b + 1) * D],
                                                start=(s == 0 and b == 0), stop=(s == S - 1 and b == KD - 1))
                    if s == S - 1:
                        last.then_inc(s_prod, 1)

            def pair(k, last_pair):
                for u in range(2):
                    t = k * 2 + u
                    for s in range(S):
                        q = t * S + s
                        if not (last_pair and u * S + s == 2 * S - 1):
                            turn(q + 1, (u * S + s + 1) % 2)
                        multiply(t, u, s, (u * S + s) % 2)
            turn(0, 0)
            pair(0, False)
            with pe.Fori(1, T // 2 - 1) as k:
                pair(k, False)
            pair(T // 2 - 1, True)

        @block.vector
        def _(dve):
            s_link = c.sem(f"{name}_link")
            if rows:
                dve.wait_ge(s_w, 16 * (len(weights) + len(rows)))

            def step(k, u):
                t = k * 2 + u
                wait(dve, s_fin, O * t)
                count = [0]
                per_tile = outputs_links(outputs)

                def link(ins):
                    count[0] += 1
                    ins.then_inc(s_link, 1)
                    wait(dve, s_link, t * per_tile + count[0])
                for o in range(O):
                    wait(dve, s_prod, O * t + o + 1)
                    if o == 0 and table is not None:
                        wait(dve, s_store[u], 16 * k)
                    outputs[o][1](link, t, c.ps[:, 2 + 2 * o + u, :], c.out[:, u, :]).then_inc(s_fin, 1)
            for u in range(2):
                step(0, u)
            with dve.Fori(1, T // 2) as k:
                for u in range(2):
                    step(k, u)


def outputs_links(outputs):
    return sum(o[2] for o in outputs)


@stage
def stage_rows(nc, c, name, pairs):
    s_in = c.sem(f"{name}_rows_in")
    with nc.Block() as block:
        @block.sync
        def _(sp):
            for buf, a in pairs:
                sp.dma_start(buf, a.partition_broadcast(P)).then_inc(s_in, 16)
            sp.wait_ge(s_in, 16 * len(pairs))


@stage
def stage_norm(nc, c, name, h, out, gamma=None, beta=None, relu=False, residual=None, copy=None, store=None):
    s_stat, s_var, s_root = (c.sem(f"{name}_{n}") for n in ("stats", "variance", "root"))
    s_link, s_out = c.sem(f"{name}_link"), c.sem(f"{name}_out")
    mv = c.mv[:, :].rearrange("p (t w) -> p t w", w=2)
    full = lambda b: b[:, :].rearrange("p (t d) -> p t d", t=T)
    wide = lambda row: row.unsqueeze(1).to_broadcast([P, T, D])
    with nc.Block() as block:
        @block.vector
        def _(dve):
            n = [0]

            def link(ins):
                n[0] += 1
                ins.then_inc(s_link, 1)
                dve.wait_ge(s_link, n[0])
            for t in range(T):
                last = nc.vector.bn_stats(c.st[:, t * 6:(t + 1) * 6], tile_of(h, t))
            link(last)
            for t in range(T):
                last = nc.vector.bn_aggr(c.mv[:, t * 2:(t + 1) * 2], c.st[:, t * 6:(t + 1) * 6])
            last.then_inc(s_var, 1)
            dve.wait_ge(s_root, 1)
            link(nc.vector.reciprocal(c.rstd[:, :], c.root[:, 0:T]))
            for t in range(T):
                last = nc.vector.tensor_scalar(tile_of(out, t), tile_of(h, t), c.mv[:, 2 * t:2 * t + 1],
                                               c.rstd[:, t:t + 1], ALU.subtract, ALU.mult)
            if gamma is not None:
                link(last)
                link(nc.vector.tensor_tensor(full(out), full(out), wide(gamma), ALU.mult))
                last = nc.vector.tensor_tensor(full(out), full(out), wide(beta), ALU.add)
            if relu:
                link(last)
                last = nc.vector.tensor_scalar(out[:, :], out[:, :], 0.0, None, ALU.max)
            if residual is not None:
                link(last)
                last = nc.vector.tensor_tensor(out[:, :], out[:, :], residual[:, :], ALU.add)
            last.then_inc(s_stat, 1)

        @block.scalar
        def _(act):
            act.wait_ge(s_var, 1)
            nc.scalar.activation(c.root[:, 0:T], mv[:, :, 1], ACT.Sqrt, bias=c.eps[:, :]).then_inc(s_root, 1)

        @block.sync
        def _(sp):
            if store is not None:
                sp.wait_ge(s_stat, 1)
                sp.dma_start(store.rearrange("(t p) d -> p t d", p=P), full(out)).then_inc(s_out, 16)
                sp.wait_ge(s_out, 16)



def gather_rows(nc, c, pool, count, table, width, source, sems, beside_half=None, beside=None):
    half = U // 2

    def step(k, u):
        i = k * U + u
        if u % half == 0:
            h = u // half
            for v in range(u, u + half):
                wait_apart(pool, sems.got[v], 16 * k, sems.passed)
            n = k * 2 + h
            nc.gpsimd.tensor_copy(c.idx[:, h * half:(h + 1) * half], source(n, half)).then_inc(sems.idx, 1)
            if beside_half:
                beside_half(k, u, n)
            wait_apart(pool, sems.idx, n + 1, sems.passed)
        if beside:
            beside(k, u)
        wait_apart(pool, sems.used, i - U + 1, sems.passed)
        pool.indirect_dma_start(out=c.G[:, u, 0:width], out_offset=None, in_=table,
                                in_offset=bass.IndirectOffsetOnAxis(ap=c.idx[:, u:u + 1], axis=0)).then_inc(sems.got[u], 16)
    run_steps(pool, count, step)


def edge_sems(c, name):
    s = Chip()
    s.got = [c.sem(f"{name}_got{u}") for u in range(U)]
    s.idx, s.used, s.passed = c.sem(f"{name}_indices"), c.sem(f"{name}_rows_used"), c.sem(f"{name}_wait_passed")
    return s


def tile_index(eng, tiles, i):
    return eng.value_load(tiles[0:1, i:i + 1] if isinstance(i, int) else tiles[0:1, bass.ds(i, 1)],
                          min_val=0, max_val=T - 1)


@stage
def stage_aggregate(nc, c, name, count, table, rec, width, tiles, first, weighted):
    s = edge_sems(c, name)
    s_hot, s_add, s_zero = (c.sem(f"{name}_{n}") for n in ("onehot", "added", "zeroed"))
    rec_i = rec.bitcast(I32)

    def source(n, half):
        lo = first + n * half
        r = rec_i.rearrange("p (c w) -> p c w", w=width)
        return r[:, lo:lo + half, 0] if isinstance(n, int) else r[:, bass.ds(lo, half), 0]
    with nc.Block() as block:
        @block.gpsimd
        def _(pool):
            gather_rows(nc, c, pool, count, table, D, source, s)

        @block.tensor
        def _(pe):
            def step(k, u):
                i = k * U + u
                wait(pe, s.got[u], 16 * (k + 1))
                wait(pe, s_hot, i + 1)
                wait(pe, s_add, i - 1)
                nc.tensor.matmul(c.ps[:, u % 2, :], c.hot[:, u % 2, :], c.G[:, u, 0:D],
                                 start=True, stop=True).then_inc(s.used, 1)
            run_steps(pe, count, step)

        @block.vector
        def _(dve):
            nc.vector.memset(c.ACC[:, :], 0.0).then_inc(s_zero, 1)
            dve.wait_ge(s_zero, 1)

            def step(k, u):
                i = k * U + u
                if live(i, count):
                    wait(dve, s.used, i - 1)
                    r = col(rec, first + i, width)
                    if weighted:
                        ins = nc.vector.tensor_scalar(c.hot[:, u % 2, :], c.iota[:, :], r[:, 1:2], r[:, 2:3],
                                                      ALU.is_equal, ALU.mult)
                    else:
                        ins = nc.vector.tensor_scalar(c.hot[:, u % 2, :], c.iota[:, :], r[:, 1:2], None, ALU.is_equal)
                    ins.then_inc(s_hot, 1)
                j, slot, _ = back(k, u, 1)
                if live(j, count):
                    t = tile_index(dve, tiles, first + j)
                    wait(dve, s.used, j + 1)
                    wait(dve, s_add, j)
                    acc = tile_of(c.ACC, t)
                    nc.vector.tensor_tensor(acc, acc, c.ps[:, slot % 2, :], ALU.add).then_inc(s_add, 1)
            run_steps(dve, count, step, lag=1)


@stage
def stage_attention_edges(nc, c, name, table, rows, we):
    s = edge_sems(c, name)
    (s_rec, s_hot, s_far, s_tr, s_ev, s_z, s_s, s_dot, s_lg, s_msk, s_mT, s_mx, s_mn, s_df, s_upd, s_exp, s_pT, s_w, s_acc,
     s_den) = (c.sem(f"{name}_{n}") for n in (
        "records_copied", "onehot", "far", "turned", "turned_copied", "product", "sum", "dot", "logit", "masked",
        "masked_turned", "chunk_max", "new_max", "shifts", "max_kept", "exp", "exp_turned", "exp_copied", "added",
        "sum_kept"))
    s_in, s_prep, s_we = c.sem(f"{name}_rows_in"), c.sem(f"{name}_prep"), c.sem(f"{name}_We_parts")

    def source(n, half):
        r = c.rec_i[:, :].rearrange("p (c w) -> p c w", w=HW)
        return r[:, n * half:(n + 1) * half, 0] if isinstance(n, int) else r[:, bass.ds(n * half, half), 0]
    B_T, B_Z, B_M, B_W, B_O = 0, 1, 3, 5, 6
    with nc.Block() as block:
        @block.sync
        def _(sp):
            for buf, a in rows:
                sp.dma_start(buf, a.partition_broadcast(P)).then_inc(s_in, 16)
            for n in range(3):
                sp.dma_start(c.We32[2 * n:2 * n + 2, :], we).then_inc(s_in, 16)

        @block.vector
        def _(dve):
            n = [0]

            def link(ins):
                n[0] += 1
                ins.then_inc(s_prep, 1)
                dve.wait_ge(s_prep, n[0])
            dve.wait_ge(s_in, 16 * (len(rows) + 3))
            for a in range(2):
                link(nc.vector.tensor_tensor_reduce(out=c.R[:, :], in0=c.WeB[:, a * D:(a + 1) * D], in1=c.attB[:, :],
                                                    scale=SLOPE, scalar=0.0, op0=ALU.mult, op1=ALU.add,
                                                    accum_out=c.cvec[:, a:a + 1]))
            lin = c.parts[:, :].rearrange("p (c w) -> p c w", w=AW)[:, :, 6]
            link(nc.vector.tensor_scalar(lin, c.rec3[:, :, 2], c.cvec[:, 0:1], None, ALU.mult))
            link(nc.vector.scalar_tensor_tensor(lin, c.rec3[:, :, 3], c.cvec[:, 1:2], lin, ALU.mult, ALU.add))
            link(nc.vector.tensor_copy(c.WeR[:, :], c.We32[:, :]))
            link(nc.vector.tensor_scalar(c.We32[:, :], c.We32[:, :], c.low[0:6, :], None, ALU.mult))
            link(nc.vector.scalar_tensor_tensor(c.WeR[:, :], c.WeR[:, :], c.sign[0:6, :], c.We32[:, :], ALU.mult, ALU.add))
            nc.vector.memset(c.ACC[:, :], 0.0)
            nc.vector.memset(c.den[:, :], 0.0)
            nc.vector.memset(c.MA[:, :].rearrange("p (t w) -> p t w", w=2)[:, :, 0], -FAR)
    half = U // 2
    with nc.Block() as block:
        @block.gpsimd
        def _(pool):
            def records(k, u, n):
                wait_apart(pool, s_msk, k * U + u - half, s.passed)
                r = c.rec[:, :].rearrange("p (c w) -> p c w", w=HW)
                loc = r[:, n * half:(n + 1) * half, 1] if isinstance(n, int) else r[:, bass.ds(n * half, half), 1]
                nc.gpsimd.tensor_copy(c.local[:, u:u + half], loc)
                nc.gpsimd.tensor_copy(c.attr[:, u:u + half, :].rearrange("p c w -> p (c w)"),
                                      col(c.parts, n, half * AW)).then_inc(s_rec, 1)

            def masks(k, u):
                i = k * U + u
                wait_apart(pool, s_msk, i - 3, s.passed)
                if u % half == 0:
                    wait_apart(pool, s_rec, 2 * k + u // half + 1, s.passed)
                loc = c.local[:, u:u + 1]
                nc.gpsimd.tensor_scalar(c.hot4[:, u % 4, :], c.iota[:, :], loc, None, ALU.is_equal).then_inc(s_hot, 1)
                wait_apart(pool, s_hot, i + 1, s.passed)
                nc.gpsimd.tensor_scalar(c.far[:, u % 4, :], c.hot4[:, u % 4, :], -1.0, FAR, ALU.add,
                                        ALU.mult).then_inc(s_far, 1)
            gather_rows(nc, c, pool, C1, table, TW, source, s, records, masks)

        @block.scalar
        def _(act):
            def step(k, u):
                j, v, _ = back(k, u, 5)
                if live(j, C1):
                    wait(act, s_df, j + 1)
                    wait(act, s_den, j - 3)
                    nc.scalar.activation(c.scale[:, v % 4:v % 4 + 1], c.diff[:, 2 * (v % 2):2 * (v % 2) + 1], ACT.Exp)
                    wait(act, s_pT, j - 1)
                    nc.scalar.activation(c.PT[:, v % 2, :], c.ps[:, B_M + v % 2, 0:P], ACT.Exp,
                                         bias=c.diff[:, 2 * (v % 2) + 1:2 * (v % 2) + 2],
                                         accum_out=c.rowsum[:, v % 4:v % 4 + 1]).then_inc(s_exp, 1)
                i, v, _ = back(k, u, 0)
                if live(i, C1):
                    wait(act, s_tr, i + 1)
                    wait(act, s_z, i - 1)
                    nc.scalar.activation(c.oT[:, v % 2, :], c.ps[:, B_T, 0:P], ACT.Copy)
                    nc.scalar.activation(c.eT[0:6, v % 2, :], c.ps[0:6, B_T, P:2 * P], ACT.Copy).then_inc(s_ev, 1)
                j, v, _ = back(k, u, 5)
                if live(j, C1):
                    wait(act, s_pT, j + 1)
                    wait(act, s.used, j - 1)
                    nc.scalar.activation(c.Wt[:, v % 2, :], c.ps[:, B_W, 0:P], ACT.Copy).then_inc(s_w, 1)
                j, v, _ = back(k, u, 2)
                if live(j, C1):
                    wait(act, s_dot, j + 1)
                    lg = c.lg[:, 2 * (v % 2):2 * (v % 2) + 2]
                    nc.scalar.activation(lg[:, 0:1], c.dot[:, v % 2:v % 2 + 1], ACT.Identity, bias=c.G[:, v, D:D + 1],
                                         scale=1.0 - SLOPE).then_inc(s_lg, 1)
                    wait(act, s_lg, 2 * j + 1)
                    nc.scalar.activation(lg[:, 1:2], lg[:, 0:1], ACT.Identity, bias=c.attr[:, v, 6:7]).then_inc(s_lg, 1)
                    wait(act, s_lg, 2 * j + 2)
                    wait(act, s_far, j + 1)
                    wait(act, s_mT, j - 1)
                    nc.scalar.activation(c.masked[:, v % 2, :], c.far[:, v % 4, :], ACT.Identity,
                                         bias=lg[:, 1:2]).then_inc(s_msk, 1)
            run_steps(act, C1, step, lag=5)

        @block.tensor
        def _(pe):
            def step(k, u):
                i, v, _ = back(k, u, 0)
                if live(i, C1):
                    wait(pe, s_hot, i + 1)
                    if v % half == 0:
                        wait(pe, s_rec, 2 * k + u // half + 1)
                    wait(pe, s_ev, i)
                    nc.tensor.transpose(c.ps[:, B_T, 0:P], c.hot4[:, v % 4, :], c.ident[:, :])
                    nc.tensor.transpose(c.ps[0:6, B_T, P:2 * P], c.attr[:, v, 0:6], c.ident[:, :]).then_inc(s_tr, 1)
                j, v, _ = back(k, u, 1)
                if live(j, C1):
                    t = tile_index(pe, c.tiles_dst, j)
                    wait(pe, s_ev, j + 1)
                    wait(pe, s_s, j - 1)
                    nc.tensor.matmul(c.ps[:, B_Z + v % 2, :], c.oT[:, v % 2, :], tile_of(c.XRh, t), start=True, stop=False)
                    nc.tensor.matmul(c.ps[:, B_Z + v % 2, :], c.oT[:, v % 2, :], tile_of(c.XRl, t), start=False, stop=False)
                    nc.tensor.matmul(c.ps[:, B_Z + v % 2, :], c.eT[0:6, v % 2, :], c.WeR[0:6, :], start=False,
                                     stop=True).then_inc(s_z, 1)
                j, v, _ = back(k, u, 3)
                if live(j, C1):
                    wait(pe, s_msk, j + 1)
                    wait(pe, s_exp, j - 1)
                    nc.tensor.transpose(c.ps[:, B_M + v % 2, 0:P], c.masked[:, v % 2, :], c.ident[:, :]).then_inc(s_mT, 1)
                j, v, _ = back(k, u, 5)
                if live(j, C1):
                    wait(pe, s_exp, j + 1)
                    wait(pe, s_w, j)
                    nc.tensor.transpose(c.ps[:, B_W, 0:P], c.PT[:, v % 2, :], c.ident[:, :]).then_inc(s_pT, 1)
                j, v, _ = back(k, u, 6)
                if live(j, C1):
                    wait(pe, s_w, j + 1)
                    wait(pe, s_acc, j - 1)
                    nc.tensor.matmul(c.ps[:, B_O + v % 2, :], c.Wt[:, v % 2, :], c.G[:, v, 0:D],
                                     start=True, stop=True).then_inc(s.used, 1)
            run_steps(pe, C1, step, lag=6)

        @block.vector
        def _(dve):
            def step(k, u):
                j, v, r = back(k, u, 2)
                if live(j, C1):
                    wait(dve, s_z, j + 1)
                    wait(dve, s.got[v], 16 * (r + 1))
                    wait(dve, s_dot, j)
                    nc.vector.tensor_tensor(c.S[:, :], c.ps[:, B_Z + v % 2, :], c.G[:, v, 0:D], ALU.add).then_inc(s_s, 1)
                m, w, _ = back(k, u, 4)
                if live(m, C1):
                    t = tile_index(dve, c.tiles_dst, m)
                    MA = c.MA[:, bass.ds(t * 2, 2)]
                    cmax, mnew = c.cmax[:, w % 2:w % 2 + 1], c.mnew[:, w % 2:w % 2 + 1]
                    wait(dve, s_mT, m + 1)
                    nc.vector.tensor_reduce(cmax, c.ps[:, B_M + w % 2, 0:P], AX.X, ALU.max).then_inc(s_mx, 1)
                if live(j, C1):
                    wait(dve, s_s, j + 1)
                    wait(dve, s_lg, 2 * j - 3)
                    nc.vector.scalar_tensor_tensor(c.R[:, :], c.S[:, :], 0.0, c.attB[:, :], ALU.max, ALU.mult,
                                                   accum_out=c.dot[:, v % 2:v % 2 + 1]).then_inc(s_dot, 1)
                if live(m, C1):
                    wait(dve, s_mx, m + 1)
                    wait(dve, s_upd, m)
                    nc.vector.scalar_tensor_tensor(mnew, cmax, MA[:, 1:2], MA[:, 0:1], ALU.add, ALU.max).then_inc(s_mn, 1)
                q, x, _ = back(k, u, 7)
                if live(q, C1):
                    t2 = tile_index(dve, c.tiles_dst, q)
                    den, acc = c.den[:, bass.ds(t2, 1)], tile_of(c.ACC, t2)
                    wait(dve, s_exp, q + 1)
                    wait(dve, s.used, q + 1)
                    wait(dve, s_acc, q)
                    nc.vector.scalar_tensor_tensor(acc, acc, c.scale[:, x % 4:x % 4 + 1], c.ps[:, B_O + x % 2, :],
                                                   ALU.mult, ALU.add).then_inc(s_acc, 1)
                if live(m, C1):
                    wait(dve, s_mn, m + 1)
                    wait(dve, s_exp, m - 1)
                    nc.vector.tensor_scalar(c.diff[:, 2 * (w % 2):2 * (w % 2) + 2], MA, mnew, None,
                                            ALU.subtract).then_inc(s_df, 1)
                if live(q, C1):
                    wait(dve, s_den, q)
                    nc.vector.scalar_tensor_tensor(den, den, c.scale[:, x % 4:x % 4 + 1], c.rowsum[:, x % 4:x % 4 + 1],
                                                   ALU.mult, ALU.add).then_inc(s_den, 1)
                if live(m, C1):
                    wait(dve, s_df, m + 1)
                    nc.vector.tensor_scalar(MA[:, 0:1], mnew, 0.0, None, ALU.add).then_inc(s_upd, 1)
            run_steps(dve, C1, step, lag=7)


@stage
def stage_attention_close(nc, c, name):
    s_link = c.sem(f"{name}_link")
    full = lambda b: b[:, :].rearrange("p (t d) -> p t d", t=T)
    with nc.Block() as block:
        @block.vector
        def _(dve):
            n = [0]

            def link(ins):
                n[0] += 1
                ins.then_inc(s_link, 1)
                dve.wait_ge(s_link, n[0])
            link(nc.vector.tensor_scalar(c.den[:, :], c.den[:, :], 1e-16, None, ALU.add))
            link(nc.vector.reciprocal(c.den[:, :], c.den[:, :]))
            for t in range(T):
                last = nc.vector.scalar_tensor_tensor(tile_of(c.ACC, t), tile_of(c.ACC, t), c.den[:, t:t + 1],
                                                      tile_of(c.X, t), ALU.mult, ALU.add)
            link(last)
            nc.vector.tensor_tensor(full(c.ACC), full(c.ACC), c.row2[:, :].unsqueeze(1).to_broadcast([P, T, D]), ALU.add)


@stage
def stage_messages(nc, c, table, w1c, w2, b2):
    s = edge_sems(c, "msg")
    (s_hot, s_tr, s_ev, s_z, s_s, s_c1, s_a1, s_q1, s_h, s_hT, s_hc, s_lo, s_o, s_c2, s_a2, s_q2, s_m, s_agg, s_acc,
     s_init) = (c.sem(f"msg_{n}") for n in (
        "onehot", "turned", "turned_copied", "product1", "sum", "clamped1", "chain1", "ratio1", "hidden",
        "hidden_turned", "hidden_high", "hidden_low", "product2", "clamped2", "chain2", "ratio2", "message", "agg",
        "acc_added", "init"))
    s_attr = [c.sem(f"msg_attr_in{u}") for u in range(U)]
    s_el = c.sem("msg_attr_low")
    s.used = s_s
    s_w, s_prep, s_wf = c.sem("msg_weights_in"), c.sem("msg_prep"), c.sem("msg_weights_free")
    B_T, B_Z, B_H, B_O, B_A = 0, 2, 4, 5, 7
    rows = c.by_dst.rearrange("(p c) w -> p c w", p=P)

    def source(n, half):
        r = c.rec_i[:, :].rearrange("p (c w) -> p c w", w=HW)
        lo = n * half + T
        return r[:, lo:lo + half, 0] if isinstance(n, int) else r[:, bass.ds(lo, half), 0]
    with nc.Block() as block:
        @block.sync
        def _(sp):
            sp.dma_start(c.S[0:EA, 0, :], w1c).then_inc(s_w, 16)
            sp.dma_start(c.S[EA:2 * EA, 0, :], w1c).then_inc(s_w, 16)
            sp.dma_start(c.H[0:1, 0, :], b2.rearrange("(o d) -> o d", o=1)).then_inc(s_w, 16)
            sp.dma_start(c.M[:, 0, :], w2[0:P, :]).then_inc(s_w, 16)
            for b in range(1, KD):
                sp.wait_ge(s_wf, b)
                sp.dma_start(c.M[:, 0, :], w2[b * P:(b + 1) * P, :]).then_inc(s_w, 16)

        @block.vector
        def _(dve):
            n = [0]

            def link(ins):
                n[0] += 1
                ins.then_inc(s_prep, 1)
                dve.wait_ge(s_prep, n[0])
            nc.vector.tensor_copy(c.one_row[:, :], c.ones[0:1, :])
            nc.vector.memset(c.ACC[:, :], 0.0)
            dve.wait_ge(s_w, 64)
            link(nc.vector.tensor_copy(c.W1ch[:, :], c.S[:, 0, :]))
            nc.vector.tensor_tensor(c.W1cl[:, :], c.S[0:EA, 0, :], c.W1ch[0:EA, :], ALU.subtract)
            link(nc.vector.tensor_copy(c.b2h[:, :], c.H[0:1, 0, :]))
            nc.vector.tensor_tensor(c.b2l[:, :], c.H[0:1, 0, :], c.b2h[:, :], ALU.subtract)
            for b in range(KD):
                dve.wait_ge(s_w, 64 + 16 * b)
                link(nc.vector.tensor_scalar(c.M[:, 0, :], c.M[:, 0, :], -2.0, None, ALU.mult))
                link(nc.vector.tensor_copy(c.W2h[:, b * D:(b + 1) * D], c.M[:, 0, :]))
                nc.vector.tensor_tensor(c.W2l[:, b * D:(b + 1) * D], c.M[:, 0, :], c.W2h[:, b * D:(b + 1) * D],
                                        ALU.subtract).then_inc(s_wf, 1)
                dve.wait_ge(s_wf, b + 1)
    with nc.Block() as block:
        @block.sync
        def _(sp):
            def step(k, u):
                i = k * U + u
                wait_apart(sp, s_tr, i - U + 1, s.passed)
                a = rows[:, i, HW:RW] if isinstance(i, int) else rows[:, bass.ds(i, 1), HW:RW]
                sp.dma_start(c.ea[:, u, :], a).then_inc(s_attr[u], 16)
            run_steps(sp, NCH, step)

        @block.gpsimd
        def _(pool):
            gather_rows(nc, c, pool, NCH, table, D, source, s)

        @block.tensor
        def _(pe):
            def step(k, u):
                i, v, r = back(k, u, 0)
                if live(i, NCH):
                    wait(pe, s_hot, i + 1)
                    wait(pe, s_attr[v], 16 * (r + 1))
                    wait(pe, s_ev, i - 1)
                    wait(pe, s_el, i - 1)
                    nc.tensor.transpose(c.ps[:, B_T + v % 2, 0:P], c.hot[:, v % 2, :], c.ident[:, :])
                    nc.tensor.transpose(c.ps[0:EA, B_T + v % 2, P:2 * P], c.ea[:, v, :], c.ident[:, :]).then_inc(s_tr, 1)
                j, v, _ = back(k, u, 4)
                if live(j, NCH):
                    wait(pe, s_h, j + 1)
                    wait(pe, s_hc, j)
                    wait(pe, s_lo, j)
                    for b in range(KD):
                        last = nc.tensor.transpose(c.ps[:, B_H, b * P:(b + 1) * P], c.H[:, v % 2, b * P:(b + 1) * P],
                                                   c.ident[:, :])
                    last.then_inc(s_hT, 1)
                j, v, _ = back(k, u, 1)
                if live(j, NCH):
                    t = tile_index(pe, c.tiles_dst, T + j)
                    wait(pe, s_ev, j + 1)
                    wait(pe, s_el, j + 1)
                    wait(pe, s_s, j - 1)
                    z = c.ps[:, B_Z + v % 2, :]
                    nc.tensor.matmul(z, c.oT[:, v % 2, :], tile_of(c.XRh, t), start=True, stop=False)
                    nc.tensor.matmul(z, c.oT[:, v % 2, :], tile_of(c.XRl, t), start=False, stop=False)
                    nc.tensor.matmul(z, c.eT2[:, v % 2, :], c.W1ch[:, :], start=False, stop=False)
                    nc.tensor.matmul(z, c.eT2[0:EA, v % 2, :], c.W1cl[:, :], start=False, stop=True).then_inc(s_z, 1)
                j, v, _ = back(k, u, 7)
                if live(j, NCH):
                    wait(pe, s_m, j + 1)
                    wait(pe, s_acc, j)
                    nc.tensor.matmul(c.ps[:, B_A, :], c.hotm[:, v % 2, :], c.M[:, v % 2, :],
                                     start=True, stop=True).then_inc(s_agg, 1)
                j, v, _ = back(k, u, 4)
                if live(j, NCH):
                    wait(pe, s_m, j - 1)
                    o = c.ps[:, B_O + v % 2, :]
                    nc.tensor.matmul(o, c.one_row[:, :], c.b2h[:, :], start=True, stop=False)
                    nc.tensor.matmul(o, c.one_row[:, :], c.b2l[:, :], start=False, stop=False)
                    wait(pe, s_hc, j + 1)
                    for b in range(KD):
                        h = c.hTh[:, v % 2, b * P:(b + 1) * P]
                        nc.tensor.matmul(o, h, c.W2h[:, b * D:(b + 1) * D], start=False, stop=False)
                        nc.tensor.matmul(o, h, c.W2l[:, b * D:(b + 1) * D], start=False, stop=False)
                    wait(pe, s_lo, j + 1)
                    for b in range(KD):
                        last = nc.tensor.matmul(o, c.hTl[:, v % 2, b * P:(b + 1) * P], c.W2h[:, b * D:(b + 1) * D],
                                                start=False, stop=(b == KD - 1))
                    last.then_inc(s_o, 1)
            run_steps(pe, NCH, step, lag=7)

        @block.scalar
        def _(act):
            def ratio(j, v, x, chain, buf, done):
                nc.scalar.activation(buf, x, ACT.Exp).then_inc(chain, 1)
                wait(act, chain, 3 * j + 1)
                nc.scalar.activation(buf, buf, ACT.Square, bias=c.ones[:, 0:1]).then_inc(chain, 1)
                wait(act, chain, 3 * j + 2)
                nc.scalar.activation(buf, buf, ACT.Ln, bias=c.ones[:, 0:1]).then_inc(chain, 1)
                wait(act, chain, 3 * j + 3)
                nc.scalar.activation(buf, buf, ACT.Exp, scale=-1.0).then_inc(done, 1)

            def step(k, u):
                i, v, _ = back(k, u, 0)
                if live(i, NCH):
                    wait(act, s_tr, i + 1)
                    wait(act, s_z, i - 1)
                    nc.scalar.activation(c.oT[:, v % 2, :], c.ps[:, B_T + v % 2, 0:P], ACT.Copy)
                    nc.scalar.activation(c.eT2[0:EA, v % 2, :], c.ps[0:EA, B_T + v % 2, P:2 * P], ACT.Copy).then_inc(s_ev, 1)
                j, v, _ = back(k, u, 4)
                if live(j, NCH):
                    wait(act, s_hT, j + 1)
                    wait(act, s_o, j - 1)
                    nc.scalar.activation(c.hTh[:, v % 2, :], c.ps[:, B_H, :], ACT.Copy).then_inc(s_hc, 1)
                j, v, _ = back(k, u, 2)
                if live(j, NCH):
                    wait(act, s_c1, j + 1)
                    wait(act, s_h, j - 1)
                    ratio(j, v, c.C1[:, v % 2, :], s_a1, c.Q[:, v % 2, :], s_q1)
                j, v, _ = back(k, u, 5)
                if live(j, NCH):
                    wait(act, s_c2, j + 1)
                    wait(act, s_m, j - 1)
                    ratio(j, v, c.C2[:, :], s_a2, c.Q2[:, v % 2, :], s_q2)
            nc.scalar.preload_act_table_set("natural_log_exp_and_others")
            run_steps(act, NCH, step, lag=5)

        @block.vector
        def _(dve):
            def step(k, u):
                i, v, _ = back(k, u, 0)
                if live(i, NCH):
                    wait(dve, s_tr, i - 1)
                    nc.vector.tensor_scalar(c.hot[:, v % 2, :], c.iota[:, :], col(c.rec, T + i, HW)[:, 1:2], None,
                                            ALU.is_equal).then_inc(s_hot, 1)
                j, v, _ = back(k, u, 8)
                if live(j, NCH):
                    t = tile_index(dve, c.tiles_dst, T + j)
                    acc = tile_of(c.ACC, t)
                    wait(dve, s_agg, j + 1)
                    wait(dve, s_acc, j)
                    nc.vector.tensor_tensor(acc, acc, c.ps[:, B_A, :], ALU.add).then_inc(s_acc, 1)
                j, v, _ = back(k, u, 6)
                if live(j, NCH):
                    wait(dve, s_agg, j - 1)
                    nc.vector.tensor_scalar(c.hotm[:, v % 2, :], c.iota[:, :], col(c.rec, T + j, HW)[:, 1:2], -2.0,
                                            ALU.is_equal, ALU.mult)
                    wait(dve, s_q2, j + 1)
                    nc.vector.scalar_tensor_tensor(c.M[:, v % 2, :], c.Q2[:, v % 2, :], 0.5, c.ps[:, B_O + v % 2, :],
                                                   ALU.subtract, ALU.mult).then_inc(s_m, 1)
                j, v, _ = back(k, u, 1)
                if live(j, NCH):
                    wait(dve, s_ev, j + 1)
                    nc.vector.tensor_tensor(c.eT2[EA:2 * EA, v % 2, :], c.ps[0:EA, B_T + v % 2, P:2 * P],
                                            c.eT2[0:EA, v % 2, :], ALU.subtract).then_inc(s_el, 1)
                j, v, r = back(k, u, 2)
                if live(j, NCH):
                    wait(dve, s_z, j + 1)
                    wait(dve, s.got[v], 16 * (r + 1))
                    wait(dve, s_h, j - 1)
                    nc.vector.tensor_tensor(c.S[:, v % 2, :], c.ps[:, B_Z + v % 2, :], c.G[:, v, 0:D], ALU.add).then_inc(s_s, 1)
                j, v, _ = back(k, u, 5)
                if live(j, NCH):
                    wait(dve, s_o, j + 1)
                    wait(dve, s_a2, 3 * j)
                    nc.vector.tensor_scalar(c.C2[:, :], c.ps[:, B_O + v % 2, :], CLAMP, None, ALU.min).then_inc(s_c2, 1)
                j, v, r = back(k, u, 2)
                if live(j, NCH):
                    wait(dve, s_s, j + 1)
                    wait(dve, s_q1, j - 1)
                    nc.vector.tensor_scalar(c.C1[:, v % 2, :], c.S[:, v % 2, :], CLAMP, None, ALU.min).then_inc(s_c1, 1)
                j, v, _ = back(k, u, 3)
                if live(j, NCH):
                    wait(dve, s_q1, j + 1)
                    wait(dve, s_hT, j - 1)
                    nc.vector.scalar_tensor_tensor(c.H[:, v % 2, :], c.Q[:, v % 2, :], 0.5, c.S[:, v % 2, :], ALU.subtract,
                                                   ALU.mult).then_inc(s_h, 1)
                j, v, _ = back(k, u, 4)
                if live(j, NCH):
                    wait(dve, s_hc, j + 1)
                    wait(dve, s_o, j - 1)
                    nc.vector.tensor_tensor(c.hTl[:, v % 2, :], c.ps[:, B_H, :], c.hTh[:, v % 2, :],
                                            ALU.subtract).then_inc(s_lo, 1)
            run_steps(dve, NCH, step, lag=8)


@stage
def stage_mish(nc, c, buf):
    s_c, s_a, s_q, s_m, s_o = (c.sem(f"mish_{n}") for n in ("clamped", "chain", "ratio", "product", "done"))
    with nc.Block() as block:
        @block.scalar
        def _(act):
            nc.scalar.preload_act_table_set("natural_log_exp_and_others")
            for t in range(T):
                q = c.Q[:, t % 2, :]
                act.wait_ge(s_c, t + 1)
                if t >= 2:
                    act.wait_ge(s_m, t - 1)
                nc.scalar.activation(q, c.S[:, t % 2, :], ACT.Exp).then_inc(s_a, 1)
                act.wait_ge(s_a, 3 * t + 1)
                nc.scalar.activation(q, q, ACT.Square, bias=c.ones[:, 0:1]).then_inc(s_a, 1)
                act.wait_ge(s_a, 3 * t + 2)
                nc.scalar.activation(q, q, ACT.Ln, bias=c.ones[:, 0:1]).then_inc(s_a, 1)
                act.wait_ge(s_a, 3 * t + 3)
                nc.scalar.activation(q, q, ACT.Exp, scale=-1.0).then_inc(s_q, 1)

        @block.vector
        def _(dve):
            for t in range(T + 1):
                if t < T:
                    if t >= 2:
                        dve.wait_ge(s_q, t - 1)
                    nc.vector.tensor_scalar(c.S[:, t % 2, :], tile_of(buf, t), CLAMP, None, ALU.min).then_inc(s_c, 1)
                if t >= 1:
                    b = tile_of(buf, t - 1)
                    dve.wait_ge(s_q, t)
                    nc.vector.scalar_tensor_tensor(b, c.Q[:, (t - 1) % 2, :], 0.5, b, ALU.subtract, ALU.mult).then_inc(s_m, 1)
                    dve.wait_ge(s_m, t)
                    nc.vector.tensor_scalar(b, b, -2.0, None, ALU.mult)


@stage
def stage_scaled_table(nc, c, table):
    s_sc, s_st = c.sem("scaled_ready"), c.sem("scaled_stored")
    with nc.Block() as block:
        @block.vector
        def _(dve):
            for t in range(T):
                last = nc.vector.tensor_scalar(tile_of(c.XR, t), tile_of(c.X, t), c.dis[:, t:t + 1], None, ALU.mult)
            last.then_inc(s_sc, 1)

        @block.sync
        def _(sp):
            sp.wait_ge(s_sc, 1)
            sp.dma_start(table.rearrange("(t p) d -> p t d", p=P), c.XR[:, :].rearrange("p (t d) -> p t d", t=T))\
              .then_inc(s_st, 16)
            sp.wait_ge(s_st, 16)


@stage
def stage_nodes_back(nc, c, table):
    s_x = c.sem("nodes_back")
    with nc.Block() as block:
        @block.sync
        def _(sp):
            sp.dma_start(c.X.rearrange("p (t d) -> p t d", t=T), table.rearrange("(t p) d -> p t d", p=P)).then_inc(s_x, 16)
            sp.wait_ge(s_x, 16)


@stage
def stage_split_attributes(nc, c):
    s_h = c.sem("split_high")
    p7, p7r = (x.rearrange("p (c w) -> p c w", w=AW) for x in (c.parts[:, :], c.parts[:, :].bitcast(F32R)))
    with nc.Block() as block:
        @block.vector
        def _(dve):
            nc.vector.tensor_copy(p7r[:, :, 0:2], c.rec3[:, :, 2:4]).then_inc(s_h, 1)
            nc.vector.tensor_copy(p7r[:, :, 2:4], c.rec3[:, :, 2:4])
            dve.wait_ge(s_h, 1)
            nc.vector.tensor_tensor(p7r[:, :, 4:6], c.rec3[:, :, 2:4], p7[:, :, 0:2], ALU.subtract)


def gnn_stack(nc, a, out):
    c = Chip()
    c.sems = []

    def sem(name):
        c.sems.append(nc.alloc_semaphore(name=name))
        return c.sems[-1]
    c.sem = sem
    numbered = [0]

    def allocator(scope):
        def sb(name, shape, dt=F32):
            numbered[0] += 1
            return scope.enter_context(nc.sbuf_tensor(f"{name}_{numbered[0]}", shape, dt))
        return sb

    def dram(name, shape):
        return nc.dram_tensor(name, shape, F32, kind="Internal").ap()

    c.by_dst, c.by_src = dram("by_dst", [P * NCH, RW]), dram("by_src", [P * NCH, SW])
    table, table_att, table_res = dram("table", [N, D]), dram("table_att", [N, TW]), dram("table_res", [N, D])
    with ExitStack() as whole:
        sb = allocator(whole)
        c.ps = whole.enter_context(nc.psum_tensor("ps", [P, 8, 512], F32))
        c.rec = sb("rec", [P, C1 * HW])[:, :]
        c.rec_i = c.rec.bitcast(I32)
        c.rec3, c.rec3_i = (r.rearrange("p (c w) -> p c w", w=HW) for r in (c.rec, c.rec_i))
        c.tiles_dst, c.tiles_src = sb("tiles_dst", [1, C1], I32), sb("tiles_src", [1, NCH], I32)
        c.iota, c.ones, c.ident, c.eps = sb("iota", [P, P]), sb("ones", [P, P]), sb("ident", [P, P]), sb("eps", [P, 1])
        c.node_i, c.tile_i, c.lane_i = sb("node_i", [P, T], I32), sb("tile_i", [P, T], I32), sb("lane_i", [P, 1], I32)
        c.lane_f, c.low, c.low2, c.sign = (sb(n, [P, 1]) for n in ("lane_f", "low", "low2", "sign"))
        c.counts, c.small, c.small_i = sb("counts", [P, T]), sb("small", [P, 4 * T]), sb("small_i", [P, 2 * T], I32)
        c.idx, c.idx0 = sb("idx", [P, U], I32), sb("idx0", [P, U], I32)
        c.deg, c.deg1, c.dis, c.root = sb("deg", [P, 3 * T]), sb("deg1", [P, T]), sb("dis", [P, T]), sb("root", [P, T])
        c.mv, c.st, c.rstd = sb("mv", [P, 2 * T]), sb("st", [P, 6 * T]), sb("rstd", [P, T])
        c.cvec, c.den, c.MA = sb("cvec", [P, 2]), sb("den", [P, T]), sb("MA", [P, 2 * T])

        with ExitStack() as scope:
            sb = allocator(scope)
            c.recs, c.recs0 = sb("recs", [P, EC * RW])[:, :], sb("recs0", [P, EC * SW])[:, :]
            c.recs3 = c.recs.rearrange("p (j w) -> p j w", w=RW)
            c.recs3_i = c.recs.bitcast(I32).rearrange("p (j w) -> p j w", w=RW)
            c.recs0_3 = c.recs0.rearrange("p (j w) -> p j w", w=SW)
            c.recs0_3i = c.recs0.bitcast(I32).rearrange("p (j w) -> p j w", w=SW)
            c.member, c.running = sb("member", [P, T * EC]), sb("running", [P, T * EC])
            c.PADS = 16
            c.pads, c.pads0 = sb("pads", [P, c.PADS * RW]), sb("pads0", [P, NCH * SW])
            c.bin_f, c.bin_g, c.edge_ones, c.weight = (sb(n, [P, EC]) for n in ("bin_f", "bin_g", "edge_ones", "weight"))
            c.attr2 = sb("attr2", [P, 2 * EC])
            c.key_src, c.key_dst, c.rows_dst, c.rows_src = (sb(n, [P, EC], I32) for n in (
                "key_src", "key_dst", "rows_dst", "rows_src"))
            c.tmp_i, c.iota_i, c.upper = sb("tmp_i", [P, 3 * EC], I32), sb("iota_i", [P, P], I32), sb("upper", [P, P])
            c.chunk_i, c.chunk_f, c.tile_f = sb("chunk_i", [P, NCH], I32), sb("chunk_f", [P, NCH]), sb("tile_f", [1, NCH])
            c.stage, c.stage0 = sb("stage", [P, U * RW]), sb("stage0", [P, U * SW])
            stage_constants(nc, c)
            stage_bin(nc, c, a["src"], a["dst"], a["edge_attr_2"], a["edge_attr_64"], a["edge_weight"])
            stage_scatter(nc, c)

        sb = allocator(whole)
        c.X, c.ACC = sb("X", [P, T * D])[:, :], sb("ACC", [P, T * D])[:, :]
        c.G = sb("G", [P, U, TW])
        c.hot = sb("hot", [P, 2, P])
        with ExitStack() as scope:
            sb = allocator(scope)
            c.rec0 = sb("rec0", [P, NCH * SW])[:, :]
            with ExitStack() as inner:
                c.wide = allocator(inner)("wide", [P, NCH * RW])
                stage_heads(nc, c, a["x"])
            c.hot4 = sb("hot4", [P, 4, P])
            stage_degrees(nc, c)
            stage_aggregate(nc, c, "L0", NCH, a["x"], c.rec0, SW, c.tiles_src, 0, weighted=True)
            linear_buffers(c, sb)
            c.XR = sb("XR", [P, T * D])[:, :]
            stage_transpose_weight(nc, c, a["L0_gnn_weight"])
            stage_linear(nc, c, "L0lin", [c.ACC], [(
                [1], lambda link, t, ps, o: nc.vector.tensor_tensor(tile_of(c.XR, t), ps, tile_of(c.X, t), ALU.add), 0)])
            stage_norm(nc, c, "L0norm", c.XR, c.X, store=table_res)

        with ExitStack() as scope:
            sb = allocator(scope)
            c.XRh, c.XRl = sb("XRh", [P, T * D], F32R)[:, :], sb("XRl", [P, T * D], F32R)[:, :]
            c.parts = sb("parts", [P, C1 * AW])
            stage_split_attributes(nc, c)
            for k in range(3):
                attention_round(nc, c, scope, allocator, a, k, table_att)
        s_res = c.sem("L1_residual_in")
        with nc.Block() as block:
            @block.sync
            def _(sp):
                sp.dma_start(c.ACC.rearrange("p (t d) -> p t d", t=T), table_res.rearrange("(t p) d -> p t d", p=P))\
                  .then_inc(s_res, 16)

            @block.vector
            def _(dve):
                dve.wait_ge(s_res, 16)
                nc.vector.tensor_tensor(c.X[:, :], c.X[:, :], c.ACC[:, :], ALU.add)
        stage_norm(nc, c, "L1norm", c.X, c.X)

        def conv1(link, t, ps, o):
            dis = col(c.dis, t)
            link(nc.vector.scalar_tensor_tensor(c.S[:, 0, :], ps, dis, c.row0[:, :], ALU.mult, ALU.add))
            return nc.vector.tensor_scalar(o[:, 0:D], c.S[:, 0, :], 0.0, dis, ALU.max, ALU.mult)

        def conv2(link, t, ps, o):
            link(nc.vector.scalar_tensor_tensor(c.S[:, 0, :], ps, col(c.dis, t), c.row0[:, :], ALU.mult, ALU.add))
            return nc.vector.tensor_tensor(tile_of(c.XR, t), c.S[:, 0, :], tile_of(c.X, t), ALU.add)
        with ExitStack() as scope:
            sb = allocator(scope)
            linear_buffers(c, sb)
            c.XR = sb("XR", [P, T * D])[:, :]
            stage_scaled_table(nc, c, table)
            stage_aggregate(nc, c, "L2a", C1, table, c.rec, HW, c.tiles_dst, 0, weighted=False)
            stage_linear(nc, c, "L2alin", [c.ACC], [([0], conv1, 1)], weights=[(a["L2_gnn_W1"], 0)],
                         rows=[(c.row0[:, :], a["L2_gnn_b1"])], table=table)
            stage_aggregate(nc, c, "L2b", C1, table, c.rec, HW, c.tiles_dst, 0, weighted=False)
            stage_linear(nc, c, "L2blin", [c.ACC], [([0], conv2, 1)], weights=[(a["L2_gnn_W2"], 0)],
                         rows=[(c.row0[:, :], a["L2_gnn_b2"])])
            stage_norm(nc, c, "L2norm", c.XR, c.X, store=table_res)

        with ExitStack() as scope:
            sb = allocator(scope)
            c.XRh, c.XRl = sb("XRh", [P, T * D], F32R)[:, :], sb("XRl", [P, T * D], F32R)[:, :]
            with ExitStack() as inner:
                linear_buffers(c, allocator(inner))

                def right(link, t, ps, o):
                    link(nc.vector.tensor_scalar(tile_of(c.XRh, t), ps, 0.0, None, ALU.add))
                    return nc.vector.tensor_tensor(tile_of(c.XRl, t), ps, tile_of(c.XRh, t), ALU.subtract)
                stage_linear(nc, c, "L3lin", [c.X], [
                    ([0], lambda link, t, ps, o: nc.vector.tensor_tensor(o[:, 0:D], ps, c.row0[:, :], ALU.add), 0),
                    ([1], right, 1)],
                    weights=[(a["L3_gnn_W1"][0:D, :], 0), (a["L3_gnn_W1"][D:2 * D, :], 1)],
                    rows=[(c.row0[:, :], a["L3_gnn_b1"])], table=table)
            with ExitStack() as inner:
                sb = allocator(inner)
                c.S, c.C1, c.Q, c.H, c.Q2, c.M = (c.X[:, n * 2 * D:(n + 1) * 2 * D].rearrange("p (b d) -> p b d", b=2)
                                                  for n in range(6))
                c.C2, c.hotm = c.X[:, 12 * D:13 * D], sb("hotm", [P, 2, P])
                c.hTh, c.hTl = sb("hTh", [P, 2, D], F32R), sb("hTl", [P, 2, D], F32R)
                c.W2h, c.W2l = sb("W2h", [P, KD * D], F32R), sb("W2l", [P, KD * D], F32R)
                c.W1ch, c.W1cl = sb("W1ch", [2 * EA, D], F32R), sb("W1cl", [EA, D], F32R)
                c.b2h, c.b2l, c.one_row = sb("b2h", [1, D], F32R), sb("b2l", [1, D], F32R), sb("one_row", [1, P], F32R)
                c.oT, c.eT2, c.ea = sb("oT", [P, 2, P], F32R), sb("eT2", [2 * EA, 2, P], F32R), sb("ea", [P, U, EA])
                stage_messages(nc, c, table, a["L3_gnn_W1"][2 * D:2 * D + EA, :], a["L3_gnn_W2"], a["L3_gnn_b2"])
            stage_nodes_back(nc, c, table_res)
        with ExitStack() as scope:
            sb = allocator(scope)
            linear_buffers(c, sb)
            c.XR = sb("XR", [P, T * D])[:, :]
            stage_linear(nc, c, "L3u", [c.X, c.ACC], [
                ([0, 1], lambda link, t, ps, o: nc.vector.tensor_tensor(tile_of(c.XR, t), ps, c.row0[:, :], ALU.add), 0)],
                weights=[(a["L3_gnn_W3"][0:D, :], 0), (a["L3_gnn_W3"][D:2 * D, :], 1)],
                rows=[(c.row0[:, :], a["L3_gnn_b3"])])
            stage_mish(nc, c, c.XR)

            def close(link, t, ps, o):
                link(nc.vector.tensor_tensor(c.S[:, 0, :], ps, c.row0[:, :], ALU.add))
                return nc.vector.tensor_tensor(tile_of(c.ACC, t), c.S[:, 0, :], tile_of(c.X, t), ALU.add)
            stage_linear(nc, c, "L3out", [c.XR], [([0], close, 1)], weights=[(a["L3_gnn_W4"], 0)],
                         rows=[(c.row0[:, :], a["L3_gnn_b4"]), (c.row1[:, :], a["L3_gnn_gamma"]),
                               (c.row2[:, :], a["L3_gnn_beta"])])
            stage_norm(nc, c, "L3norm", c.ACC, c.XR, gamma=c.row1[:, :], beta=c.row2[:, :], residual=c.X)
            stage_norm(nc, c, "outnorm", c.XR, c.ACC, store=out)


def linear_buffers(c, sb):
    c.W = sb("W", [P, 2, KD * D])
    c.row0, c.row1, c.row2 = (sb(f"row{n}", [P, D]) for n in range(3))
    c.xs, c.xT, c.out = sb("xs", [P, 2, D]), sb("xT", [P, 2, D]), sb("out", [P, 2, TW])
    c.S, c.Q = sb("S", [P, 2, D]), sb("Q", [P, 2, D])


def attention_round(nc, c, scope, allocator, a, k, table):
    n = f"L1_{k}"
    wl, wr, we = a["L1_gnn_Wl"][k], a["L1_gnn_Wr"][k], a["L1_gnn_We"][k]

    def left(link, t, ps, o):
        link(nc.vector.tensor_tensor(o[:, 0:D], ps, c.row0[:, :], ALU.add))
        return nc.vector.tensor_tensor_reduce(out=c.S[:, 0, :], in0=o[:, 0:D], in1=c.row2[:, :], scale=SLOPE,
                                              scalar=0.0, op0=ALU.mult, op1=ALU.add, accum_out=o[:, D:D + 1])

    def right(link, t, ps, o):
        r = c.S[:, 1, :]
        link(nc.vector.tensor_tensor(r, ps, c.row1[:, :], ALU.add))
        ar = c.MA[:, 2 * t + 1:2 * t + 2] if isinstance(t, int) else c.MA[:, bass.ds(2 * t + 1, 1)]
        nc.vector.scalar_tensor_tensor(c.Q[:, 1, :], r, SLOPE, c.row2[:, :], ALU.mult, ALU.mult,
                                       accum_out=c.cvec[:, 0:1])
        link(nc.vector.tensor_scalar(tile_of(c.XRh, t), r, 0.0, None, ALU.add))
        nc.vector.tensor_tensor(tile_of(c.XRl, t), r, tile_of(c.XRh, t), ALU.subtract)
        return nc.vector.tensor_scalar(ar, c.cvec[:, 0:1], 0.0, None, ALU.add)
    with ExitStack() as inner:
        linear_buffers(c, allocator(inner))
        s_pad = c.sem(f"{n}_pad")
        with nc.Block() as block:
            @block.gpsimd
            def _(pool):
                pool.memset(c.out[:, :, D:TW], 0.0).then_inc(s_pad, 1)
        stage_linear(nc, c, n + "lin", [c.X], [([0], left, 1), ([1], right, 2)], weights=[(wl, 0), (wr, 1)],
                     rows=[(c.row0[:, :], a["L1_gnn_bl"][k]), (c.row1[:, :], a["L1_gnn_br"][k]),
                           (c.row2[:, :], a["L1_gnn_att"][k])], table=table)
    with ExitStack() as inner:
        sb = allocator(inner)
        c.attB, c.WeB, c.We32, c.WeR = sb("attB", [P, D]), sb("WeB", [P, 2 * D]), sb("We32", [6, D]), sb("WeR", [6, D], F32R)
        c.S, c.R = sb("S", [P, D]), sb("R", [P, D])
        c.oT, c.eT = sb("oT", [P, 2, P], F32R), sb("eT", [6, 2, P], F32R)
        c.local, c.attr = sb("local", [P, U]), sb("attr", [P, U, AW])
        c.hot4, c.far = sb("hot4", [P, 4, P]), sb("far", [P, 4, P])
        c.masked, c.PT, c.Wt = (sb(m, [P, 2, P]) for m in ("masked", "PT", "Wt"))
        c.dot, c.lg, c.cmax, c.mnew = sb("dot", [P, 2]), sb("lg", [P, 4]), sb("cmax", [P, 2]), sb("mnew", [P, 2])
        c.scale, c.rowsum, c.diff = (sb(m, [P, 4]) for m in ("scale", "rowsum", "diff"))
        stage_attention_edges(nc, c, n, table, [(c.attB[:, :], a["L1_gnn_att"][k]),
                                                (c.WeB[:, :], we.rearrange("a d -> (a d)"))], we)
    with ExitStack() as inner:
        linear_buffers(c, allocator(inner))
        stage_rows(nc, c, n + "affine", [(c.row2[:, :], a["L1_gnn_b_out"][k]), (c.row0[:, :], a["L1_gnn_gamma"][k]),
                              (c.row1[:, :], a["L1_gnn_beta"][k])])
        stage_attention_close(nc, c, n + "close")
        stage_norm(nc, c, n + "norm", c.ACC, c.X, gamma=c.row0[:, :], beta=c.row1[:, :], relu=True)


_INS = ['x', 'src', 'dst', 'edge_attr_2', 'edge_attr_64', 'edge_weight', 'L0_gnn_weight', 'L1_gnn_Wl', 'L1_gnn_bl',
        'L1_gnn_Wr', 'L1_gnn_br', 'L1_gnn_We', 'L1_gnn_att', 'L1_gnn_b_out', 'L1_gnn_gamma', 'L1_gnn_beta',
        'L2_gnn_W1', 'L2_gnn_b1', 'L2_gnn_W2', 'L2_gnn_b2', 'L3_gnn_W1', 'L3_gnn_b1', 'L3_gnn_W2', 'L3_gnn_b2',
        'L3_gnn_W3', 'L3_gnn_b3', 'L3_gnn_W4', 'L3_gnn_b4', 'L3_gnn_gamma', 'L3_gnn_beta']


def kernel(**inputs):
    import numpy as _np
    import concourse.bacc as _bacc
    from concourse import mybir as _mybir
    from concourse.bass_utils import run_bass_kernel_spmd as _run

    nc = _bacc.Bacc("TRN2", target_bir_lowering=False, num_devices=1)
    arrays, args = {}, {}
    for name in _INS:
        v = _np.ascontiguousarray(inputs[name])
        arrays[f"in_{name}_dram"] = v
        args[name] = nc.dram_tensor(f"in_{name}_dram", v.shape, _mybir.dt.from_np(v.dtype), kind="ExternalInput").ap()
    out = nc.dram_tensor("out_0_dram", (N, D), F32, kind="ExternalOutput").ap()
    gnn_stack(nc, args, out)
    r = _run(nc, [arrays], core_ids=[0])
    return r.results[0]["out_0_dram"]
```

```python
from contextlib import ExitStack

import concourse.bass as bass
from concourse import mybir

F32 = mybir.dt.float32
I32 = mybir.dt.int32
F32R = mybir.dt.float32r
ALU = mybir.AluOpType
ACT = mybir.ActivationFunctionType
AX = mybir.AxisListType

P = 128
N, D, E = 2048, 512, 32768
T = N // P
KD = D // P
EC = E // P
EA = 64
NCH = 272
C1 = T + NCH
HW = 5
RW = HW + EA
SW = 4
TW = 520
AW = 7
SLOPE = 0.2
EPS = 1e-5
CLAMP = 20.0
FAR = 1e30
U = 8
assert NCH * P >= E + T * (P - 1) and NCH % U == 0 and C1 % U == 0


class Chip:
    pass



def wait(eng, sem, value):
    if isinstance(value, int) and value <= 0:
        return
    eng.wait_ge(sem, value)


def wait_apart(eng, sem, value, passed):
    if isinstance(value, int) and value <= 0:
        return
    eng.wait_ge(sem, value)
    eng.sem_inc(passed, 1)


def back(k, u, lag):
    return k * U + (u - lag), (u - lag) % U, (k if u >= lag else k - 1)


def live(i, count):
    return not isinstance(i, int) or 0 <= i < count


def run_steps(eng, count, step, lag=0):
    peeled = max(1, -(-lag // U))
    for k in range(peeled):
        for u in range(U):
            step(k, u)
    with eng.Fori(peeled, count // U) as k:
        for u in range(U):
            step(k, u)
    for u in range(lag):
        step(count // U, u)


def tile_of(buf, t):
    return buf[:, t * D:(t + 1) * D] if isinstance(t, int) else buf[:, bass.ds(t * D, D)]


def col(buf, i, n=1):
    return buf[:, i * n:(i + 1) * n] if isinstance(i, int) else buf[:, bass.ds(i * n, n)]


def end_stage(nc, c):
    nc.clear_and_free_semaphores(c.sems)
    nc.all_engine_barrier()
    c.sems.clear()


def stage(build):
    def built(nc, c, *args, **named):
        build(nc, c, *args, **named)
        end_stage(nc, c)
    return built



@stage
def stage_constants(nc, c):
    s_low = c.sem("const_low")
    s_fill, s_shape = c.sem("const_filled"), c.sem("const_shaped")
    with nc.Block() as block:
        @block.gpsimd
        def _(pool):
            pool.iota(c.iota_i[:, :], pattern=[[1, P]], base=0, channel_multiplier=0).then_inc(s_fill, 1)
            pool.iota(c.node_i[:, :], pattern=[[P, T]], base=0, channel_multiplier=1).then_inc(s_fill, 1)
            pool.iota(c.chunk_i[:, :], pattern=[[1, NCH]], base=0, channel_multiplier=0).then_inc(s_fill, 1)
            pool.iota(c.tile_i[:, :], pattern=[[1, T]], base=0, channel_multiplier=0).then_inc(s_fill, 1)
            pool.iota(c.lane_i[:, :], pattern=[[0, 1]], base=0, channel_multiplier=1).then_inc(s_fill, 1)
            pool.memset(c.ones[:, :], 1.0).then_inc(s_fill, 1)
            pool.memset(c.ident[:, :], 0.0).then_inc(s_fill, 1)
            pool.wait_ge(s_fill, 7)
            pool.affine_select(out=c.ident[:, :], in_=c.ident[:, :], compare_op=ALU.not_equal, fill=1.0, base=0,
                               pattern=[[-1, P]], channel_multiplier=1).then_inc(s_shape, 1)
            pool.affine_select(out=c.upper[:, :], in_=c.ones[:, :], compare_op=ALU.is_gt, fill=0.0, base=0,
                               pattern=[[1, P]], channel_multiplier=-1).then_inc(s_shape, 1)

        @block.vector
        def _(dve):
            dve.wait_ge(s_fill, 7)
            nc.vector.tensor_copy(c.iota[:, :], c.iota_i[:, :])
            nc.vector.tensor_copy(c.chunk_f[:, :], c.chunk_i[:, :])
            nc.vector.tensor_copy(c.lane_f[:, :], c.lane_i[:, :]).then_inc(s_low, 1)
            dve.wait_ge(s_low, 1)
            nc.vector.memset(c.eps[:, :], EPS)
            nc.vector.tensor_scalar(c.low2[:, :], c.lane_f[:, :], 4.0, None, ALU.is_lt).then_inc(s_low, 1)
            dve.wait_ge(s_low, 2)
            nc.vector.scalar_tensor_tensor(c.low[:, :], c.lane_f[:, :], 2.0, c.low2[:, :], ALU.is_ge, ALU.mult).then_inc(s_low, 1)
            dve.wait_ge(s_low, 3)
            nc.vector.tensor_scalar(c.sign[:, :], c.low[:, :], -2.0, 1.0, ALU.mult, ALU.add)
            nc.vector.tensor_copy(c.tiles_dst[0:1, 0:T], c.tile_i[0:1, :])


def bin_edges(nc, c, dve, chain, key, rec_local, rows, ends_sem, totals_sem, tiles_out, uses):
    def link(ins):
        chain[0] += 1
        ins.then_inc(c.s_chain, 1)
        dve.wait_ge(c.s_chain, chain[0])

    link(nc.vector.tensor_scalar(c.tmp_i[:, 0:EC], key, 7, None, ALU.logical_shift_right))
    link(nc.vector.tensor_copy(c.bin_f[:, :], c.tmp_i[:, 0:EC]))
    link(nc.vector.tensor_scalar(c.tmp_i[:, 0:EC], key, P - 1, None, ALU.bitwise_and))
    nc.vector.tensor_copy(rec_local, c.tmp_i[:, 0:EC])
    for b in range(T):
        last = nc.vector.tensor_scalar(c.member[:, b * EC:(b + 1) * EC], c.bin_f[:, :], float(b), None, ALU.is_equal)
    link(last)
    for b in range(T):
        last = nc.vector.tensor_tensor_scan(c.running[:, b * EC:(b + 1) * EC], c.edge_ones[:, :],
                                            c.member[:, b * EC:(b + 1) * EC], 0.0, ALU.mult, ALU.add)
    link(last)
    counts = c.running[:, :].rearrange("p (b j) -> p b j", b=T)[:, :, EC - 1]
    nc.vector.tensor_copy(c.counts[:, :], counts).then_inc(ends_sem, 1)
    dve.wait_ge(totals_sem, uses)
    before, total = c.ps[:, 0, 0:T], c.ps[:, 1, 0:T]
    link(nc.vector.tensor_scalar(c.small[:, 0:T], total, float(P - 1), None, ALU.add))
    link(nc.vector.tensor_copy(c.small_i[:, 0:T], c.small[:, 0:T]))
    link(nc.vector.tensor_scalar(c.small_i[:, T:2 * T], c.small_i[:, 0:T], 7, None, ALU.logical_shift_right))
    link(nc.vector.tensor_copy(c.small[:, T:2 * T], c.small_i[:, T:2 * T]))
    link(nc.vector.tensor_tensor_scan(c.small[:, 2 * T:3 * T], c.ones[:, 0:T], c.small[:, T:2 * T], 0.0,
                                      ALU.mult, ALU.add))
    link(nc.vector.tensor_tensor(c.small[:, 3 * T:4 * T], c.small[:, 2 * T:3 * T], c.small[:, T:2 * T], ALU.subtract))
    link(nc.vector.tensor_scalar(c.small[:, 3 * T:4 * T], c.small[:, 3 * T:4 * T], float(P), -1.0, ALU.mult, ALU.add))
    link(nc.vector.tensor_tensor(c.small[:, 3 * T:4 * T], c.small[:, 3 * T:4 * T], before, ALU.add))
    for b in range(T):
        run = c.running[:, b * EC:(b + 1) * EC]
        last = nc.vector.scalar_tensor_tensor(run, run, c.small[:, 3 * T + b:3 * T + b + 1],
                                              c.member[:, b * EC:(b + 1) * EC], ALU.add, ALU.mult)
    link(last)
    link(nc.vector.tensor_reduce(c.bin_f[:, :], c.running[:, :].rearrange("p (b j) -> p j b", b=T), AX.X, ALU.add))
    link(nc.vector.tensor_copy(c.tmp_i[:, 0:EC], c.bin_f[:, :]))
    nc.vector.tensor_scalar(c.tmp_i[:, EC:2 * EC], c.tmp_i[:, 0:EC], 7, None, ALU.logical_shift_right)
    link(nc.vector.tensor_scalar(c.tmp_i[:, 2 * EC:3 * EC], c.tmp_i[:, 0:EC], P - 1, None, ALU.bitwise_and))
    nc.vector.tensor_copy(c.bin_f[:, :], c.tmp_i[:, EC:2 * EC])
    link(nc.vector.tensor_copy(c.bin_g[:, :], c.tmp_i[:, 2 * EC:3 * EC]))
    link(nc.vector.scalar_tensor_tensor(c.bin_g[:, :], c.bin_g[:, :], float(NCH), c.bin_f[:, :], ALU.mult, ALU.add))
    link(nc.vector.tensor_copy(rows, c.bin_g[:, :]))
    link(nc.vector.memset(c.tile_f[0:1, :], 0.0))
    for b in range(T - 1):
        link(nc.vector.scalar_tensor_tensor(c.tile_f[0:1, :], c.chunk_f[0:1, :], c.small[0:1, 2 * T + b:2 * T + b + 1],
                                            c.tile_f[0:1, :], ALU.is_ge, ALU.add))
    link(nc.vector.tensor_copy(tiles_out, c.tile_f[0:1, :]))


@stage
def stage_bin(nc, c, src, dst, edge_attr_2, edge_attr_64, edge_weight):
    s_key, s_attr, s_wide, s_pads = (c.sem(f"bin_{n}") for n in ("keys_in", "attrs_in", "wide_in", "pads_out"))
    s_cnt, s_tot, s_pad = (c.sem(f"bin_{n}") for n in ("counts", "totals", "pad_rows"))
    c.chain, c.s_chain = [0], c.sem("bin_chain")
    by_p = lambda a: a.rearrange("(p j) -> p j", p=P)
    with nc.Block() as block:
        @block.sync
        def _(sp):
            sp.dma_start(c.key_src[:, :], by_p(src)).then_inc(s_key, 16)
            sp.dma_start(c.key_dst[:, :], by_p(dst)).then_inc(s_key, 16)
            sp.dma_start(c.attr2[:, :], edge_attr_2.rearrange("(p j) a -> p (j a)", p=P)).then_inc(s_attr, 16)
            sp.dma_start(c.weight[:, :], by_p(edge_weight)).then_inc(s_attr, 16)
            sp.dma_start(c.recs3[:, :, HW:RW], edge_attr_64.rearrange("(p j) a -> p j a", p=P)).then_inc(s_wide, 16)
            sp.wait_ge(s_pad, 2)
            for n in range(NCH // c.PADS):
                sp.dma_start(c.by_dst.rearrange("(p c) w -> p (c w)", p=P)[:, n * c.PADS * RW:(n + 1) * c.PADS * RW],
                             c.pads[:, :]).then_inc(s_pads, 16)
            sp.dma_start(c.by_src.rearrange("(p c) w -> p (c w)", p=P), c.pads0[:, :]).then_inc(s_pads, 16)
            sp.wait_ge(s_pads, 16 * (NCH // c.PADS + 1))
            sp.wait_ge(s_wide, 16)

        @block.gpsimd
        def _(pool):
            s_zero = c.sem("bin_zeroed")
            pool.memset(c.pads[:, :], 0.0).then_inc(s_zero, 1)
            pool.memset(c.pads0[:, :], 0.0).then_inc(s_zero, 1)
            pool.wait_ge(s_zero, 2)
            pool.memset(c.pads[:, :].rearrange("p (c w) -> p c w", w=RW)[:, :, 1], -1.0).then_inc(s_pad, 1)
            pool.memset(c.pads0[:, :].rearrange("p (c w) -> p c w", w=SW)[:, :, 1], -1.0).then_inc(s_pad, 1)

        @block.tensor
        def _(pe):
            for n in range(2):
                pe.wait_ge(s_cnt, n + 1)
                nc.tensor.matmul(c.ps[:, 0, 0:T], c.upper[:, :], c.counts[:, :], start=True, stop=True)
                nc.tensor.matmul(c.ps[:, 1, 0:T], c.ones[:, :], c.counts[:, :], start=True, stop=True).then_inc(s_tot, 1)

        @block.vector
        def _(dve):
            chain = c.chain
            nc.vector.memset(c.edge_ones[:, :], 1.0)
            nc.vector.memset(c.recs3[:, :, 4], 1.0)
            nc.vector.memset(c.recs0_3[:, :, 3], 0.0)
            dve.wait_ge(s_key, 32)
            nc.vector.tensor_copy(c.recs3_i[:, :, 0], c.key_src[:, :])
            nc.vector.tensor_copy(c.recs0_3i[:, :, 0], c.key_dst[:, :])
            bin_edges(nc, c, dve, chain, c.key_dst[:, :], c.recs3[:, :, 1], c.rows_dst[:, :], s_cnt, s_tot,
                      c.tiles_dst[0:1, T:C1], 1)
            bin_edges(nc, c, dve, chain, c.key_src[:, :], c.recs0_3[:, :, 1], c.rows_src[:, :], s_cnt, s_tot,
                      c.tiles_src[0:1, :], 2)
            dve.wait_ge(s_attr, 32)
            nc.vector.tensor_copy(c.recs3[:, :, 2:4], c.attr2[:, :].rearrange("p (j a) -> p j a", a=2))
            nc.vector.tensor_copy(c.recs0_3[:, :, 2], c.weight[:, :])


@stage
def stage_scatter(nc, c):
    s_rec, s_rec0 = c.sem("scatter_staged_dst"), c.sem("scatter_staged_src")
    s_passed, s_idx = c.sem("scatter_wait_passed"), c.sem("scatter_rows_copied")
    s_out = [c.sem(f"scatter_dst_out{u}") for u in range(U)]
    s_out0 = [c.sem(f"scatter_src_out{u}") for u in range(U)]
    with nc.Block() as block:
        @block.scalar
        def _(act):
            def step(k, u):
                i = k * U + u
                wait_apart(act, s_out[u], 16 * k, s_passed)
                nc.scalar.activation(c.stage[:, u * RW:(u + 1) * RW], col(c.recs, i, RW), ACT.Copy).then_inc(s_rec, 1)
                wait_apart(act, s_out0[u], 16 * k, s_passed)
                nc.scalar.activation(c.stage0[:, u * SW:(u + 1) * SW], col(c.recs0, i, SW), ACT.Copy).then_inc(s_rec0, 1)
            run_steps(act, EC, step)

        @block.gpsimd
        def _(pool):
            half = U // 2

            def step(k, u):
                i = k * U + u
                if u % half == 0:
                    h = u // half
                    for v in range(u, u + half):
                        wait_apart(pool, s_out[v], 16 * k, s_passed)
                        wait_apart(pool, s_out0[v], 16 * k, s_passed)
                    n = k * 2 + h
                    nc.gpsimd.tensor_copy(c.idx[:, h * half:(h + 1) * half], col(c.rows_dst, n, half)).then_inc(s_idx, 1)
                    nc.gpsimd.tensor_copy(c.idx0[:, h * half:(h + 1) * half], col(c.rows_src, n, half)).then_inc(s_idx, 1)
                    wait_apart(pool, s_idx, 2 * n + 2, s_passed)
                wait_apart(pool, s_rec, i + 1, s_passed)
                pool.indirect_dma_start(out=c.by_dst, out_offset=bass.IndirectOffsetOnAxis(ap=c.idx[:, u:u + 1], axis=0),
                                        in_=c.stage[:, u * RW:(u + 1) * RW], in_offset=None).then_inc(s_out[u], 16)
                wait_apart(pool, s_rec0, i + 1, s_passed)
                pool.indirect_dma_start(out=c.by_src, out_offset=bass.IndirectOffsetOnAxis(ap=c.idx0[:, u:u + 1], axis=0),
                                        in_=c.stage0[:, u * SW:(u + 1) * SW], in_offset=None).then_inc(s_out0[u], 16)
            run_steps(pool, EC, step)
            for u in range(U):
                pool.wait_ge(s_out[u], 16 * (EC // U))
                pool.wait_ge(s_out0[u], 16 * (EC // U))


@stage
def stage_heads(nc, c):
    s_all, s_head0 = c.sem("heads_rows_in"), c.sem("heads_src_in")
    with nc.Block() as block:
        @block.sync
        def _(sp):
            sp.dma_start(c.wide[:, :], c.by_dst.rearrange("(p c) w -> p (c w)", p=P)).then_inc(s_all, 16)
            sp.dma_start(c.rec0[:, :], c.by_src.rearrange("(p c) w -> p (c w)", p=P)).then_inc(s_head0, 16)
            sp.wait_ge(s_head0, 16)

        @block.vector
        def _(dve):
            dve.wait_ge(s_all, 16)
            wide = c.wide[:, :].rearrange("p (c w) -> p c w", w=RW)
            nc.vector.tensor_copy(c.rec3[:, T:C1, 1:HW], wide[:, :, 1:HW])
            nc.vector.tensor_copy(c.rec3_i[:, T:C1, 0], wide.bitcast(I32)[:, :, 0])


@stage
def stage_degrees(nc, c):
    c.chain, c.s_chain = [0], c.sem("degree_chain")
    s_sq, s_rt = c.sem("degree_plus_one"), c.sem("degree_root")
    with nc.Block() as block:
        @block.vector
        def _(dve):
            def link(ins):
                c.chain[0] += 1
                ins.then_inc(c.s_chain, 1)
                dve.wait_ge(c.s_chain, c.chain[0])
            deg = c.deg[:, :].rearrange("p (t w) -> p t w", w=3)
            nc.vector.tensor_scalar(c.deg1[:, :], deg[:, :, 2], 1.0, None, ALU.add).then_inc(s_sq, 1)
            link(nc.vector.tensor_scalar(c.dis[:, :], deg[:, :, 2], 1.0, None, ALU.max))
            link(nc.vector.reciprocal(c.small[:, 0:T], c.dis[:, :]))
            for a in range(2):
                nc.vector.tensor_tensor(c.rec3[:, 0:T, 2 + a], deg[:, :, a], c.small[:, 0:T], ALU.mult)
            nc.vector.tensor_copy(c.rec3_i[:, 0:T, 0], c.node_i[:, :])
            nc.vector.tensor_scalar(c.rec3[:, 0:T, 1], c.ones[:, 0:T], c.lane_f[:, :], None, ALU.mult)
            nc.vector.tensor_copy(c.rec3[:, 0:T, 4], c.ones[:, 0:T])
            dve.wait_ge(s_rt, 1)
            nc.vector.reciprocal(c.dis[:, :], c.root[:, 0:T])

        @block.scalar
        def _(act):
            act.wait_ge(s_sq, 1)
            nc.scalar.activation(c.root[:, 0:T], c.deg1[:, :], ACT.Sqrt).then_inc(s_rt, 1)



def load_weights(sp, c, sem, w, slot):
    sp.dma_start(c.W[:, slot, :].rearrange("p (k o) -> p k o", k=KD), w.rearrange("(k p) o -> p k o", p=P)).then_inc(sem, 16)


@stage
def stage_transpose_weight(nc, c, w):
    s_in, s_t, s_c = c.sem("wt_in"), c.sem("wt_turned"), c.sem("wt_copied")
    with nc.Block() as block:
        @block.sync
        def _(sp):
            load_weights(sp, c, s_in, w, 0)

        @block.tensor
        def _(pe):
            pe.wait_ge(s_in, 16)
            for k in range(KD):
                for o in range(KD):
                    last = nc.tensor.transpose(c.ps[:, k, o * P:(o + 1) * P], c.W[:, 0, o * D + k * P:o * D + (k + 1) * P],
                                               c.ident[:, :])
                last.then_inc(s_t, 1)

        @block.vector
        def _(dve):
            for k in range(KD):
                dve.wait_ge(s_t, k + 1)
                nc.vector.tensor_copy(c.W[:, 1, k * D:(k + 1) * D], c.ps[:, k, :])


@stage
def stage_linear(nc, c, name, sources, outputs, weights=(), rows=(), table=None):
    S, O = len(sources), len(outputs)
    s_w, s_in, s_turn, s_even, s_prod, s_fin, s_store = (
        c.sem(f"{name}_{n}") for n in ("weights_in", "staged", "turned", "turned_copied", "product", "finished", "stored0"))
    s_store = [s_store, c.sem(f"{name}_stored1")]
    with nc.Block() as block:
        @block.sync
        def _(sp):
            for w, slot in weights:
                load_weights(sp, c, s_w, w, slot)
            for buf, a in rows:
                sp.dma_start(buf, a.partition_broadcast(P)).then_inc(s_w, 16)
            if table is not None:
                width = table.shape[1]

                def store(k, u):
                    t = k * 2 + u
                    wait(sp, s_fin, O * t + 1)
                    row = table[t * P:(t + 1) * P, :] if isinstance(t, int) else table[bass.ds(t * P, P), :]
                    sp.dma_start(row, c.out[:, u, 0:width]).then_inc(s_store[u], 16)
                with sp.Fori(0, T // 2) as k:
                    for u in range(2):
                        store(k, u)
                for u in range(2):
                    sp.wait_ge(s_store[u], 16 * (T // 2))

        @block.scalar
        def _(act):
            def stage(t, s, slot):
                nc.scalar.activation(c.xs[:, slot, :], tile_of(sources[s], t), ACT.Copy).then_inc(s_in, 1)

            def turn(q, slot, t, o_done):
                wait(act, s_turn, q + 1)
                wait(act, s_prod, o_done)
                nc.scalar.activation(c.xT[:, slot, :], c.ps[:, slot, :], ACT.Copy).then_inc(s_even, 1)

            def pair(k, first=False):
                for u in range(2):
                    t = k * 2 + u
                    for s in range(S):
                        slot = (u * S + s) % 2
                        q = t * S + s
                        turn(q, slot, t, 0 if first and q < 2 else O * ((q - 2) // S + 1) if first else
                             (O * (t - 1) if S == 1 else O * t))
                        nq = u * S + s + 2
                        if isinstance(k, int) and k == T // 2 - 1 and nq >= 2 * S:
                            continue
                        stage(k * 2 + nq // S, nq % S, slot)
            stage(0, 0, 0)
            stage(1 // S, 1 % S, 1)
            pair(0, first=True)
            with act.Fori(1, T // 2 - 1) as k:
                pair(k)
            pair(T // 2 - 1)

        @block.tensor
        def _(pe):
            pe.wait_ge(s_w, 16 * (len(weights) + len(rows))) if weights or rows else None

            def turn(q, slot):
                wait(pe, s_in, q + 1)
                wait(pe, s_even, q - 1)
                for b in range(KD):
                    last = nc.tensor.transpose(c.ps[:, slot, b * P:(b + 1) * P], c.xs[:, slot, b * P:(b + 1) * P],
                                               c.ident[:, :])
                last.then_inc(s_turn, 1)

            def multiply(t, u, s, slot):
                wait(pe, s_even, t * S + s + 1)
                for o in range(O):
                    if s == 0:
                        wait(pe, s_fin, O * (t - 2) + o + 1)
                    for b in range(KD):
                        last = nc.tensor.matmul(c.ps[:, 2 + 2 * o + u, :], c.xT[:, slot, b * P:(b + 1) * P],
                                                c.W[:, outputs[o][0][s], b * D:(b + 1) * D],
                                                start=(s == 0 and b == 0), stop=(s == S - 1 and b == KD - 1))
                    if s == S - 1:
                        last.then_inc(s_prod, 1)

            def pair(k, last_pair):
                for u in range(2):
                    t = k * 2 + u
                    for s in range(S):
                        q = t * S + s
                        if not (last_pair and u * S + s == 2 * S - 1):
                            turn(q + 1, (u * S + s + 1) % 2)
                        multiply(t, u, s, (u * S + s) % 2)
            turn(0, 0)
            pair(0, False)
            with pe.Fori(1, T // 2 - 1) as k:
                pair(k, False)
            pair(T // 2 - 1, True)

        @block.vector
        def _(dve):
            s_link = c.sem(f"{name}_link")
            if rows:
                dve.wait_ge(s_w, 16 * (len(weights) + len(rows)))

            def step(k, u):
                t = k * 2 + u
                wait(dve, s_fin, O * t)
                count = [0]
                per_tile = outputs_links(outputs)

                def link(ins):
                    count[0] += 1
                    ins.then_inc(s_link, 1)
                    wait(dve, s_link, t * per_tile + count[0])
                for o in range(O):
                    wait(dve, s_prod, O * t + o + 1)
                    if o == 0 and table is not None:
                        wait(dve, s_store[u], 16 * k)
                    outputs[o][1](link, t, c.ps[:, 2 + 2 * o + u, :], c.out[:, u, :]).then_inc(s_fin, 1)
            for u in range(2):
                step(0, u)
            with dve.Fori(1, T // 2) as k:
                for u in range(2):
                    step(k, u)


def outputs_links(outputs):
    return sum(o[2] for o in outputs)


@stage
def stage_rows(nc, c, name, pairs):
    s_in = c.sem(f"{name}_rows_in")
    with nc.Block() as block:
        @block.sync
        def _(sp):
            for buf, a in pairs:
                sp.dma_start(buf, a.partition_broadcast(P)).then_inc(s_in, 16)
            sp.wait_ge(s_in, 16 * len(pairs))


@stage
def stage_norm(nc, c, name, h, out, gamma=None, beta=None, relu=False, residual=None, copy=None, store=None):
    s_stat, s_var, s_root = (c.sem(f"{name}_{n}") for n in ("stats", "variance", "root"))
    s_link, s_out, s_mid, s_aff = (c.sem(f"{name}_{n}") for n in ("link", "out", "scaled", "affine"))
    mv = c.mv[:, :].rearrange("p (t w) -> p t w", w=2)
    full = lambda b: b[:, :].rearrange("p (t d) -> p t d", t=T)
    with nc.Block() as block:
        @block.vector
        def _(dve):
            n = [0]

            def link(ins):
                n[0] += 1
                ins.then_inc(s_link, 1)
                dve.wait_ge(s_link, n[0])
            for t in range(T):
                last = nc.vector.bn_stats(c.st[:, t * 6:(t + 1) * 6], tile_of(h, t))
            link(last)
            for t in range(T):
                last = nc.vector.bn_aggr(c.mv[:, t * 2:(t + 1) * 2], c.st[:, t * 6:(t + 1) * 6])
            last.then_inc(s_var, 1)
            dve.wait_ge(s_root, 1)
            link(nc.vector.reciprocal(c.rstd[:, :], c.root[:, 0:T]))
            mean, rstd = (lambda t: c.mv[:, 2 * t:2 * t + 1]), (lambda t: c.rstd[:, t:t + 1])
            for t in range(T):
                o = tile_of(out, t)
                if gamma is None:
                    last = nc.vector.tensor_scalar(o, tile_of(h, t), mean(t), rstd(t), ALU.subtract, ALU.mult)
                    continue
                nc.vector.scalar_tensor_tensor(o, tile_of(h, t), mean(t), gamma, ALU.subtract, ALU.mult).then_inc(s_mid, 1)
                if t > 0:
                    p = tile_of(out, t - 1)
                    dve.wait_ge(s_mid, t)
                    last = nc.vector.scalar_tensor_tensor(p, p, rstd(t - 1), beta, ALU.mult, ALU.add)
                    if relu:
                        last.then_inc(s_aff, 1)
            if gamma is not None:
                p = tile_of(out, T - 1)
                dve.wait_ge(s_mid, T)
                last = nc.vector.scalar_tensor_tensor(p, p, rstd(T - 1), beta, ALU.mult, ALU.add)
                if relu:
                    last.then_inc(s_aff, 1)
            if residual is not None:
                link(last)
                last = nc.vector.tensor_tensor(out[:, :], out[:, :], residual[:, :], ALU.add)
            if store is not None:
                last.then_inc(s_stat, 1)

        @block.scalar
        def _(act):
            act.wait_ge(s_var, 1)
            nc.scalar.activation(c.root[:, 0:T], mv[:, :, 1], ACT.Sqrt, bias=c.eps[:, :]).then_inc(s_root, 1)
            if relu:
                for t in range(T):
                    act.wait_ge(s_aff, t + 1)
                    nc.scalar.activation(tile_of(out, t), tile_of(out, t), ACT.Relu)

        @block.sync
        def _(sp):
            if store is not None:
                sp.wait_ge(s_stat, 1)
                sp.dma_start(store.rearrange("(t p) d -> p t d", p=P), full(out)).then_inc(s_out, 16)
                sp.wait_ge(s_out, 16)



def gather_rows(nc, c, pool, count, table, width, source, sems, beside_half=None, beside=None):
    half = U // 2

    def step(k, u):
        i = k * U + u
        if u % half == 0:
            h = u // half
            for v in range(u, u + half):
                wait_apart(pool, sems.got[v], 16 * k, sems.passed)
            n = k * 2 + h
            nc.gpsimd.tensor_copy(c.idx[:, h * half:(h + 1) * half], source(n, half)).then_inc(sems.idx, 1)
            if beside_half:
                beside_half(k, u, n)
            wait_apart(pool, sems.idx, n + 1, sems.passed)
        if beside:
            beside(k, u)
        wait_apart(pool, sems.used, i - U + 1, sems.passed)
        pool.indirect_dma_start(out=c.G[:, u, 0:width], out_offset=None, in_=table,
                                in_offset=bass.IndirectOffsetOnAxis(ap=c.idx[:, u:u + 1], axis=0)).then_inc(sems.got[u], 16)
    run_steps(pool, count, step)


def edge_sems(c, name):
    s = Chip()
    s.got = [c.sem(f"{name}_got{u}") for u in range(U)]
    s.idx, s.used, s.passed = c.sem(f"{name}_indices"), c.sem(f"{name}_rows_used"), c.sem(f"{name}_wait_passed")
    return s


class Tiles:
    AHEAD = 8

    def __init__(self, nc, eng, tiles, first, count, lag):
        self.nc, self.eng, self.tiles, self.first, self.count, self.lag, self.held = nc, eng, tiles, first, count, lag, {}

    def of(self, k, u):
        n = self.AHEAD
        if u % n == 0:
            j = k * U + u - self.lag
            live = [v for v in range(n) if not isinstance(j, int) or 0 <= j + v < self.count]
            if live:
                lo, m = self.first + j + live[0], len(live)
                _, values = self.nc.values_load_multi_w_load_instructions(
                    self.tiles[0:1, lo:lo + m] if isinstance(j, int) else self.tiles[0:1, bass.ds(lo, m)],
                    engines=[self.eng.engine], min_val=0, max_val=T - 1,
                    skip_runtime_bounds_check_because="it counts which of the first T - 1 tiles end before a chunk")
                self.held = dict(zip(live, values))
        return self.held.get(u % n)


@stage
def stage_aggregate(nc, c, name, table):
    s = edge_sems(c, name)
    s_hot, s_add, s_zero = (c.sem(f"{name}_{n}") for n in ("onehot", "added", "zeroed"))

    def source(n, half):
        lo = n * half
        return c.rec3_i[:, lo:lo + half, 0] if isinstance(n, int) else c.rec3_i[:, bass.ds(lo, half), 0]
    with nc.Block() as block:
        @block.gpsimd
        def _(pool):
            gather_rows(nc, c, pool, C1, table, D, source, s)

        @block.tensor
        def _(pe):
            def step(k, u):
                i = k * U + u
                wait(pe, s.got[u], 16 * (k + 1))
                wait(pe, s_hot, i + 1)
                wait(pe, s_add, i - 1)
                nc.tensor.matmul(c.ps[:, u % 2, :], c.hot[:, u % 2, :], c.G[:, u, 0:D],
                                 start=True, stop=True).then_inc(s.used, 1)
            run_steps(pe, C1, step)

        @block.vector
        def _(dve):
            nc.vector.memset(c.ACC[:, :], 0.0).then_inc(s_zero, 1)
            dve.wait_ge(s_zero, 1)

            def step(k, u):
                i = k * U + u
                if live(i, C1):
                    wait(dve, s.used, i - 1)
                    nc.vector.tensor_scalar(c.hot[:, u % 2, :], c.iota[:, :], col(c.rec, i, HW)[:, 1:2], None,
                                            ALU.is_equal).then_inc(s_hot, 1)
                j, slot, _ = back(k, u, 1)
                t = tiles.of(k, u)
                if live(j, C1):
                    wait(dve, s.used, j + 1)
                    wait(dve, s_add, j)
                    acc = tile_of(c.ACC, t)
                    nc.vector.tensor_tensor(acc, acc, c.ps[:, slot % 2, :], ALU.add).then_inc(s_add, 1)
            tiles = Tiles(nc, dve, c.tiles_dst, 0, C1, 1)
            run_steps(dve, C1, step, lag=1)


@stage
def stage_first_sums(nc, c, x):
    name = "L0"
    s = edge_sems(c, name)
    s_hot, s_add, s_zero = (c.sem(f"{name}_{n}") for n in ("onehot", "added", "zeroed"))
    s_dhot, s_dsum, s_dadd = (c.sem(f"degree_{n}") for n in ("onehot", "summed", "added"))
    s_x = c.sem("nodes_in")
    rec_i = c.rec0.bitcast(I32).rearrange("p (c w) -> p c w", w=SW)
    B_D = 2

    def source(n, half):
        lo = n * half
        return rec_i[:, lo:lo + half, 0] if isinstance(n, int) else rec_i[:, bass.ds(lo, half), 0]
    with nc.Block() as block:
        @block.sync
        def _(sp):
            sp.dma_start(c.X.rearrange("p (t d) -> p t d", t=T), x.rearrange("(t p) d -> p t d", p=P)).then_inc(s_x, 16)
            sp.wait_ge(s_x, 16)

        @block.gpsimd
        def _(pool):
            gather_rows(nc, c, pool, NCH, x, D, source, s)

        @block.tensor
        def _(pe):
            def step(k, u):
                i = k * U + u
                wait(pe, s_dhot, i + 1)
                wait(pe, s_dadd, i - 3)
                nc.tensor.matmul(c.ps[:, B_D + u % 4, 0:3], c.hot4[:, u % 4, :], col(c.rec, T + i, HW)[:, 2:5],
                                 start=True, stop=True).then_inc(s_dsum, 1)
                wait(pe, s.got[u], 16 * (k + 1))
                wait(pe, s_hot, i + 1)
                wait(pe, s_add, i - 1)
                nc.tensor.matmul(c.ps[:, u % 2, :], c.hot[:, u % 2, :], c.G[:, u, 0:D],
                                 start=True, stop=True).then_inc(s.used, 1)
            run_steps(pe, NCH, step)

        @block.vector
        def _(dve):
            nc.vector.memset(c.ACC[:, :], 0.0)
            nc.vector.memset(c.deg[:, :], 0.0).then_inc(s_zero, 1)
            dve.wait_ge(s_zero, 1)

            def step(k, u):
                i = k * U + u
                if live(i, NCH):
                    wait(dve, s.used, i - 1)
                    r = col(c.rec0, i, SW)
                    nc.vector.tensor_scalar(c.hot[:, u % 2, :], c.iota[:, :], r[:, 1:2], r[:, 2:3],
                                            ALU.is_equal, ALU.mult).then_inc(s_hot, 1)
                    wait(dve, s_dsum, i - 3)
                    nc.vector.tensor_scalar(c.hot4[:, u % 4, :], c.iota[:, :], col(c.rec, T + i, HW)[:, 1:2], None,
                                            ALU.is_equal).then_inc(s_dhot, 1)
                j, slot, _ = back(k, u, 1)
                t = by_src.of(k, u)
                if live(j, NCH):
                    acc = tile_of(c.ACC, t)
                    wait(dve, s.used, j + 1)
                    wait(dve, s_add, j)
                    nc.vector.tensor_tensor(acc, acc, c.ps[:, slot % 2, :], ALU.add).then_inc(s_add, 1)
                j, slot, _ = back(k, u, 3)
                t = by_dst.of(k, u)
                if live(j, NCH):
                    acc = c.deg[:, bass.ds(t * 3, 3)]
                    wait(dve, s_dsum, j + 1)
                    wait(dve, s_dadd, j)
                    nc.vector.tensor_tensor(acc, acc, c.ps[:, B_D + slot % 4, 0:3], ALU.add).then_inc(s_dadd, 1)
            by_src, by_dst = Tiles(nc, dve, c.tiles_src, 0, NCH, 1), Tiles(nc, dve, c.tiles_dst, T, NCH, 3)
            run_steps(dve, NCH, step, lag=3)


@stage
def stage_attention_edges(nc, c, name, table, rows, we):
    s = edge_sems(c, name)
    (s_rec, s_hot, s_far, s_tr, s_ev, s_z, s_s, s_dot, s_lg, s_msk, s_mT, s_mx, s_mn, s_df, s_upd, s_exp, s_pT, s_w, s_acc,
     s_den) = (c.sem(f"{name}_{n}") for n in (
        "records_copied", "onehot", "far", "turned", "turned_copied", "product", "sum", "dot", "logit", "masked",
        "masked_turned", "chunk_max", "new_max", "shifts", "max_kept", "exp", "exp_turned", "exp_copied", "added",
        "sum_kept"))
    s_in, s_prep, s_we = c.sem(f"{name}_rows_in"), c.sem(f"{name}_prep"), c.sem(f"{name}_We_parts")

    def source(n, half):
        r = c.rec_i[:, :].rearrange("p (c w) -> p c w", w=HW)
        return r[:, n * half:(n + 1) * half, 0] if isinstance(n, int) else r[:, bass.ds(n * half, half), 0]
    B_T, B_Z, B_M, B_W, B_O = 0, 1, 3, 5, 6
    with nc.Block() as block:
        @block.sync
        def _(sp):
            for buf, a in rows:
                sp.dma_start(buf, a.partition_broadcast(P)).then_inc(s_in, 16)
            for n in range(3):
                sp.dma_start(c.We32[2 * n:2 * n + 2, :], we).then_inc(s_in, 16)

        @block.gpsimd
        def _(pool):
            nc.gpsimd.memset(c.ACC[:, :], 0.0)

        @block.vector
        def _(dve):
            n = [0]

            def link(ins):
                n[0] += 1
                ins.then_inc(s_prep, 1)
                dve.wait_ge(s_prep, n[0])
            dve.wait_ge(s_in, 16 * (len(rows) + 3))
            for a in range(2):
                link(nc.vector.tensor_tensor_reduce(out=c.R[:, :], in0=c.WeB[:, a * D:(a + 1) * D], in1=c.attB[:, :],
                                                    scale=SLOPE, scalar=0.0, op0=ALU.mult, op1=ALU.add,
                                                    accum_out=c.cvec[:, a:a + 1]))
            lin = c.parts[:, :].rearrange("p (c w) -> p c w", w=AW)[:, :, 6]
            link(nc.vector.tensor_scalar(lin, c.rec3[:, :, 2], c.cvec[:, 0:1], None, ALU.mult))
            link(nc.vector.scalar_tensor_tensor(lin, c.rec3[:, :, 3], c.cvec[:, 1:2], lin, ALU.mult, ALU.add))
            link(nc.vector.tensor_copy(c.WeR[:, :], c.We32[:, :]))
            link(nc.vector.tensor_scalar(c.We32[:, :], c.We32[:, :], c.low[0:6, :], None, ALU.mult))
            link(nc.vector.scalar_tensor_tensor(c.WeR[:, :], c.WeR[:, :], c.sign[0:6, :], c.We32[:, :], ALU.mult, ALU.add))
            nc.vector.memset(c.den[:, :], 0.0)
            nc.vector.memset(c.MA[:, :].rearrange("p (t w) -> p t w", w=2)[:, :, 0], -FAR)
    half = U // 2
    with nc.Block() as block:
        @block.gpsimd
        def _(pool):
            def records(k, u, n):
                wait_apart(pool, s_msk, k * U + u - half, s.passed)
                r = c.rec[:, :].rearrange("p (c w) -> p c w", w=HW)
                loc = r[:, n * half:(n + 1) * half, 1] if isinstance(n, int) else r[:, bass.ds(n * half, half), 1]
                nc.gpsimd.tensor_copy(c.local[:, u:u + half], loc)
                nc.gpsimd.tensor_copy(c.attr[:, u:u + half, :].rearrange("p c w -> p (c w)"),
                                      col(c.parts, n, half * AW)).then_inc(s_rec, 1)

            def masks(k, u):
                i = k * U + u
                wait_apart(pool, s_msk, i - U + 1, s.passed)
                if u % half == 0:
                    wait_apart(pool, s_rec, 2 * k + u // half + 1, s.passed)
                loc = c.local[:, u:u + 1]
                nc.gpsimd.tensor_scalar(c.hot8[:, u, :], c.iota[:, :], loc, None, ALU.is_equal).then_inc(s_hot, 1)
                wait_apart(pool, s_hot, i + 1, s.passed)
                nc.gpsimd.tensor_scalar(c.far[:, u, :], c.hot8[:, u, :], -1.0, FAR, ALU.add,
                                        ALU.mult).then_inc(s_far, 1)
            gather_rows(nc, c, pool, C1, table, TW, source, s, records, masks)

        @block.scalar
        def _(act):
            def step(k, u):
                j, v, _ = back(k, u, 5)
                if live(j, C1):
                    wait(act, s_df, j + 1)
                    wait(act, s_den, j - 3)
                    nc.scalar.activation(c.scale[:, v % 4:v % 4 + 1], c.diff[:, 2 * (v % 2):2 * (v % 2) + 1], ACT.Exp)
                    wait(act, s_pT, j - 1)
                    nc.scalar.activation(c.PT[:, v % 2, :], c.ps[:, B_M + v % 2, 0:P], ACT.Exp,
                                         bias=c.diff[:, 2 * (v % 2) + 1:2 * (v % 2) + 2],
                                         accum_out=c.rowsum[:, v % 4:v % 4 + 1]).then_inc(s_exp, 1)
                i, v, _ = back(k, u, 0)
                if live(i, C1):
                    wait(act, s_tr, i + 1)
                    wait(act, s_z, i - 1)
                    nc.scalar.activation(c.oT[:, v % 2, :], c.ps[:, B_T, 0:P], ACT.Copy)
                    nc.scalar.activation(c.eT[0:6, v % 2, :], c.ps[0:6, B_T, P:2 * P], ACT.Copy).then_inc(s_ev, 1)
                j, v, _ = back(k, u, 5)
                if live(j, C1):
                    wait(act, s_pT, j + 1)
                    wait(act, s.used, j - 1)
                    nc.scalar.activation(c.Wt[:, v % 2, :], c.ps[:, B_W, 0:P], ACT.Copy).then_inc(s_w, 1)
                j, v, _ = back(k, u, 2)
                if live(j, C1):
                    wait(act, s_dot, j + 1)
                    lg = c.lg[:, 2 * (v % 2):2 * (v % 2) + 2]
                    nc.scalar.activation(lg[:, 0:1], c.dot[:, v % 2:v % 2 + 1], ACT.Identity, bias=c.G[:, v, D:D + 1],
                                         scale=1.0 - SLOPE).then_inc(s_lg, 1)
                    wait(act, s_lg, 2 * j + 1)
                    nc.scalar.activation(lg[:, 1:2], lg[:, 0:1], ACT.Identity, bias=c.attr[:, v, 6:7]).then_inc(s_lg, 1)
                    wait(act, s_lg, 2 * j + 2)
                    wait(act, s_far, j + 1)
                    wait(act, s_mT, j - 1)
                    nc.scalar.activation(c.masked[:, v % 2, :], c.far[:, v, :], ACT.Identity,
                                         bias=lg[:, 1:2]).then_inc(s_msk, 1)
            run_steps(act, C1, step, lag=5)

        @block.tensor
        def _(pe):
            def step(k, u):
                i, v, _ = back(k, u, 0)
                if live(i, C1):
                    wait(pe, s_hot, i + 1)
                    if v % half == 0:
                        wait(pe, s_rec, 2 * k + u // half + 1)
                    wait(pe, s_ev, i)
                    nc.tensor.transpose(c.ps[:, B_T, 0:P], c.hot8[:, v, :], c.ident[:, :])
                    nc.tensor.transpose(c.ps[0:6, B_T, P:2 * P], c.attr[:, v, 0:6], c.ident[:, :]).then_inc(s_tr, 1)
                j, v, _ = back(k, u, 1)
                t = tiles.of(k, u)
                if live(j, C1):
                    wait(pe, s_ev, j + 1)
                    wait(pe, s_s, j - 1)
                    nc.tensor.matmul(c.ps[:, B_Z + v % 2, :], c.oT[:, v % 2, :], tile_of(c.XRh, t), start=True, stop=False)
                    nc.tensor.matmul(c.ps[:, B_Z + v % 2, :], c.oT[:, v % 2, :], tile_of(c.XRl, t), start=False, stop=False)
                    nc.tensor.matmul(c.ps[:, B_Z + v % 2, :], c.eT[0:6, v % 2, :], c.WeR[0:6, :], start=False,
                                     stop=True).then_inc(s_z, 1)
                j, v, _ = back(k, u, 3)
                if live(j, C1):
                    wait(pe, s_msk, j + 1)
                    wait(pe, s_exp, j - 1)
                    nc.tensor.transpose(c.ps[:, B_M + v % 2, 0:P], c.masked[:, v % 2, :], c.ident[:, :]).then_inc(s_mT, 1)
                j, v, _ = back(k, u, 5)
                if live(j, C1):
                    wait(pe, s_exp, j + 1)
                    wait(pe, s_w, j)
                    nc.tensor.transpose(c.ps[:, B_W, 0:P], c.PT[:, v % 2, :], c.ident[:, :]).then_inc(s_pT, 1)
                j, v, _ = back(k, u, 6)
                if live(j, C1):
                    wait(pe, s_w, j + 1)
                    wait(pe, s_acc, j - 1)
                    nc.tensor.matmul(c.ps[:, B_O + v % 2, :], c.Wt[:, v % 2, :], c.G[:, v, 0:D],
                                     start=True, stop=True).then_inc(s.used, 1)
            tiles = Tiles(nc, pe, c.tiles_dst, 0, C1, 1)
            run_steps(pe, C1, step, lag=6)

        @block.vector
        def _(dve):
            def step(k, u):
                m, w, _ = back(k, u, 4)
                if live(m, C1):
                    cmax, mnew = c.cmax[:, w % 2:w % 2 + 1], c.mnew[:, w % 2:w % 2 + 1]
                    wait(dve, s_mT, m + 1)
                    nc.vector.tensor_reduce(cmax, c.ps[:, B_M + w % 2, 0:P], AX.X, ALU.max).then_inc(s_mx, 1)
                j, v, r = back(k, u, 2)
                if live(j, C1):
                    wait(dve, s_z, j + 1)
                    wait(dve, s.got[v], 16 * (r + 1))
                    wait(dve, s_dot, j)
                    nc.vector.tensor_tensor(c.S[:, :], c.ps[:, B_Z + v % 2, :], c.G[:, v, 0:D], ALU.add).then_inc(s_s, 1)
                t = of_max.of(k, u)
                if live(m, C1):
                    MA = c.MA[:, bass.ds(t * 2, 2)]
                    wait(dve, s_mx, m + 1)
                    wait(dve, s_upd, m)
                    nc.vector.scalar_tensor_tensor(mnew, cmax, MA[:, 1:2], MA[:, 0:1], ALU.add, ALU.max).then_inc(s_mn, 1)
                if live(j, C1):
                    wait(dve, s_s, j + 1)
                    wait(dve, s_lg, 2 * j - 3)
                    nc.vector.scalar_tensor_tensor(c.R[:, :], c.S[:, :], 0.0, c.attB[:, :], ALU.max, ALU.mult,
                                                   accum_out=c.dot[:, v % 2:v % 2 + 1]).then_inc(s_dot, 1)
                q, x, _ = back(k, u, 7)
                t = of_sum.of(k, u)
                if live(m, C1):
                    wait(dve, s_mn, m + 1)
                    wait(dve, s_exp, m - 1)
                    nc.vector.tensor_scalar(c.diff[:, 2 * (w % 2):2 * (w % 2) + 2], MA, mnew, None,
                                            ALU.subtract).then_inc(s_df, 1)
                if live(q, C1):
                    den, acc = c.den[:, bass.ds(t, 1)], tile_of(c.ACC, t)
                    wait(dve, s_exp, q + 1)
                    wait(dve, s.used, q + 1)
                    wait(dve, s_acc, q)
                    nc.vector.scalar_tensor_tensor(acc, acc, c.scale[:, x % 4:x % 4 + 1], c.ps[:, B_O + x % 2, :],
                                                   ALU.mult, ALU.add).then_inc(s_acc, 1)
                    wait(dve, s_den, q)
                    nc.vector.scalar_tensor_tensor(den, den, c.scale[:, x % 4:x % 4 + 1], c.rowsum[:, x % 4:x % 4 + 1],
                                                   ALU.mult, ALU.add).then_inc(s_den, 1)
                if live(m, C1):
                    wait(dve, s_df, m + 1)
                    nc.vector.tensor_scalar(MA[:, 0:1], mnew, 0.0, None, ALU.add).then_inc(s_upd, 1)
            of_max, of_sum = (Tiles(nc, dve, c.tiles_dst, 0, C1, lag) for lag in (4, 7))
            run_steps(dve, C1, step, lag=7)


@stage
def stage_attention_close(nc, c, name):
    s_link = c.sem(f"{name}_link")
    full = lambda b: b[:, :].rearrange("p (t d) -> p t d", t=T)
    with nc.Block() as block:
        @block.vector
        def _(dve):
            n = [0]

            def link(ins):
                n[0] += 1
                ins.then_inc(s_link, 1)
                dve.wait_ge(s_link, n[0])
            link(nc.vector.tensor_scalar(c.den[:, :], c.den[:, :], 1e-16, None, ALU.add))
            link(nc.vector.reciprocal(c.den[:, :], c.den[:, :]))
            for t in range(T):
                last = nc.vector.scalar_tensor_tensor(tile_of(c.ACC, t), tile_of(c.ACC, t), c.den[:, t:t + 1],
                                                      tile_of(c.X, t), ALU.mult, ALU.add)
            link(last)
            nc.vector.tensor_tensor(full(c.ACC), full(c.ACC), c.row2[:, :].unsqueeze(1).to_broadcast([P, T, D]), ALU.add)


@stage
def stage_messages(nc, c, table, w1c, w2, b2):
    s = edge_sems(c, "msg")
    (s_hot, s_tr, s_ev, s_z, s_s, s_c1, s_a1, s_q1, s_h, s_hT, s_hc, s_lo, s_o, s_c2, s_a2, s_q2, s_m, s_agg, s_acc,
     s_loc, s_eh, s_el) = (c.sem(f"msg_{n}") for n in (
        "onehot", "turned", "turned_copied", "product1", "sum", "clamped1", "chain1", "ratio1", "hidden",
        "hidden_turned", "hidden_high", "hidden_low", "product2", "clamped2", "chain2", "ratio2", "message", "agg",
        "acc_added", "local_copied", "attr_high", "attr_low"))
    s_attr = [c.sem(f"msg_attr_in{u}") for u in range(U)]
    s.used = s_s
    s_w, s_prep, s_wf = c.sem("msg_weights_in"), c.sem("msg_prep"), c.sem("msg_weights_free")
    B_T, B_Z, B_H, B_O, B_A = 0, 1, 3, 5, 7
    half = U // 2
    rows = c.by_dst.rearrange("(p c) w -> p c w", p=P)

    def source(n, half):
        r = c.rec_i[:, :].rearrange("p (c w) -> p c w", w=HW)
        lo = n * half + T
        return r[:, lo:lo + half, 0] if isinstance(n, int) else r[:, bass.ds(lo, half), 0]
    with nc.Block() as block:
        @block.sync
        def _(sp):
            sp.dma_start(c.S[0:EA, 0, :], w1c).then_inc(s_w, 16)
            sp.dma_start(c.S[EA:2 * EA, 0, :], w1c).then_inc(s_w, 16)
            sp.dma_start(c.H[0:1, 0, :], b2.rearrange("(o d) -> o d", o=1)).then_inc(s_w, 16)
            sp.dma_start(c.M[:, 0, :], w2[0:P, :]).then_inc(s_w, 16)
            for b in range(1, KD):
                sp.wait_ge(s_wf, b)
                sp.dma_start(c.M[:, 0, :], w2[b * P:(b + 1) * P, :]).then_inc(s_w, 16)

        @block.gpsimd
        def _(pool):
            nc.gpsimd.memset(c.ACC[:, :], 0.0)

        @block.vector
        def _(dve):
            n = [0]

            def link(ins):
                n[0] += 1
                ins.then_inc(s_prep, 1)
                dve.wait_ge(s_prep, n[0])
            nc.vector.tensor_copy(c.one_row[:, :], c.ones[0:1, :])
            dve.wait_ge(s_w, 64)
            link(nc.vector.tensor_copy(c.W1ch[:, :], c.S[:, 0, :]))
            nc.vector.tensor_tensor(c.W1cl[:, :], c.S[0:EA, 0, :], c.W1ch[0:EA, :], ALU.subtract)
            link(nc.vector.tensor_copy(c.b2h[:, :], c.H[0:1, 0, :]))
            nc.vector.tensor_tensor(c.b2l[:, :], c.H[0:1, 0, :], c.b2h[:, :], ALU.subtract)
            for b in range(KD):
                dve.wait_ge(s_w, 64 + 16 * b)
                link(nc.vector.tensor_scalar(c.M[:, 0, :], c.M[:, 0, :], -2.0, None, ALU.mult))
                link(nc.vector.tensor_copy(c.W2h[:, b * D:(b + 1) * D], c.M[:, 0, :]))
                nc.vector.tensor_tensor(c.W2l[:, b * D:(b + 1) * D], c.M[:, 0, :], c.W2h[:, b * D:(b + 1) * D],
                                        ALU.subtract).then_inc(s_wf, 1)
                dve.wait_ge(s_wf, b + 1)
    with nc.Block() as block:
        @block.sync
        def _(sp):
            def step(k, u):
                i = k * U + u
                wait_apart(sp, s_el, i - U + 1, s.passed)
                a = rows[:, i, HW:RW] if isinstance(i, int) else rows[:, bass.ds(i, 1), HW:RW]
                sp.dma_start(c.ea[:, u, :], a).then_inc(s_attr[u], 16)
            run_steps(sp, NCH, step)

        @block.gpsimd
        def _(pool):
            def records(k, u, n):
                wait_apart(pool, s_hot, k * U + u - half, s.passed)
                r = c.rec[:, :].rearrange("p (c w) -> p c w", w=HW)
                lo = n * half + T
                loc = r[:, lo:lo + half, 1] if isinstance(n, int) else r[:, bass.ds(lo, half), 1]
                nc.gpsimd.tensor_copy(c.local[:, u:u + half], loc).then_inc(s_loc, 1)

            def split(k, u):
                i = k * U + u
                wait_apart(pool, s_tr, i - U + 1, s.passed)
                if u % half == 0:
                    wait_apart(pool, s_loc, 2 * k + u // half + 1, s.passed)
                nc.gpsimd.tensor_scalar(c.hot8[:, u, :], c.iota[:, :], c.local[:, u:u + 1], None,
                                        ALU.is_equal).then_inc(s_hot, 1)
                wait_apart(pool, s_attr[u], 16 * (k + 1), s.passed)
                nc.gpsimd.tensor_copy(c.ea2[:, u, 0:EA].bitcast(F32R), c.ea[:, u, :]).then_inc(s_eh, 1)
                wait_apart(pool, s_eh, i + 1, s.passed)
                nc.gpsimd.tensor_tensor(c.ea2[:, u, EA:2 * EA], c.ea[:, u, :], c.ea2[:, u, 0:EA],
                                        ALU.subtract).then_inc(s_el, 1)
            gather_rows(nc, c, pool, NCH, table, D, source, s, records, split)

        @block.tensor
        def _(pe):
            def step(k, u):
                i, v, _ = back(k, u, 0)
                if live(i, NCH):
                    wait(pe, s_el, i + 1)
                    wait(pe, s_ev, i)
                    nc.tensor.transpose(c.ps[:, B_T, 0:P], c.hot8[:, v, :], c.ident[:, :])
                    nc.tensor.transpose(c.ps[:, B_T, P:2 * P], c.ea2[:, v, :], c.ident[:, :]).then_inc(s_tr, 1)
                j, v, _ = back(k, u, 1)
                t = tiles.of(k, u)
                if live(j, NCH):
                    wait(pe, s_ev, j + 1)
                    wait(pe, s_s, j - 1)
                    z = c.ps[:, B_Z + v % 2, :]
                    nc.tensor.matmul(z, c.oT[:, v % 2, :], tile_of(c.XRh, t), start=True, stop=False)
                    nc.tensor.matmul(z, c.oT[:, v % 2, :], tile_of(c.XRl, t), start=False, stop=False)
                    nc.tensor.matmul(z, c.eT2[:, v % 2, :], c.W1ch[:, :], start=False, stop=False)
                    nc.tensor.matmul(z, c.eT2[0:EA, v % 2, :], c.W1cl[:, :], start=False, stop=True).then_inc(s_z, 1)
                j, v, _ = back(k, u, 5)
                if live(j, NCH):
                    wait(pe, s_h, j + 1)
                    wait(pe, s_lo, j - 1)
                    for b in range(KD):
                        last = nc.tensor.transpose(c.ps[:, B_H + v % 2, b * P:(b + 1) * P],
                                                   c.H[:, v % 2, b * P:(b + 1) * P], c.ident[:, :])
                    last.then_inc(s_hT, 1)
                j, v, _ = back(k, u, 6)
                if live(j, NCH):
                    wait(pe, s_lo, j + 1)
                    wait(pe, s_m, j - 1)
                    o = c.ps[:, B_O + v % 2, :]
                    nc.tensor.matmul(o, c.one_row[:, :], c.b2h[:, :], start=True, stop=False)
                    nc.tensor.matmul(o, c.one_row[:, :], c.b2l[:, :], start=False, stop=False)
                    for b in range(KD):
                        h = c.hTh[:, v % 2, b * P:(b + 1) * P]
                        nc.tensor.matmul(o, h, c.W2h[:, b * D:(b + 1) * D], start=False, stop=False)
                        nc.tensor.matmul(o, h, c.W2l[:, b * D:(b + 1) * D], start=False, stop=False)
                        last = nc.tensor.matmul(o, c.hTl[:, v % 2, b * P:(b + 1) * P], c.W2h[:, b * D:(b + 1) * D],
                                                start=False, stop=(b == KD - 1))
                    last.then_inc(s_o, 1)
                j, v, _ = back(k, u, 9)
                if live(j, NCH):
                    wait(pe, s_m, j + 1)
                    wait(pe, s_acc, j)
                    nc.tensor.matmul(c.ps[:, B_A, :], c.hotm[:, v % 2, :], c.M[:, v % 2, :],
                                     start=True, stop=True).then_inc(s_agg, 1)
            tiles = Tiles(nc, pe, c.tiles_dst, T, NCH, 1)
            run_steps(pe, NCH, step, lag=9)

        @block.scalar
        def _(act):
            nc.scalar.preload_act_table_set("natural_log_exp_and_others")

            def step(k, u):
                j, v, _ = back(k, u, 3)
                m, w, _ = back(k, u, 7)
                i, x, _ = back(k, u, 0)
                h, y, _ = back(k, u, 5)
                q1, q2 = c.Q[:, v % 2, :], c.Q2[:, w % 2, :]
                if live(j, NCH):
                    wait(act, s_c1, j + 1)
                    wait(act, s_h, j - 1)
                    nc.scalar.activation(q1, c.C1[:, v % 2, :], ACT.Exp).then_inc(s_a1, 1)
                if live(i, NCH):
                    wait(act, s_tr, i + 1)
                    wait(act, s_z, i - 1)
                    nc.scalar.activation(c.oT[:, x % 2, :], c.ps[:, B_T, 0:P], ACT.Copy)
                    nc.scalar.activation(c.eT2[:, x % 2, :], c.ps[:, B_T, P:2 * P], ACT.Copy).then_inc(s_ev, 1)
                if live(j, NCH):
                    wait(act, s_a1, 3 * j + 1)
                    nc.scalar.activation(q1, q1, ACT.Square, bias=c.ones[:, 0:1]).then_inc(s_a1, 1)
                if live(h, NCH):
                    wait(act, s_hT, h + 1)
                    wait(act, s_o, h - 1)
                    nc.scalar.activation(c.hTh[:, y % 2, :], c.ps[:, B_H + y % 2, :], ACT.Copy).then_inc(s_hc, 1)
                if live(j, NCH):
                    wait(act, s_a1, 3 * j + 2)
                    nc.scalar.activation(q1, q1, ACT.Ln, bias=c.ones[:, 0:1]).then_inc(s_a1, 1)
                if live(m, NCH):
                    wait(act, s_c2, m + 1)
                    wait(act, s_m, m - 1)
                    nc.scalar.activation(q2, c.C2[:, :], ACT.Exp).then_inc(s_a2, 1)
                if live(j, NCH):
                    wait(act, s_a1, 3 * j + 3)
                    nc.scalar.activation(q1, q1, ACT.Exp, scale=-1.0).then_inc(s_q1, 1)
                if live(m, NCH):
                    wait(act, s_a2, 3 * m + 1)
                    nc.scalar.activation(q2, q2, ACT.Square, bias=c.ones[:, 0:1]).then_inc(s_a2, 1)
                if live(m, NCH):
                    wait(act, s_a2, 3 * m + 2)
                    nc.scalar.activation(q2, q2, ACT.Ln, bias=c.ones[:, 0:1]).then_inc(s_a2, 1)
                if live(m, NCH):
                    wait(act, s_a2, 3 * m + 3)
                    nc.scalar.activation(q2, q2, ACT.Exp, scale=-1.0).then_inc(s_q2, 1)
            run_steps(act, NCH, step, lag=7)

        @block.vector
        def _(dve):
            def step(k, u):
                j, v, _ = back(k, u, 6)
                if live(j, NCH):
                    wait(dve, s_hc, j + 1)
                    wait(dve, s_o, j - 1)
                    nc.vector.tensor_tensor(c.hTl[:, v % 2, :], c.ps[:, B_H + v % 2, :], c.hTh[:, v % 2, :],
                                            ALU.subtract).then_inc(s_lo, 1)
                t = tiles.of(k, u)
                j, v, _ = back(k, u, 8)
                if live(j, NCH):
                    wait(dve, s_agg, j - 1)
                    nc.vector.tensor_scalar(c.hotm[:, v % 2, :], c.iota[:, :], col(c.rec, T + j, HW)[:, 1:2], -2.0,
                                            ALU.is_equal, ALU.mult)
                    wait(dve, s_q2, j + 1)
                    nc.vector.scalar_tensor_tensor(c.M[:, v % 2, :], c.Q2[:, v % 2, :], 0.5, c.ps[:, B_O + v % 2, :],
                                                   ALU.subtract, ALU.mult).then_inc(s_m, 1)
                m, w, _ = back(k, u, 10)
                if live(m, NCH):
                    acc = tile_of(c.ACC, t)
                    wait(dve, s_agg, m + 1)
                    wait(dve, s_acc, m)
                    nc.vector.tensor_tensor(acc, acc, c.ps[:, B_A, :], ALU.add).then_inc(s_acc, 1)
                j, v, _ = back(k, u, 4)
                if live(j, NCH):
                    wait(dve, s_q1, j + 1)
                    wait(dve, s_hT, j - 1)
                    nc.vector.scalar_tensor_tensor(c.H[:, v % 2, :], c.Q[:, v % 2, :], 0.5, c.S[:, v % 2, :], ALU.subtract,
                                                   ALU.mult).then_inc(s_h, 1)
                j, v, _ = back(k, u, 7)
                if live(j, NCH):
                    wait(dve, s_o, j + 1)
                    wait(dve, s_a2, 3 * j)
                    nc.vector.tensor_scalar(c.C2[:, :], c.ps[:, B_O + v % 2, :], CLAMP, None, ALU.min).then_inc(s_c2, 1)
                j, v, r = back(k, u, 2)
                if live(j, NCH):
                    wait(dve, s_z, j + 1)
                    wait(dve, s.got[v], 16 * (r + 1))
                    wait(dve, s_h, j - 1)
                    nc.vector.tensor_tensor(c.S[:, v % 2, :], c.ps[:, B_Z + v % 2, :], c.G[:, v, 0:D], ALU.add).then_inc(s_s, 1)
                if live(j, NCH):
                    wait(dve, s_s, j + 1)
                    wait(dve, s_a1, 3 * (j - 2) + 1)
                    nc.vector.tensor_scalar(c.C1[:, v % 2, :], c.S[:, v % 2, :], CLAMP, None, ALU.min).then_inc(s_c1, 1)
            tiles = Tiles(nc, dve, c.tiles_dst, T, NCH, 10)
            run_steps(dve, NCH, step, lag=10)


@stage
def stage_mish(nc, c, buf):
    s_c, s_a, s_q, s_m, s_o = (c.sem(f"mish_{n}") for n in ("clamped", "chain", "ratio", "product", "done"))
    with nc.Block() as block:
        @block.scalar
        def _(act):
            nc.scalar.preload_act_table_set("natural_log_exp_and_others")
            for t in range(T):
                q = c.Q[:, t % 2, :]
                act.wait_ge(s_c, t + 1)
                if t >= 2:
                    act.wait_ge(s_m, t - 1)
                nc.scalar.activation(q, c.S[:, t % 2, :], ACT.Exp).then_inc(s_a, 1)
                act.wait_ge(s_a, 3 * t + 1)
                nc.scalar.activation(q, q, ACT.Square, bias=c.ones[:, 0:1]).then_inc(s_a, 1)
                act.wait_ge(s_a, 3 * t + 2)
                nc.scalar.activation(q, q, ACT.Ln, bias=c.ones[:, 0:1]).then_inc(s_a, 1)
                act.wait_ge(s_a, 3 * t + 3)
                nc.scalar.activation(q, q, ACT.Exp, scale=-1.0).then_inc(s_q, 1)

        @block.vector
        def _(dve):
            for t in range(T + 1):
                if t < T:
                    if t >= 2:
                        dve.wait_ge(s_q, t - 1)
                    nc.vector.tensor_scalar(c.S[:, t % 2, :], tile_of(buf, t), CLAMP, None, ALU.min).then_inc(s_c, 1)
                if t >= 1:
                    b = tile_of(buf, t - 1)
                    dve.wait_ge(s_q, t)
                    nc.vector.scalar_tensor_tensor(b, c.Q[:, (t - 1) % 2, :], 0.5, b, ALU.subtract, ALU.mult).then_inc(s_m, 1)
                    dve.wait_ge(s_m, t)
                    nc.vector.tensor_scalar(b, b, -2.0, None, ALU.mult)


@stage
def stage_scaled_table(nc, c, table):
    s_sc, s_st = c.sem("scaled_ready"), c.sem("scaled_stored")
    with nc.Block() as block:
        @block.vector
        def _(dve):
            for t in range(T):
                last = nc.vector.tensor_scalar(tile_of(c.XR, t), tile_of(c.X, t), c.dis[:, t:t + 1], None, ALU.mult)
            last.then_inc(s_sc, 1)

        @block.sync
        def _(sp):
            sp.wait_ge(s_sc, 1)
            sp.dma_start(table.rearrange("(t p) d -> p t d", p=P), c.XR[:, :].rearrange("p (t d) -> p t d", t=T))\
              .then_inc(s_st, 16)
            sp.wait_ge(s_st, 16)


@stage
def stage_nodes_back(nc, c, table):
    s_x = c.sem("nodes_back")
    with nc.Block() as block:
        @block.sync
        def _(sp):
            sp.dma_start(c.X.rearrange("p (t d) -> p t d", t=T), table.rearrange("(t p) d -> p t d", p=P)).then_inc(s_x, 16)
            sp.wait_ge(s_x, 16)


@stage
def stage_split_attributes(nc, c):
    s_h = c.sem("split_high")
    p7, p7r = (x.rearrange("p (c w) -> p c w", w=AW) for x in (c.parts[:, :], c.parts[:, :].bitcast(F32R)))
    with nc.Block() as block:
        @block.vector
        def _(dve):
            nc.vector.tensor_copy(p7r[:, :, 0:2], c.rec3[:, :, 2:4]).then_inc(s_h, 1)
            nc.vector.tensor_copy(p7r[:, :, 2:4], c.rec3[:, :, 2:4])
            dve.wait_ge(s_h, 1)
            nc.vector.tensor_tensor(p7r[:, :, 4:6], c.rec3[:, :, 2:4], p7[:, :, 0:2], ALU.subtract)


def gnn_stack(nc, a, out):
    c = Chip()
    c.sems = []

    def sem(name):
        c.sems.append(nc.alloc_semaphore(name=name))
        return c.sems[-1]
    c.sem = sem
    numbered = [0]

    def allocator(scope):
        def sb(name, shape, dt=F32):
            numbered[0] += 1
            return scope.enter_context(nc.sbuf_tensor(f"{name}_{numbered[0]}", shape, dt))
        return sb

    def dram(name, shape):
        return nc.dram_tensor(name, shape, F32, kind="Internal").ap()

    c.by_dst, c.by_src = dram("by_dst", [P * NCH, RW]), dram("by_src", [P * NCH, SW])
    table, table_att, table_res = dram("table", [N, D]), dram("table_att", [N, TW]), dram("table_res", [N, D])
    with ExitStack() as whole:
        sb = allocator(whole)
        c.ps = whole.enter_context(nc.psum_tensor("ps", [P, 8, 512], F32))
        c.rec = sb("rec", [P, C1 * HW])[:, :]
        c.rec_i = c.rec.bitcast(I32)
        c.rec3, c.rec3_i = (r.rearrange("p (c w) -> p c w", w=HW) for r in (c.rec, c.rec_i))
        c.tiles_dst, c.tiles_src = sb("tiles_dst", [1, C1], I32), sb("tiles_src", [1, NCH], I32)
        c.iota, c.ones, c.ident, c.eps = sb("iota", [P, P]), sb("ones", [P, P]), sb("ident", [P, P]), sb("eps", [P, 1])
        c.node_i, c.tile_i, c.lane_i = sb("node_i", [P, T], I32), sb("tile_i", [P, T], I32), sb("lane_i", [P, 1], I32)
        c.lane_f, c.low, c.low2, c.sign = (sb(n, [P, 1]) for n in ("lane_f", "low", "low2", "sign"))
        c.counts, c.small, c.small_i = sb("counts", [P, T]), sb("small", [P, 4 * T]), sb("small_i", [P, 2 * T], I32)
        c.idx, c.idx0 = sb("idx", [P, U], I32), sb("idx0", [P, U], I32)
        c.deg, c.deg1, c.dis, c.root = sb("deg", [P, 3 * T]), sb("deg1", [P, T]), sb("dis", [P, T]), sb("root", [P, T])
        c.mv, c.st, c.rstd = sb("mv", [P, 2 * T]), sb("st", [P, 6 * T]), sb("rstd", [P, T])
        c.cvec, c.den, c.MA = sb("cvec", [P, 2]), sb("den", [P, T]), sb("MA", [P, 2 * T])

        with ExitStack() as scope:
            sb = allocator(scope)
            c.recs, c.recs0 = sb("recs", [P, EC * RW])[:, :], sb("recs0", [P, EC * SW])[:, :]
            c.recs3 = c.recs.rearrange("p (j w) -> p j w", w=RW)
            c.recs3_i = c.recs.bitcast(I32).rearrange("p (j w) -> p j w", w=RW)
            c.recs0_3 = c.recs0.rearrange("p (j w) -> p j w", w=SW)
            c.recs0_3i = c.recs0.bitcast(I32).rearrange("p (j w) -> p j w", w=SW)
            c.member, c.running = sb("member", [P, T * EC]), sb("running", [P, T * EC])
            c.PADS = 16
            c.pads, c.pads0 = sb("pads", [P, c.PADS * RW]), sb("pads0", [P, NCH * SW])
            c.bin_f, c.bin_g, c.edge_ones, c.weight = (sb(n, [P, EC]) for n in ("bin_f", "bin_g", "edge_ones", "weight"))
            c.attr2 = sb("attr2", [P, 2 * EC])
            c.key_src, c.key_dst, c.rows_dst, c.rows_src = (sb(n, [P, EC], I32) for n in (
                "key_src", "key_dst", "rows_dst", "rows_src"))
            c.tmp_i, c.iota_i, c.upper = sb("tmp_i", [P, 3 * EC], I32), sb("iota_i", [P, P], I32), sb("upper", [P, P])
            c.chunk_i, c.chunk_f, c.tile_f = sb("chunk_i", [P, NCH], I32), sb("chunk_f", [P, NCH]), sb("tile_f", [1, NCH])
            c.stage, c.stage0 = sb("stage", [P, U * RW]), sb("stage0", [P, U * SW])
            stage_constants(nc, c)
            stage_bin(nc, c, a["src"], a["dst"], a["edge_attr_2"], a["edge_attr_64"], a["edge_weight"])
            stage_scatter(nc, c)

        sb = allocator(whole)
        c.X, c.ACC = sb("X", [P, T * D])[:, :], sb("ACC", [P, T * D])[:, :]
        c.G = sb("G", [P, U, TW])
        c.hot = sb("hot", [P, 2, P])
        with ExitStack() as scope:
            sb = allocator(scope)
            c.rec0 = sb("rec0", [P, NCH * SW])[:, :]
            with ExitStack() as inner:
                c.wide = allocator(inner)("wide", [P, NCH * RW])
                stage_heads(nc, c)
            c.hot4 = sb("hot4", [P, 4, P])
            stage_first_sums(nc, c, a["x"])
            stage_degrees(nc, c)
            linear_buffers(c, sb)
            c.XR = sb("XR", [P, T * D])[:, :]
            stage_transpose_weight(nc, c, a["L0_gnn_weight"])
            stage_linear(nc, c, "L0lin", [c.ACC], [(
                [1], lambda link, t, ps, o: nc.vector.tensor_tensor(tile_of(c.XR, t), ps, tile_of(c.X, t), ALU.add), 0)])
            stage_norm(nc, c, "L0norm", c.XR, c.X, store=table_res)

        with ExitStack() as scope:
            sb = allocator(scope)
            c.XRh, c.XRl = sb("XRh", [P, T * D], F32R)[:, :], sb("XRl", [P, T * D], F32R)[:, :]
            c.parts = sb("parts", [P, C1 * AW])
            stage_split_attributes(nc, c)
            for k in range(3):
                attention_round(nc, c, scope, allocator, a, k, table_att)
        s_res = c.sem("L1_residual_in")
        with nc.Block() as block:
            @block.sync
            def _(sp):
                sp.dma_start(c.ACC.rearrange("p (t d) -> p t d", t=T), table_res.rearrange("(t p) d -> p t d", p=P))\
                  .then_inc(s_res, 16)

            @block.vector
            def _(dve):
                dve.wait_ge(s_res, 16)
                nc.vector.tensor_tensor(c.X[:, :], c.X[:, :], c.ACC[:, :], ALU.add)
        stage_norm(nc, c, "L1norm", c.X, c.X)

        def conv1(link, t, ps, o):
            dis = col(c.dis, t)
            link(nc.vector.scalar_tensor_tensor(c.S[:, 0, :], ps, dis, c.row0[:, :], ALU.mult, ALU.add))
            return nc.vector.tensor_scalar(o[:, 0:D], c.S[:, 0, :], 0.0, dis, ALU.max, ALU.mult)

        def conv2(link, t, ps, o):
            link(nc.vector.scalar_tensor_tensor(c.S[:, 0, :], ps, col(c.dis, t), c.row0[:, :], ALU.mult, ALU.add))
            return nc.vector.tensor_tensor(tile_of(c.XR, t), c.S[:, 0, :], tile_of(c.X, t), ALU.add)
        with ExitStack() as scope:
            sb = allocator(scope)
            linear_buffers(c, sb)
            c.XR = sb("XR", [P, T * D])[:, :]
            stage_scaled_table(nc, c, table)
            stage_aggregate(nc, c, "L2a", table)
            stage_linear(nc, c, "L2alin", [c.ACC], [([0], conv1, 1)], weights=[(a["L2_gnn_W1"], 0)],
                         rows=[(c.row0[:, :], a["L2_gnn_b1"])], table=table)
            stage_aggregate(nc, c, "L2b", table)
            stage_linear(nc, c, "L2blin", [c.ACC], [([0], conv2, 1)], weights=[(a["L2_gnn_W2"], 0)],
                         rows=[(c.row0[:, :], a["L2_gnn_b2"])])
            stage_norm(nc, c, "L2norm", c.XR, c.X, store=table_res)

        with ExitStack() as scope:
            sb = allocator(scope)
            c.XRh, c.XRl = sb("XRh", [P, T * D], F32R)[:, :], sb("XRl", [P, T * D], F32R)[:, :]
            with ExitStack() as inner:
                linear_buffers(c, allocator(inner))

                def right(link, t, ps, o):
                    link(nc.vector.tensor_scalar(tile_of(c.XRh, t), ps, 0.0, None, ALU.add))
                    return nc.vector.tensor_tensor(tile_of(c.XRl, t), ps, tile_of(c.XRh, t), ALU.subtract)
                stage_linear(nc, c, "L3lin", [c.X], [
                    ([0], lambda link, t, ps, o: nc.vector.tensor_tensor(o[:, 0:D], ps, c.row0[:, :], ALU.add), 0),
                    ([1], right, 1)],
                    weights=[(a["L3_gnn_W1"][0:D, :], 0), (a["L3_gnn_W1"][D:2 * D, :], 1)],
                    rows=[(c.row0[:, :], a["L3_gnn_b1"])], table=table)
            with ExitStack() as inner:
                sb = allocator(inner)
                c.S, c.C1, c.Q, c.H, c.Q2, c.M = (c.X[:, n * 2 * D:(n + 1) * 2 * D].rearrange("p (b d) -> p b d", b=2)
                                                  for n in range(6))
                c.C2, c.hotm = c.X[:, 12 * D:13 * D], sb("hotm", [P, 2, P])
                c.hTh, c.hTl = sb("hTh", [P, 2, D], F32R), sb("hTl", [P, 2, D], F32R)
                c.W2h, c.W2l = sb("W2h", [P, KD * D], F32R), sb("W2l", [P, KD * D], F32R)
                c.W1ch, c.W1cl = sb("W1ch", [2 * EA, D], F32R), sb("W1cl", [EA, D], F32R)
                c.b2h, c.b2l, c.one_row = sb("b2h", [1, D], F32R), sb("b2l", [1, D], F32R), sb("one_row", [1, P], F32R)
                c.oT, c.eT2 = sb("oT", [P, 2, P], F32R), sb("eT2", [2 * EA, 2, P], F32R)
                c.hot8 = c.X[:, 13 * D:15 * D].rearrange("p (u d) -> p u d", u=U)
                c.ea = c.X[:, 15 * D:16 * D].rearrange("p (u a) -> p u a", u=U)
                c.ea2, c.local = sb("ea2", [P, U, 2 * EA]), sb("local", [P, U])
                stage_messages(nc, c, table, a["L3_gnn_W1"][2 * D:2 * D + EA, :], a["L3_gnn_W2"], a["L3_gnn_b2"])
            stage_nodes_back(nc, c, table_res)
        with ExitStack() as scope:
            sb = allocator(scope)
            linear_buffers(c, sb)
            c.XR = sb("XR", [P, T * D])[:, :]
            stage_linear(nc, c, "L3u", [c.X, c.ACC], [
                ([0, 1], lambda link, t, ps, o: nc.vector.tensor_tensor(tile_of(c.XR, t), ps, c.row0[:, :], ALU.add), 0)],
                weights=[(a["L3_gnn_W3"][0:D, :], 0), (a["L3_gnn_W3"][D:2 * D, :], 1)],
                rows=[(c.row0[:, :], a["L3_gnn_b3"])])
            stage_mish(nc, c, c.XR)

            def close(link, t, ps, o):
                link(nc.vector.tensor_tensor(c.S[:, 0, :], ps, c.row0[:, :], ALU.add))
                return nc.vector.tensor_tensor(tile_of(c.ACC, t), c.S[:, 0, :], tile_of(c.X, t), ALU.add)
            stage_linear(nc, c, "L3out", [c.XR], [([0], close, 1)], weights=[(a["L3_gnn_W4"], 0)],
                         rows=[(c.row0[:, :], a["L3_gnn_b4"]), (c.row1[:, :], a["L3_gnn_gamma"]),
                               (c.row2[:, :], a["L3_gnn_beta"])])
            stage_norm(nc, c, "L3norm", c.ACC, c.XR, gamma=c.row1[:, :], beta=c.row2[:, :], residual=c.X)
            stage_norm(nc, c, "outnorm", c.XR, c.ACC, store=out)


def linear_buffers(c, sb):
    c.W = sb("W", [P, 2, KD * D])
    c.row0, c.row1, c.row2 = (sb(f"row{n}", [P, D]) for n in range(3))
    c.xs, c.xT, c.out = sb("xs", [P, 2, D]), sb("xT", [P, 2, D]), sb("out", [P, 2, TW])
    c.S, c.Q = sb("S", [P, 2, D]), sb("Q", [P, 2, D])


def attention_round(nc, c, scope, allocator, a, k, table):
    n = f"L1_{k}"
    wl, wr, we = a["L1_gnn_Wl"][k], a["L1_gnn_Wr"][k], a["L1_gnn_We"][k]

    def left(link, t, ps, o):
        link(nc.vector.tensor_tensor(o[:, 0:D], ps, c.row0[:, :], ALU.add))
        return nc.vector.tensor_tensor_reduce(out=c.S[:, 0, :], in0=o[:, 0:D], in1=c.row2[:, :], scale=SLOPE,
                                              scalar=0.0, op0=ALU.mult, op1=ALU.add, accum_out=o[:, D:D + 1])

    def right(link, t, ps, o):
        r = c.S[:, 1, :]
        link(nc.vector.tensor_tensor(r, ps, c.row1[:, :], ALU.add))
        ar = c.MA[:, 2 * t + 1:2 * t + 2] if isinstance(t, int) else c.MA[:, bass.ds(2 * t + 1, 1)]
        nc.vector.scalar_tensor_tensor(c.Q[:, 1, :], r, SLOPE, c.row2[:, :], ALU.mult, ALU.mult,
                                       accum_out=c.cvec[:, 0:1])
        link(nc.vector.tensor_scalar(tile_of(c.XRh, t), r, 0.0, None, ALU.add))
        nc.vector.tensor_tensor(tile_of(c.XRl, t), r, tile_of(c.XRh, t), ALU.subtract)
        return nc.vector.tensor_scalar(ar, c.cvec[:, 0:1], 0.0, None, ALU.add)
    with ExitStack() as inner:
        linear_buffers(c, allocator(inner))
        s_pad = c.sem(f"{n}_pad")
        with nc.Block() as block:
            @block.gpsimd
            def _(pool):
                pool.memset(c.out[:, :, D:TW], 0.0).then_inc(s_pad, 1)
        stage_linear(nc, c, n + "lin", [c.X], [([0], left, 1), ([1], right, 2)], weights=[(wl, 0), (wr, 1)],
                     rows=[(c.row0[:, :], a["L1_gnn_bl"][k]), (c.row1[:, :], a["L1_gnn_br"][k]),
                           (c.row2[:, :], a["L1_gnn_att"][k])], table=table)
    with ExitStack() as inner:
        sb = allocator(inner)
        c.attB, c.WeB, c.We32, c.WeR = sb("attB", [P, D]), sb("WeB", [P, 2 * D]), sb("We32", [6, D]), sb("WeR", [6, D], F32R)
        c.S, c.R = sb("S", [P, D]), sb("R", [P, D])
        c.oT, c.eT = sb("oT", [P, 2, P], F32R), sb("eT", [6, 2, P], F32R)
        c.local, c.attr = sb("local", [P, U]), sb("attr", [P, U, AW])
        c.hot8, c.far = sb("hot8", [P, U, P]), sb("far", [P, U, P])
        c.masked, c.PT, c.Wt = (sb(m, [P, 2, P]) for m in ("masked", "PT", "Wt"))
        c.dot, c.lg, c.cmax, c.mnew = sb("dot", [P, 2]), sb("lg", [P, 4]), sb("cmax", [P, 2]), sb("mnew", [P, 2])
        c.scale, c.rowsum, c.diff = (sb(m, [P, 4]) for m in ("scale", "rowsum", "diff"))
        stage_attention_edges(nc, c, n, table, [(c.attB[:, :], a["L1_gnn_att"][k]),
                                                (c.WeB[:, :], we.rearrange("a d -> (a d)"))], we)
    with ExitStack() as inner:
        linear_buffers(c, allocator(inner))
        stage_rows(nc, c, n + "affine", [(c.row2[:, :], a["L1_gnn_b_out"][k]), (c.row0[:, :], a["L1_gnn_gamma"][k]),
                              (c.row1[:, :], a["L1_gnn_beta"][k])])
        stage_attention_close(nc, c, n + "close")
        stage_norm(nc, c, n + "norm", c.ACC, c.X, gamma=c.row0[:, :], beta=c.row1[:, :], relu=True)


_INS = ['x', 'src', 'dst', 'edge_attr_2', 'edge_attr_64', 'edge_weight', 'L0_gnn_weight', 'L1_gnn_Wl', 'L1_gnn_bl',
        'L1_gnn_Wr', 'L1_gnn_br', 'L1_gnn_We', 'L1_gnn_att', 'L1_gnn_b_out', 'L1_gnn_gamma', 'L1_gnn_beta',
        'L2_gnn_W1', 'L2_gnn_b1', 'L2_gnn_W2', 'L2_gnn_b2', 'L3_gnn_W1', 'L3_gnn_b1', 'L3_gnn_W2', 'L3_gnn_b2',
        'L3_gnn_W3', 'L3_gnn_b3', 'L3_gnn_W4', 'L3_gnn_b4', 'L3_gnn_gamma', 'L3_gnn_beta']


def kernel(**inputs):
    import numpy as _np
    import concourse.bacc as _bacc
    from concourse import mybir as _mybir
    from concourse.bass_utils import run_bass_kernel_spmd as _run

    nc = _bacc.Bacc("TRN2", target_bir_lowering=False, num_devices=1)
    arrays, args = {}, {}
    for name in _INS:
        v = _np.ascontiguousarray(inputs[name])
        arrays[f"in_{name}_dram"] = v
        args[name] = nc.dram_tensor(f"in_{name}_dram", v.shape, _mybir.dt.from_np(v.dtype), kind="ExternalInput").ap()
    out = nc.dram_tensor("out_0_dram", (N, D), F32, kind="ExternalOutput").ap()
    gnn_stack(nc, args, out)
    r = _run(nc, [arrays], core_ids=[0])
    return r.results[0]["out_0_dram"]
```
